# Optimizing a Trainium2 kernel written in Bass

```python
import numpy as np
import jax
import jax.numpy as jnp

def _softmax(x, axis=-1):
    return jax.nn.softmax(x, axis=axis)

def _gelu(x):
    return jax.nn.gelu(x, approximate=True)

def _silu(x):
    return jax.nn.silu(x)

def _sigmoid(x):
    return jax.nn.sigmoid(x)

def _layernorm(x, axis=-1, eps=1e-05):
    m = jnp.mean(x, axis=axis, keepdims=True)
    v = jnp.var(x, axis=axis, keepdims=True)
    return (x - m) / jnp.sqrt(v + eps)

def _scatter_add(tgt, idx, src, axis=0):
    return tgt.at[idx].add(src)

def _segment_sum(src, seg, n):
    return jax.ops.segment_sum(src, seg, n)
kernel_name = 'mk_perceiver_d2_seqx_r4_6416e2'

def setup_inputs(seed: int=0):
    np.random.seed(seed)
    _w = jnp.asarray

    def _rec_inputs():
        import jax
        import jax.numpy as jnp
        _rk = jax.random.key(seed)
        x = 7.22e-05 + 1 * jax.random.normal(jax.random.fold_in(_rk, 1), (1, 128, 256), jnp.float32)
        _lenS = 128 - jax.random.randint(jax.random.fold_in(_rk, 7), (1,), 0, max(1, 128 // 4) + 1, jnp.int32)
        _lenS2 = 12544 - jax.random.randint(jax.random.fold_in(_rk, 8), (1,), 0, max(1, 12544 // 4) + 1, jnp.int32)
        _ctx_768P = jax.random.normal(jax.random.fold_in(_rk, 11), (1, 16, 192), jnp.float32)
        _ctx_768c = jax.random.dirichlet(jax.random.fold_in(_rk, 511), 0.3 * jnp.ones((16,), jnp.float32), (1, 12544))
        _ctx_768t = jnp.einsum('bsk,bkd->bsd', _ctx_768c, _ctx_768P)
        _ctx_768t = _ctx_768t * jax.lax.rsqrt(jnp.mean(jnp.square(_ctx_768t)) + 1e-12) * 0.953939
        ctx_768 = -0.000191848 + 0.999787 * (_ctx_768t + 0.3 * jax.random.normal(jax.random.fold_in(_rk, 611), (1, 12544, 192), jnp.float32))
        return (x, ctx_768)
    x, ctx_768 = _rec_inputs()

    def _L0_xattn_setup():
        import jax, jax.numpy as jnp
        import numpy as np
        NUM_HEADS = 16
        CLAMP = 10000.0
        key = jax.random.key(seed)
        ks = jax.random.split(key, 8)
        B, Nq, Nkv, Cq, Ckv = (4, 512, 512, 256, 192)
        s_q = 1.0 / np.sqrt(Cq)
        s_kv = 1.0 / np.sqrt(Ckv)
        return {'query': jax.random.normal(ks[0], (B, Nq, Cq), jnp.float32), 'key_value': jax.random.normal(ks[1], (B, Nkv, Ckv), jnp.float32), 'Wq': jax.random.normal(ks[2], (Cq, Cq), jnp.float32) * s_q, 'bq': jnp.zeros((Cq,), jnp.float32), 'Wk': jax.random.normal(ks[3], (Ckv, Cq), jnp.float32) * s_kv, 'bk': jnp.zeros((Cq,), jnp.float32), 'Wv': jax.random.normal(ks[4], (Ckv, Cq), jnp.float32) * s_kv, 'bv': jnp.zeros((Cq,), jnp.float32), 'Wo': jax.random.normal(ks[5], (Cq, Cq), jnp.float32) * s_q, 'bo': jnp.zeros((Cq,), jnp.float32)}
    _L0_xattn_all = _L0_xattn_setup()
    _L0_xattn_in = {k: v for k, v in _L0_xattn_all.items() if k in ('Wq', 'bq', 'Wk', 'bk', 'Wv', 'bv', 'Wo', 'bo')}
    del _L0_xattn_all

    def _L0_attn_setup():
        import jax, jax.numpy as jnp
        import numpy as np
        D_MODEL = 256
        D_INNER = 512
        D_STATE = 16
        DT_RANK = 64
        D_CONV = 4
        EPS = 1e-05
        B_SZ, L = (2, 512)

        def _silu(x):
            return x * jax.nn.sigmoid(x)
        key = jax.random.key(seed)
        ks = jax.random.split(key, 8)
        s = 0.02
        inp = {'x': jax.random.normal(ks[0], (B_SZ, L, D_MODEL), jnp.float32), 'in_proj_w': jax.random.normal(ks[1], (D_MODEL, 2 * D_INNER), jnp.float32) * s, 'conv_w': jax.random.normal(ks[2], (D_INNER, 1, D_CONV), jnp.float32) * s, 'conv_b': jnp.zeros((D_INNER,), jnp.float32), 'x_proj_w': jax.random.normal(ks[3], (D_INNER, DT_RANK + 2 * D_STATE), jnp.float32) * s, 'dt_proj_w': jax.random.normal(ks[4], (DT_RANK, D_INNER), jnp.float32) * s, 'dt_proj_b': jax.random.normal(ks[5], (D_INNER,), jnp.float32) * s, 'A_log': jnp.log(jnp.broadcast_to(jnp.arange(1, D_STATE + 1, dtype=jnp.float32), (D_INNER, D_STATE))), 'D': jnp.ones((D_INNER,), jnp.float32), 'out_proj_w': jax.random.normal(ks[6], (D_INNER, D_MODEL), jnp.float32) * s, 'norm_w': jnp.ones((D_MODEL,), jnp.float32)}
        return inp
    _L0_attn_all = _L0_attn_setup()
    _L0_attn_in = {k: v for k, v in _L0_attn_all.items() if k in ('in_proj_w', 'conv_w', 'conv_b', 'x_proj_w', 'dt_proj_w', 'dt_proj_b', 'A_log', 'D', 'out_proj_w', 'norm_w')}
    del _L0_attn_all

    def _L0_ffn_setup():
        import jax, jax.numpy as jnp
        import numpy as np
        B, S, H, D, E = (4, 256, 256, 1024, 8)
        key = jax.random.key(seed)
        ks = jax.random.split(key, 12)

        def init(k, shape, fan_in):
            return jax.random.normal(k, shape, jnp.float32) / np.float32(np.sqrt(fan_in))
        return {'x': jax.random.normal(ks[0], (B, S, H), jnp.float32), 'Wq': init(ks[1], (H, H), H), 'bq': jnp.zeros((H,), jnp.float32), 'Wk': init(ks[2], (H, H), H), 'bk': jnp.zeros((H,), jnp.float32), 'Wv': init(ks[3], (H, H), H), 'bv': jnp.zeros((H,), jnp.float32), 'Wo': init(ks[4], (H, H), H), 'bo': jnp.zeros((H,), jnp.float32), 'Wg': init(ks[5], (H, E), H), 'bg': jnp.zeros((E,), jnp.float32), 'W1': init(ks[6], (E, H, D), H), 'b1': jnp.zeros((E, D), jnp.float32), 'W2': init(ks[7], (E, D, H), D), 'b2': jnp.zeros((E, H), jnp.float32)}
    _L0_ffn_all = _L0_ffn_setup()
    _L0_ffn_in = {k: v for k, v in _L0_ffn_all.items() if k in ('Wq', 'bq', 'Wk', 'bk', 'Wv', 'bv', 'Wo', 'bo', 'Wg', 'bg', 'W1', 'b1', 'W2', 'b2')}
    del _L0_ffn_all

    def _L1_xattn_setup():
        import jax, jax.numpy as jnp
        import numpy as np
        NUM_HEADS = 16
        key = jax.random.key(seed)
        ks = jax.random.split(key, 8)
        dim, cond_dim = (256, 192)
        B, N, condN = (4, 512, 256)
        s = lambda k, shp, fan: jax.random.normal(k, shp, dtype=jnp.float32) * fan ** (-0.5)
        return {'x': jax.random.normal(ks[0], (B, N, dim), dtype=jnp.float32), 'cond': jax.random.normal(ks[1], (B, condN, cond_dim), dtype=jnp.float32), 'q_w': s(ks[2], (dim, dim), dim), 'q_b': jnp.zeros((dim,), jnp.float32), 'kv_w': s(ks[3], (cond_dim, 2 * dim), cond_dim), 'kv_b': jnp.zeros((2 * dim,), jnp.float32), 'proj_w': s(ks[4], (dim, dim), dim), 'proj_b': jnp.zeros((dim,), jnp.float32)}
    _L1_xattn_all = _L1_xattn_setup()
    _L1_xattn_in = {k: v for k, v in _L1_xattn_all.items() if k in ('q_w', 'q_b', 'kv_w', 'kv_b', 'proj_w', 'proj_b')}
    del _L1_xattn_all

    def _L1_attn_setup():
        import jax, jax.numpy as jnp
        import numpy as np
        B, L, E, H = (4, 1024, 256, 16)
        D = E // H
        MLP = 1024
        EPS = 1e-06

        def layer_norm(x, g, b):
            mu = jnp.mean(x, -1, keepdims=True)
            v = jnp.mean((x - mu) ** 2, -1, keepdims=True)
            return (x - mu) * jax.lax.rsqrt(v + 1e-05) * g + b
        key = jax.random.key(seed)
        ks = jax.random.split(key, 16)
        s = 1.0 / np.sqrt(E)
        inp = {'x': jax.random.normal(ks[0], (B, L, E), jnp.float32), 'Wq': jax.random.normal(ks[1], (E, E), jnp.float32) * s, 'bq': jnp.zeros((E,), jnp.float32), 'lnq_g': jnp.ones((E,), jnp.float32), 'lnq_b': jnp.zeros((E,), jnp.float32), 'Wk': jax.random.normal(ks[2], (E, E), jnp.float32) * s, 'bk': jnp.zeros((E,), jnp.float32), 'lnk_g': jnp.ones((E,), jnp.float32), 'lnk_b': jnp.zeros((E,), jnp.float32), 'Wv': jax.random.normal(ks[3], (E, E), jnp.float32) * s, 'bv': jnp.zeros((E,), jnp.float32), 'lnv_g': jnp.ones((E,), jnp.float32), 'lnv_b': jnp.zeros((E,), jnp.float32), 'Wphi_q': jax.random.normal(ks[4], (E, E), jnp.float32) * s, 'bphi_q': jax.random.normal(ks[5], (E,), jnp.float32) * 0.01, 'Wphi_k': jax.random.normal(ks[6], (E, E), jnp.float32) * s, 'bphi_k': jax.random.normal(ks[7], (E,), jnp.float32) * 0.01, 'lna_g': jnp.ones((E,), jnp.float32), 'lna_b': jnp.zeros((E,), jnp.float32), 'W1': jax.random.normal(ks[8], (E, MLP), jnp.float32) * s, 'b1': jnp.zeros((MLP,), jnp.float32), 'W2': jax.random.normal(ks[9], (MLP, E), jnp.float32) * (1.0 / np.sqrt(MLP)), 'b2': jnp.zeros((E,), jnp.float32), 'gamma': jnp.float32(0.1), 'conv_w': jax.random.normal(ks[10], (E, E // H, 5), jnp.float32) * (1.0 / np.sqrt(E // H * 5)), 'conv_b': jnp.zeros((E,), jnp.float32)}
        return inp
    _L1_attn_all = _L1_attn_setup()
    _L1_attn_in = {k: v for k, v in _L1_attn_all.items() if k in ('Wq', 'bq', 'lnq_g', 'lnq_b', 'Wk', 'bk', 'lnk_g', 'lnk_b', 'Wv', 'bv', 'lnv_g', 'lnv_b', 'Wphi_q', 'bphi_q', 'Wphi_k', 'bphi_k', 'lna_g', 'lna_b', 'W1', 'b1', 'W2', 'b2', 'gamma', 'conv_w', 'conv_b')}
    del _L1_attn_all

    def _L1_ffn_setup():
        import jax, jax.numpy as jnp
        import numpy as np
        DM, NE, ES, ESZ = (256, 16, 4, 64)
        BATCH, SEQ = (8, 512)
        key = jax.random.key(seed)
        k = jax.random.split(key, 5)
        scale = 0.02
        return {'x': jax.random.normal(k[0], (BATCH, SEQ, DM), dtype=jnp.float32), 'controller': jax.random.normal(k[1], (DM, NE, ES), dtype=jnp.float32) * scale, 'f1': jax.random.normal(k[2], (DM, NE, ES, ESZ), dtype=jnp.float32) * scale, 'f2': jax.random.normal(k[3], (NE, ES, ESZ, DM), dtype=jnp.float32) * scale, 'bias': jax.random.normal(k[4], (NE, ES, ESZ), dtype=jnp.float32) * scale}
    _L1_ffn_all = _L1_ffn_setup()
    _L1_ffn_in = {k: v for k, v in _L1_ffn_all.items() if k in ('controller', 'f1', 'f2', 'bias')}
    del _L1_ffn_all
    return {'x': x, 'ctx_768': ctx_768, 'L0_xattn_Wq': _L0_xattn_in['Wq'], 'L0_xattn_bq': _L0_xattn_in['bq'], 'L0_xattn_Wk': _L0_xattn_in['Wk'], 'L0_xattn_bk': _L0_xattn_in['bk'], 'L0_xattn_Wv': _L0_xattn_in['Wv'], 'L0_xattn_bv': _L0_xattn_in['bv'], 'L0_xattn_Wo': _L0_xattn_in['Wo'], 'L0_xattn_bo': _L0_xattn_in['bo'], 'L0_attn_in_proj_w': _L0_attn_in['in_proj_w'], 'L0_attn_conv_w': _L0_attn_in['conv_w'], 'L0_attn_conv_b': _L0_attn_in['conv_b'], 'L0_attn_x_proj_w': _L0_attn_in['x_proj_w'], 'L0_attn_dt_proj_w': _L0_attn_in['dt_proj_w'], 'L0_attn_dt_proj_b': _L0_attn_in['dt_proj_b'], 'L0_attn_A_log': _L0_attn_in['A_log'], 'L0_attn_D': _L0_attn_in['D'], 'L0_attn_out_proj_w': _L0_attn_in['out_proj_w'], 'L0_attn_norm_w': _L0_attn_in['norm_w'], 'L0_ffn_Wq': _L0_ffn_in['Wq'], 'L0_ffn_bq': _L0_ffn_in['bq'], 'L0_ffn_Wk': _L0_ffn_in['Wk'], 'L0_ffn_bk': _L0_ffn_in['bk'], 'L0_ffn_Wv': _L0_ffn_in['Wv'], 'L0_ffn_bv': _L0_ffn_in['bv'], 'L0_ffn_Wo': _L0_ffn_in['Wo'], 'L0_ffn_bo': _L0_ffn_in['bo'], 'L0_ffn_Wg': _L0_ffn_in['Wg'], 'L0_ffn_bg': _L0_ffn_in['bg'], 'L0_ffn_W1': _L0_ffn_in['W1'], 'L0_ffn_b1': _L0_ffn_in['b1'], 'L0_ffn_W2': _L0_ffn_in['W2'], 'L0_ffn_b2': _L0_ffn_in['b2'], 'L1_xattn_q_w': _L1_xattn_in['q_w'], 'L1_xattn_q_b': _L1_xattn_in['q_b'], 'L1_xattn_kv_w': _L1_xattn_in['kv_w'], 'L1_xattn_kv_b': _L1_xattn_in['kv_b'], 'L1_xattn_proj_w': _L1_xattn_in['proj_w'], 'L1_xattn_proj_b': _L1_xattn_in['proj_b'], 'L1_attn_Wq': _L1_attn_in['Wq'], 'L1_attn_bq': _L1_attn_in['bq'], 'L1_attn_lnq_g': _L1_attn_in['lnq_g'], 'L1_attn_lnq_b': _L1_attn_in['lnq_b'], 'L1_attn_Wk': _L1_attn_in['Wk'], 'L1_attn_bk': _L1_attn_in['bk'], 'L1_attn_lnk_g': _L1_attn_in['lnk_g'], 'L1_attn_lnk_b': _L1_attn_in['lnk_b'], 'L1_attn_Wv': _L1_attn_in['Wv'], 'L1_attn_bv': _L1_attn_in['bv'], 'L1_attn_lnv_g': _L1_attn_in['lnv_g'], 'L1_attn_lnv_b': _L1_attn_in['lnv_b'], 'L1_attn_Wphi_q': _L1_attn_in['Wphi_q'], 'L1_attn_bphi_q': _L1_attn_in['bphi_q'], 'L1_attn_Wphi_k': _L1_attn_in['Wphi_k'], 'L1_attn_bphi_k': _L1_attn_in['bphi_k'], 'L1_attn_lna_g': _L1_attn_in['lna_g'], 'L1_attn_lna_b': _L1_attn_in['lna_b'], 'L1_attn_W1': _L1_attn_in['W1'], 'L1_attn_b1': _L1_attn_in['b1'], 'L1_attn_W2': _L1_attn_in['W2'], 'L1_attn_b2': _L1_attn_in['b2'], 'L1_attn_gamma': _L1_attn_in['gamma'], 'L1_attn_conv_w': _L1_attn_in['conv_w'], 'L1_attn_conv_b': _L1_attn_in['conv_b'], 'L1_ffn_controller': _L1_ffn_in['controller'], 'L1_ffn_f1': _L1_ffn_in['f1'], 'L1_ffn_f2': _L1_ffn_in['f2'], 'L1_ffn_bias': _L1_ffn_in['bias']}

def reference(x, ctx_768, L0_xattn_Wq, L0_xattn_bq, L0_xattn_Wk, L0_xattn_bk, L0_xattn_Wv, L0_xattn_bv, L0_xattn_Wo, L0_xattn_bo, L0_attn_in_proj_w, L0_attn_conv_w, L0_attn_conv_b, L0_attn_x_proj_w, L0_attn_dt_proj_w, L0_attn_dt_proj_b, L0_attn_A_log, L0_attn_D, L0_attn_out_proj_w, L0_attn_norm_w, L0_ffn_Wq, L0_ffn_bq, L0_ffn_Wk, L0_ffn_bk, L0_ffn_Wv, L0_ffn_bv, L0_ffn_Wo, L0_ffn_bo, L0_ffn_Wg, L0_ffn_bg, L0_ffn_W1, L0_ffn_b1, L0_ffn_W2, L0_ffn_b2, L1_xattn_q_w, L1_xattn_q_b, L1_xattn_kv_w, L1_xattn_kv_b, L1_xattn_proj_w, L1_xattn_proj_b, L1_attn_Wq, L1_attn_bq, L1_attn_lnq_g, L1_attn_lnq_b, L1_attn_Wk, L1_attn_bk, L1_attn_lnk_g, L1_attn_lnk_b, L1_attn_Wv, L1_attn_bv, L1_attn_lnv_g, L1_attn_lnv_b, L1_attn_Wphi_q, L1_attn_bphi_q, L1_attn_Wphi_k, L1_attn_bphi_k, L1_attn_lna_g, L1_attn_lna_b, L1_attn_W1, L1_attn_b1, L1_attn_W2, L1_attn_b2, L1_attn_gamma, L1_attn_conv_w, L1_attn_conv_b, L1_ffn_controller, L1_ffn_f1, L1_ffn_f2, L1_ffn_bias):
    import jax
    import jax.numpy as jnp

    def _L0_xattn_ref(query, key_value, Wq, bq, Wk, bk, Wv, bv, Wo, bo):
        import jax, jax.numpy as jnp
        import numpy as np
        NUM_HEADS = 16
        CLAMP = 10000.0
        B, Nq, Cq = query.shape
        Nkv = key_value.shape[1]
        H = NUM_HEADS
        D = Cq // H
        scale = D ** (-0.5)
        q = (query @ Wq + bq).reshape(B, Nq, H, D).transpose(0, 2, 1, 3)
        k = (key_value @ Wk + bk).reshape(B, Nkv, H, D).transpose(0, 2, 1, 3)
        v = (key_value @ Wv + bv).reshape(B, Nkv, H, D).transpose(0, 2, 1, 3)
        attn = jnp.einsum('bhqd,bhkd->bhqk', q, k) * scale
        attn = jnp.clip(attn, -CLAMP, CLAMP)
        attn = jax.nn.softmax(attn, axis=-1)
        attn = jnp.where(jnp.any(jnp.isnan(attn)), jnp.asarray(1.0 / Nkv, attn.dtype), attn)
        x = jnp.einsum('bhqk,bhkd->bqhd', attn, v).reshape(B, Nq, Cq)
        return x @ Wo + bo

    def _L0_attn_ref(x, in_proj_w, conv_w, conv_b, x_proj_w, dt_proj_w, dt_proj_b, A_log, D, out_proj_w, norm_w):
        import jax, jax.numpy as jnp
        import numpy as np
        D_MODEL = 256
        D_INNER = 512
        D_STATE = 16
        DT_RANK = 64
        D_CONV = 4
        EPS = 1e-05
        B_SZ, L = (2, 512)

        def _silu(x):
            return x * jax.nn.sigmoid(x)
        b, l, d = x.shape
        xn = x * jax.lax.rsqrt(jnp.mean(x * x, axis=-1, keepdims=True) + EPS) * norm_w
        x_and_res = xn @ in_proj_w
        xi, res = jnp.split(x_and_res, 2, axis=-1)
        xc = jax.lax.conv_general_dilated(xi.transpose(0, 2, 1), conv_w, window_strides=(1,), padding=[(D_CONV - 1, 0)], feature_group_count=D_INNER, dimension_numbers=('NCH', 'OIH', 'NCH')) + conv_b[None, :, None]
        xi = _silu(xc.transpose(0, 2, 1))
        x_dbl = xi @ x_proj_w
        delta, Bm, Cm = jnp.split(x_dbl, [DT_RANK, DT_RANK + D_STATE], axis=-1)
        delta = jax.nn.softplus(delta @ dt_proj_w + dt_proj_b)
        A = -jnp.exp(A_log)
        deltaA = jnp.exp(delta[..., None] * A)
        deltaB_u = delta[..., None] * Bm[:, :, None, :] * xi[..., None]

        def step(state, inputs):
            dA_t, dBu_t, C_t = inputs
            state = dA_t * state + dBu_t
            y_t = jnp.einsum('bdn,bn->bd', state, C_t)
            return (state, y_t)
        state0 = jnp.zeros((b, D_INNER, D_STATE), xi.dtype)
        _, ys = jax.lax.scan(step, state0, (deltaA.transpose(1, 0, 2, 3), deltaB_u.transpose(1, 0, 2, 3), Cm.transpose(1, 0, 2)))
        y = ys.transpose(1, 0, 2) + xi * D
        y = y * _silu(res)
        out = y @ out_proj_w + x
        return out

    def _L0_ffn_ref(x, Wq, bq, Wk, bk, Wv, bv, Wo, bo, Wg, bg, W1, b1, W2, b2):
        import jax, jax.numpy as jnp
        import numpy as np
        B, S, H, D, E = (4, 256, 256, 1024, 8)
        q = x @ Wq + bq
        k = x @ Wk + bk
        v = x @ Wv + bv
        scale = jnp.asarray(1.0 / np.sqrt(H), x.dtype)
        scores = jnp.einsum('bqh,bkh->bqk', q, k) * scale
        attn = jax.nn.softmax(scores, axis=-1)
        a = jnp.einsum('bqk,bkh->bqh', attn, v) @ Wo + bo
        x = x + a
        gates = jax.nn.softmax(x @ Wg + bg, axis=-1)
        hmid = jax.nn.relu(jnp.einsum('bsh,ehd->bsed', x, W1) + b1)
        eout = jnp.einsum('bsed,edh->bseh', hmid, W2) + b2
        y = jnp.einsum('bse,bseh->bsh', gates, eout)
        return x + y

    def _L1_xattn_ref(x, cond, q_w, q_b, kv_w, kv_b, proj_w, proj_b):
        import jax, jax.numpy as jnp
        import numpy as np
        NUM_HEADS = 16
        B, N, C = x.shape
        condN = cond.shape[1]
        H = NUM_HEADS
        hd = C // H
        scale = hd ** (-0.5)
        q = (x @ q_w + q_b).reshape(B, N, H, hd).transpose(0, 2, 1, 3)
        kv = (cond @ kv_w + kv_b).reshape(B, condN, 2, H, hd)
        k = kv[:, :, 0].transpose(0, 2, 1, 3)
        v = kv[:, :, 1].transpose(0, 2, 1, 3)
        attn = jnp.einsum('bhnd,bhmd->bhnm', q * scale, k)
        attn = jax.nn.softmax(attn, axis=-1)
        out = jnp.einsum('bhnm,bhmd->bhnd', attn, v)
        out = out.transpose(0, 2, 1, 3).reshape(B, N, C)
        return out @ proj_w + proj_b

    def _L1_attn_ref(x, Wq, bq, lnq_g, lnq_b, Wk, bk, lnk_g, lnk_b, Wv, bv, lnv_g, lnv_b, Wphi_q, bphi_q, Wphi_k, bphi_k, lna_g, lna_b, W1, b1, W2, b2, gamma, conv_w, conv_b):
        import jax, jax.numpy as jnp
        import numpy as np
        B, L, E, H = (4, 1024, 256, 16)
        D = E // H
        MLP = 1024
        EPS = 1e-06

        def layer_norm(x, g, b):
            mu = jnp.mean(x, -1, keepdims=True)
            v = jnp.mean((x - mu) ** 2, -1, keepdims=True)
            return (x - mu) * jax.lax.rsqrt(v + 1e-05) * g + b
        Bx, Lq, Ex = x.shape
        Q = layer_norm(x @ Wq + bq, lnq_g, lnq_b)
        K = layer_norm(x @ Wk + bk, lnk_g, lnk_b)
        V = layer_norm(x @ Wv + bv, lnv_g, lnv_b)
        Z = jnp.zeros((Bx, 1, Ex), x.dtype)
        K = jnp.concatenate([Z, K], axis=1)
        V = jnp.concatenate([Z, V], axis=1)
        phiQ = jnp.tanh(Q @ Wphi_q + bphi_q) + 1.0
        phiK = jnp.tanh(K @ Wphi_k + bphi_k) + 1.0
        sh = lambda t: t.reshape(Bx, -1, H, D)
        Qh, Kh, Vh, pQ, pK = (sh(Q), sh(K), sh(V), sh(phiQ), sh(phiK))
        qg = jnp.mean(Qh, axis=1, keepdims=True) / np.sqrt(D)
        scores = jnp.einsum('bihd,blhd->bihl', qg, Kh)
        alpha = jax.nn.softmax(scores, axis=-1) * Lq
        alpha = jnp.transpose(alpha[:, 0], (0, 2, 1))[..., None]
        pKs = pK * alpha
        K_sum = pKs.sum(axis=1)
        KV = jnp.einsum('blhd,blhe->bhde', pKs, Vh)
        num = jnp.einsum('blhd,bhde->blhe', pQ, KV)
        den = jnp.einsum('blhd,bhd->blh', pQ, K_sum)[..., None] + EPS
        attn = (num / den).reshape(Bx, Lq, Ex)
        xt = jnp.transpose(attn, (0, 2, 1))
        conv = jax.lax.conv_general_dilated(xt, conv_w, (1,), [(2, 2)], feature_group_count=H)
        local = gamma * (conv + conv_b[None, :, None])
        attn = attn + jnp.transpose(local, (0, 2, 1))
        attn = layer_norm(attn, lna_g, lna_b)
        h = jax.nn.gelu(attn @ W1 + b1, approximate=False) @ W2 + b2
        return attn + h + x

    def _L1_ffn_ref(x, controller, f1, f2, bias):
        import jax, jax.numpy as jnp
        import numpy as np
        DM, NE, ES, ESZ = (256, 16, 4, 64)
        BATCH, SEQ = (8, 512)
        ne = controller.shape[1]
        d = x.shape[-1]
        grouped = x.reshape(x.shape[:-2] + (-1, ne, d))
        logits = jnp.einsum('...btd,des->...btes', grouped, controller)
        tie = jnp.linspace(0.0, 1e-06, ne, dtype=logits.dtype).reshape(ne, 1, 1)
        logits = logits + tie
        perm = (logits == jnp.max(logits, axis=-3, keepdims=True)).astype(x.dtype)
        sel = jnp.einsum('...btd,...btes->...besd', grouped, perm)
        inner = jax.nn.relu(jnp.einsum('...besd,desf->...besf', sel, f1) + bias)
        inter = jnp.einsum('...besf,esfd->...besd', inner, f2)
        out = jnp.einsum('...besd,...btes->...btd', inter, perm)
        return out.reshape(x.shape)
    x = x + _L0_xattn_ref(_layernorm(x, axis=-1), ctx_768, L0_xattn_Wq, L0_xattn_bq, L0_xattn_Wk, L0_xattn_bk, L0_xattn_Wv, L0_xattn_bv, L0_xattn_Wo, L0_xattn_bo)
    x = x + _L0_attn_ref(_layernorm(x, axis=-1), L0_attn_in_proj_w, L0_attn_conv_w, L0_attn_conv_b, L0_attn_x_proj_w, L0_attn_dt_proj_w, L0_attn_dt_proj_b, L0_attn_A_log, L0_attn_D, L0_attn_out_proj_w, L0_attn_norm_w)
    x = x + _L0_ffn_ref(_layernorm(x, axis=-1), L0_ffn_Wq, L0_ffn_bq, L0_ffn_Wk, L0_ffn_bk, L0_ffn_Wv, L0_ffn_bv, L0_ffn_Wo, L0_ffn_bo, L0_ffn_Wg, L0_ffn_bg, L0_ffn_W1, L0_ffn_b1, L0_ffn_W2, L0_ffn_b2)
    x = x + _L1_xattn_ref(_layernorm(x, axis=-1), ctx_768, L1_xattn_q_w, L1_xattn_q_b, L1_xattn_kv_w, L1_xattn_kv_b, L1_xattn_proj_w, L1_xattn_proj_b)
    x = x + _L1_attn_ref(_layernorm(x, axis=-1), L1_attn_Wq, L1_attn_bq, L1_attn_lnq_g, L1_attn_lnq_b, L1_attn_Wk, L1_attn_bk, L1_attn_lnk_g, L1_attn_lnk_b, L1_attn_Wv, L1_attn_bv, L1_attn_lnv_g, L1_attn_lnv_b, L1_attn_Wphi_q, L1_attn_bphi_q, L1_attn_Wphi_k, L1_attn_bphi_k, L1_attn_lna_g, L1_attn_lna_b, L1_attn_W1, L1_attn_b1, L1_attn_W2, L1_attn_b2, L1_attn_gamma, L1_attn_conv_w, L1_attn_conv_b)
    x = x + _L1_ffn_ref(_layernorm(x, axis=-1), L1_ffn_controller, L1_ffn_f1, L1_ffn_f2, L1_ffn_bias)
    return x

_drawn_inputs = setup_inputs


def setup_inputs(seed=0):
    import zlib

    import numpy as np

    out = dict(_drawn_inputs(seed))
    spreads = {'L0_xattn_bq': (0.0, 0.354),
     'L0_xattn_bk': (0.0, 2.0),
     'L0_xattn_bv': (0.0, 0.1),
     'L0_xattn_bo': (0.0, 0.1),
     'L0_attn_conv_b': (0.0, 0.8),
     'L0_attn_D': (1.0, 0.6),
     'L0_attn_norm_w': (1.0, 0.6),
     'L0_ffn_bq': (0.0, 2.0),
     'L0_ffn_bk': (0.0, 2.0),
     'L0_ffn_bv': (0.0, 0.8),
     'L0_ffn_bo': (0.0, 0.8),
     'L0_ffn_bg': (0.0, 2.0),
     'L0_ffn_b1': (0.0, 2.0),
     'L0_ffn_b2': (0.0, 2.0),
     'L1_xattn_q_b': (0.0, 2.0),
     'L1_xattn_kv_b': (0.0, 2.0),
     'L1_xattn_proj_b': (0.0, 2.0),
     'L1_attn_bq': (0.0, 2.0),
     'L1_attn_lnq_g': (1.0, 0.6),
     'L1_attn_lnq_b': (0.0, 2.0),
     'L1_attn_bk': (0.0, 2.0),
     'L1_attn_lnk_g': (1.0, 0.6),
     'L1_attn_lnk_b': (0.0, 2.0),
     'L1_attn_bv': (0.0, 2.0),
     'L1_attn_lnv_g': (1.0, 0.6),
     'L1_attn_lnv_b': (0.0, 2.0),
     'L1_attn_lna_g': (1.0, 0.6),
     'L1_attn_lna_b': (0.0, 2.0),
     'L1_attn_b1': (0.0, 2.0),
     'L1_attn_b2': (0.0, 2.0),
     'L1_attn_conv_b': (0.0, 2.0)}
    factors = {'L0_attn_in_proj_w': 8.0,
     'L0_attn_conv_w': 8.0,
     'L0_attn_x_proj_w': 8.0,
     'L0_attn_dt_proj_w': 8.0,
     'L0_attn_dt_proj_b': 8.0,
     'L0_attn_A_log': 8.0,
     'L0_attn_out_proj_w': 8.0,
     'L1_attn_Wphi_q': 200.0,
     'L1_attn_bphi_q': 200.0,
     'L1_attn_Wphi_k': 200.0,
     'L1_attn_bphi_k': 200.0,
     'L1_ffn_controller': 28.496,
     'L1_ffn_f1': 104.607,
     'L1_ffn_f2': 27.696,
     'L1_ffn_bias': 200.0,
     'L0_ffn_Wq': 8.0,
     'L0_ffn_Wk': 8.0,
     'L0_ffn_Wv': 8.0,
     'L0_ffn_Wo': 8.0,
     'L0_ffn_Wg': 8.0,
     'L0_ffn_W1': 8.0,
     'L0_ffn_W2': 8.0,
     'L1_xattn_q_w': 8.0,
     'L1_xattn_kv_w': 8.0,
     'L1_xattn_proj_w': 8.0,
     'L1_attn_Wq': 64.0,
     'L1_attn_Wk': 31.984,
     'L1_attn_Wv': 31.907,
     'L1_attn_W1': 8.0,
     'L1_attn_W2': 8.0,
     'L1_attn_conv_w': 38.941}
    for name, (base, spread) in spreads.items():
        noise = np.random.default_rng([zlib.crc32(name.encode()), seed]).standard_normal(out[name].shape)
        drawn = base * np.exp(spread * noise) if base else spread * noise
        out[name] = jnp.asarray(drawn.astype(out[name].dtype))
    for name, factor in factors.items():
        out[name] = (out[name] * factor).astype(out[name].dtype)
    return out
```

```python
from contextlib import ExitStack

import concourse.bass as bass
from concourse import mybir

ALU = mybir.AluOpType
ACT = mybir.ActivationFunctionType
F32 = mybir.dt.float32
BF16 = mybir.dt.bfloat16
AX_X = mybir.AxisListType.X

P = 128
TOK = 128
D = 256
KC = D // P
CTX = 12544
CC = 192
CP = 96
H = 16
HD = D // H
CK = 896
NCH = CTX // CK
TPC = CK // P
HALF = CK // 2
SLOTS = 6
VW = 32
UNITS = 2 * TPC
Q_SPLIT = (0, 1, 2, 0, 1, 0)
K_SPLIT = (0, 0, 0, 1, 1, 2)
EPS = 1e-5
PAIR_OF_ONES = 1.0019378662109375
DI = 512
NB = DI // P
NS = 16
RANK = 64
TAPS = 4
NE = 8
HID = 1024
HB = HID // P
CONV = 5
GR = 16
NG = TOK // GR
ES = 64
EF = 64
PAIRS = ES // 2

A_KST, A_V, A_CTX = 0, 14336, 21504
A_KTF, A_RES, A_KP, A_O, ARENA = 25088, 26880, 28672, 31360, 32768
W_WORDS = 6304

COLS = {}
_n = 0
for _name, _w in (("L0_xattn_bq", KC), ("L0_xattn_bk", KC), ("L1_xattn_q_b", KC), ("L1_xattn_k_b", KC),
                  ("norm_w", KC), ("conv_w", NB * TAPS), ("conv_b", NB), ("dt_b", NB), ("D", NB),
                  ("A_log", NB * NS), ("ffn_bq", KC), ("ffn_bk", KC), ("ffn_b1", NE * HB),
                  ("lconv_b", KC), ("mlp_b1", HB), ("bias", PAIRS)):
    COLS[_name] = (_n, _n + _w)
    _n += _w
NCOLS = _n
ROWS = {}
_n = 0
for _name, _w in (("L0_xattn_bv", D), ("L0_xattn_bo", D), ("L1_xattn_v_b", D), ("L1_xattn_proj_b", D),
                  ("ffn_bv", D), ("ffn_bo", D), ("ffn_bg", NE), ("tie", TOK), ("gamma", 1)):
    ROWS[_name] = (_n, _n + _w)
    _n += _w
NROWS = _n
ROWS1 = {}
_n = 0
for _name, _w in (("bq", D), ("bk", D), ("bv", D), ("lnq_g", D), ("lnk_g", D), ("lnv_g", D),
                  ("lnq_b", D), ("lnk_b", D), ("lnv_b", D), ("bphi_q", D), ("bphi_k", D),
                  ("lna_g", D), ("lna_b", D), ("b2", D)):
    ROWS1[_name] = (_n, _n + _w)
    _n += _w
NROWS1 = _n
STACK = 16 * SLOTS * KC
C_ID, C_BLOCK, C_GROUP, NCONST = 0, 128, 256, 256 + NG


def iteration_plan():
    plan = [("row", 0)] + [("v", n) for n in range(4)] + [("o", 0)]
    plan += [("s", 0), ("e", 0), ("s", 1), ("e", 1)]
    maxima = [("b", n) for n in range(2 * H)]
    keys = {0: 0, 1: 1, 3: 2, 4: 3}
    splits = {2: [("k1", 0), ("r", 0)], 5: [("k1", 1), ("r", 1)], 6: [("k2", 0), ("k3", 0)],
              7: [("k2", 1), ("k3", 1)]}
    for u in range(UNITS):
        plan.append(("pv", u))
        if u + 2 < UNITS:
            plan += [("s", u + 2), ("e", u + 2)]
        if u in keys:
            plan.append(("k", keys[u]))
        plan += [maxima.pop(0) for _ in range(min(2 if u in keys else 3, len(maxima)))]
        plan += splits.get(u, [])
    plan += maxima + [("m", 0), ("ot", 0)]
    return plan


RING_STEPS = ("row", "v", "o", "b", "k")
RING = 3

SIGNALS = {
    "mamba_pe": ("rmsT_full", "x_dbl_full", "dt_full", "mamba_full"),
    "mamba_act": ("M_std", "M2_std", "A_exp", "res_exp", "xc_exp", "sp_exp", "sp_ln"),
    "mamba_dve": ("M_var", "M_normed", "M2_var", "rms_normed", "rmsT_ready", "A_ready", "conv_ready", "xi_ready",
                  "dr_ready", "bcT_ready", "negabs_ready", "sp_u", "delta_ready", "dtu_ready", "y_ready",
                  "mamba_done"),
    "ffn_pe": ("FxT_full", "Fqk_full", "Fv_full", "Fs_full", "FpT_full", "Fa_full", "FaT_full", "Fo_full",
               "Fx1T_full", "Fg_full", "FgT_full", "Fb2_full"),
    "ffn_act": ("F_std", "FxT_ready", "Fexp_done", "FpT_ready", "Fa_ready", "FaT_ready", "Fx1T_ready",
                "Fgexp_done", "FgT_ready"),
    "ffn_dve": ("F_var", "F_normed", "Fqk_ready", "Fmax_ready", "Fp_ready", "Fx1_ready", "Fgmax_ready",
                "Fg_ready", "ffn_done"),
    "linear_pe": ("GxT_full", "Gqg_full", "GQT_full", "GscT_full", "Gal_full", "GpQT_full", "Gks_full",
                  "GKV_full", "Gnum_full", "GaT_full", "Gconv_full", "Ga2_full", "Ga3T_full", "Gy_full"),
    "linear_act": ("G_std", "GxT_ready", "GQ_std", "GQT_ready", "Gexp_done", "GpQT_ready", "GaT_ready", "GA_std",
                   "Ga3T_ready", "GgT_ready"),
    "linear_dve": ("G_var", "G_normed", "GQ_var", "Gqkv_ready", "Gsc_ready", "GscT_ready", "Gphi_biased",
                   "GalT_ready", "Gphi_ready", "Gpks_ready", "GKV_ready", "Gattn_ready", "GaT2_ready", "GA_var",
                   "GA_normed", "Ga3_ready"),
    "sets_pe": ("SxT_full", "Slog_full", "Sperm_full", "Sinn_full", "Sy_full"),
    "sets_act": ("S_std", "SxT_ready", "Ssel_ready"),
    "sets_dve": ("S_var", "S_normed", "perm_ready", "Spd_ready", "Sgx_ready"),
}
GROUP_OF = {name: (group, n + 1) for group, names in SIGNALS.items() for n, name in enumerate(names)}


def slots_of(plan, first):
    out, pos = {}, first
    last = {}
    for step in plan:
        if step[0] in RING_STEPS:
            out[step] = (pos % RING, last.get(pos % RING))
            last[pos % RING] = step
            pos += 1
    return out, last


def build(nc, a, out, stop=99):
    with ExitStack() as ctx:
        def sb(name, shape, dt=F32):
            return ctx.enter_context(nc.sbuf_tensor(name, shape, dt))

        sems = {}

        def sem(name):
            if name not in sems:
                sems[name] = ctx.enter_context(nc.semaphore(name))
            return sems[name]

        signalled = {}

        def signal(name):
            group, n = GROUP_OF.get(name, (None, 1))
            if group:
                assert signalled.get(group, 0) == n - 1, name
                signalled[group] = n
            return sem(group or name), 1

        def done_of(name):
            group, n = GROUP_OF.get(name, (None, 1))
            return sem(group or name), n

        arena = sb("arena", [P, ARENA])
        warena = sb("warena", [P, W_WORDS])
        cols = sb("cols_sb", [P, NCOLS])
        rows = sb("rows_sb", [P, NROWS])
        consts = sb("consts_sb", [P, NCONST])
        xr = sb("xr", [P, D])
        xn = sb("xn", [P, D])
        xT = sb("xT", [P, KC, TOK])
        wx = sb("wx", [P, 2, 2, D])
        wkv = sb("wkv", [CP, 2, 2, D])
        qst = sb("qst", [CP + 1, 2, H, TOK], BF16)
        qparts = sb("qparts", [P, 3, KC, TOK], BF16)
        mpart = sb("mpart", [P, 2 * H])
        mneg = sb("mneg", [P, H])
        nmb = sb("nmb", [P, 2, H], BF16)
        nmf = sb("nmf", [P, 2, H])
        mdiff = sb("mdiff", [P, H])
        alpha = sb("alpha", [P, 2, H])
        rowb = sb("rowb", [H, TOK], BF16)
        stats = sb("stats", [P, 3, 6])
        mv = sb("mv", [P, 3, 2])
        var = sb("var", [P, 3])
        std = sb("std", [P, 3])
        rstd = sb("rstd", [P, 3])
        tmp = [sb(f"tmp{i}", [P, D]) for i in range(2)]
        small = sb("small", [P, 64])

        def af(lo, n):
            return arena[:, lo:lo + n]

        kst = arena[:, A_KST:A_V].bitcast(BF16).rearrange("p (b h k) -> p b h k", b=2, h=H)
        vv = af(A_V, 2 * TPC * H * VW).rearrange("p (b t h d) -> p b t h d", b=2, t=TPC, h=H)
        ctxt = af(A_CTX, 2 * 2 * CK).rearrange("p (b c k) -> p b c k", b=2, c=2)
        ktf = af(A_KTF, 2 * CK)
        res = af(A_RES, 2 * CK)
        kparts = af(A_KP, 3 * CK).bitcast(BF16).rearrange("p (s k) -> p s k", s=3)
        oacc = af(A_O, H * VW).rearrange("p (h d) -> p h d", h=H)
        ots = af(A_O + H * VW, 4 * TOK)
        work = sb("work", [P, 3976])
        pbuf = work[:, 0:2 * 8 * TOK].rearrange("p (b k) -> p b k", b=2)

        st = ctx.enter_context(nc.psum_tensor("st", [P, 4, 512], F32))
        ot = ctx.enter_context(nc.psum_tensor("ot", [P, 512], F32))
        ring = ctx.enter_context(nc.psum_tensor("ring", [P, RING, 512], F32))
        pb = [st[:, i] for i in range(4)] + [ot[:, :]] + [ring[:, i] for i in range(RING)]

        ident = consts[:, C_ID:C_ID + P]
        blockmask = consts[:, C_BLOCK:C_BLOCK + P]
        groupmask = consts[:, C_GROUP:C_GROUP + NG]

        def col(name):
            return cols[:, COLS[name][0]:COLS[name][1]]

        def row(name):
            return rows[:, ROWS[name][0]:ROWS[name][1]]

        def row1(name):
            return rows1[:, ROWS1[name][0]:ROWS1[name][1]]

        scratch_bc = nc.dram_tensor("scratch_bc", [2 * NS, TOK], F32).ap()
        scratch_perm = nc.dram_tensor("scratch_perm", [ES, TOK], F32).ap()

        def carve(base, shapes):
            views, at = {}, 0
            for name, dims in shapes:
                n = 1
                for d in dims:
                    n *= d
                v = base[:, at:at + n]
                if len(dims) == 2:
                    v = v.rearrange("p (a b) -> p a b", a=dims[0])
                if len(dims) == 3:
                    v = v.rearrange("p (a b c) -> p a b c", a=dims[0], b=dims[1])
                views[name] = v
                at += n
            assert at <= base.shape[1], (at, base.shape)
            return views

        w0 = carve(warena[:, :], (("in_proj", (KC, 2 * DI)), ("x_proj", (NB, RANK + 2 * NS)), ("dt_proj", (DI,)),
                                  ("out_proj", (NB, D)), ("Wq", (KC, D)), ("Wk", (KC, D)), ("Wv", (KC, D)),
                                  ("Wo", (KC, D)), ("Wg", (KC, NE)), ("b2", (D,))))
        w1 = carve(warena[:, :], (("Wq", (KC, D)), ("Wk", (KC, D)), ("Wv", (KC, D)), ("Wphi_q", (KC, D)),
                                  ("Wphi_k", (KC, D)), ("W1", (KC, HID)),
                                  ("conv_w", (KC, CONV, HD)), ("controller", (KC, ES))))
        m_ = carve(arena[:, 4 * 4096:], (("dA", (2, NS * TOK)), ("dBu", (2, NS * TOK)), ("h", (NS * TOK,)),
                                         ("bc", (2 * NS * TOK,)), ("dr", (TOK,)), ("bcT", (TOK,)),
                                         ("A", (NB * NS,))))
        m2 = carve(arena[:, 4 * 4096 + 14656:], (("xpad", (NB, TOK + TAPS - 1)), ("xi", (NB, TOK)),
                                                       ("sres", (NB, TOK))))
        m3 = carve(work[:, :], tuple((n, (NB, TOK)) for n in ("z", "e", "u", "l", "dtu")))
        ew = [carve(af(4096 * e, 4096), (("W1", (KC, HID)), ("W2", (HB, D)))) for e in range(NE)]
        f_ = carve(work[:, :], (("q", (KC, TOK)), ("k", (KC, TOK)), ("v", (D,)), ("p", (TOK,)),
                                                 ("pT", (TOK,)), ("aT", (KC, TOK)), ("x1", (D,)),
                                                 ("hT", (HB, TOK)), ("hT1", (HB, TOK)), ("g", (NE,)), ("gT", (TOK,)), ("y", (D,))))
        hT2 = [f_["hT"], f_["hT1"]]

        f1 = af(0, KC * ES * EF).rearrange("p (k n) -> p k n", k=KC)
        f2 = af(8192, PAIRS * D).rearrange("p (k n) -> p k n", k=PAIRS)
        permx = af(16384, PAIRS * TOK).rearrange("p (k n) -> p k n", k=PAIRS)
        mlp_w2 = af(16384, HB * D).rearrange("p (k n) -> p k n", k=HB)
        rows1 = af(20480, NROWS1)
        l_ = carve(arena[:, 24576:], (("qkv", (3, D)), ("QT", (2, KC, TOK)), ("phi", (2, D)), ("prod", (D,)),
                                      ("scT", (TOK + 1,)), ("pks", (D,)), ("pk0", (D,)), ("KV", (KC, P)),
                                      ("pQT", (KC, TOK)), ("attn", (D,)), ("aT", (KC, TOK + CONV - 1)),
                                      ("aT2", (KC, TOK)), ("a3", (D,)), ("gT", (HB, TOK)),
                                      ("cw", (KC * CONV, P)), ("mean", (P,)), ("ones", (P,)), ("permT", (TOK,)), ("perm", (ES,)),
                                      ("gmax", (NG,)), ("alpha", (H,)), ("ksum", (D,)), ("den", (H,))))
        pdiag = af(20480, ES * NG).rearrange("p (e g) -> p e g", g=NG)
        selT = af(20480 + 512, KC * 512).rearrange("p (k n) -> p k n", k=KC)
        innT = af(20480 + 1536, PAIRS * NG).rearrange("p (k n) -> p k n", k=PAIRS)

        block = ctx.enter_context(nc.Block())

        
        FREE = {"row": ("row_out", 1), "v": ("v_out", 4), "o": ("o_added", 1), "b": ("b_max", 2 * H), "k": ("k_out", 4)}
        AHEAD = {"row": 0, "v": 1, "o": 1, "b": 1, "k": 2}

        def ring_free(pe, lay, step, c):
            kind, n = step
            name, per = FREE[kind]
            pe.wait_ge(sem(f"{lay}_{name}"), (c + AHEAD[kind]) * per + n + 1)

        PLAN = iteration_plan()
        LOOP_SLOTS, LOOP_LAST = slots_of(PLAN, 0)
        PRO = [("k", n) for n in range(4)] + [("k", 4 + n) for n in range(4)] + [("v", n) for n in range(4)] + \
              [("b", n) for n in range(2 * H)]
        PRO_SLOTS, PRO_LAST = slots_of(PRO, 1)
        assert {s: x for s, x in LOOP_LAST.items()} == PRO_LAST and sum(s[0] in RING_STEPS for s in PLAN) % RING == 0

        @block.sync
        def _(sp):
            def load(dst, src, name):
                sp.dma_start(dst, src).then_inc(sem(name), 16)

            def chunked(w):
                return w.rearrange("(k p) n -> p k n", p=P)

            load(xr[:, :], a["x"], "x_in")
            load(consts[:, :], a["consts"], "const_in")
            load(cols[:, :], a["cols"], "const_in")
            load(rows[:, :], a["rows"].partition_broadcast(P), "const_in")

            def attention_weights(lay, pre):
                load(wx[:, 0], chunked(a[f"{lay}_wq"]), f"{lay}_w_in")
                load(wx[:, 1], chunked(a[f"{lay}_wo"]), f"{lay}_w_in")
                for n in range(2):
                    load(wkv[:, :, n], a[f"{lay}_wkv"][n].rearrange("(k p) n -> p k n", p=CP), f"{lay}_w_in")

            def load_ctx(lay, par, at):
                load(ctxt[0:CP, par], a["ctxT"].rearrange("(k p) n -> p k n", p=CP)[:, :, bass.ds(at, CK)],
                     f"{lay}_ctx_in{par}")

            def stack(lay, par, count):
                for s, part in enumerate(K_SPLIT):
                    if s in (0, 3, 5):
                        sp.wait_ge(sem(f"{lay}_k{part + 1}_done"), KC * count)
                    for m in range(KC):
                        load(kst[HD * s:HD * (s + 1), par, 8 * m:8 * m + 8],
                             kparts[:, part, m * CK:(m + 1) * CK], f"{lay}_kst_in{par}")

            def attention_loads(lay):
                sp.wait_ge(*done_of(f"{lay}_q_split"))
                for b in range(2):
                    for s, part in enumerate(Q_SPLIT):
                        for m in range(KC):
                            load(qst[HD * s:HD * (s + 1), b, 8 * m:8 * m + 8], qparts[:, part, m],
                                 f"{lay}_qst_in")
                stack(lay, 0, 1)
                sp.wait_ge(sem(f"{lay}_v_full"), 4)
                load_ctx(lay, 0, 2 * CK)

                stack(lay, 1, 2)

                def step(par, c, more):
                    sp.wait_ge(sem(f"{lay}_s_full"), (c + 1) * UNITS)
                    if more:
                        load_ctx(lay, 1 - par, (c + 3) * CK)
                    stack(lay, par, c + 3)

                with sp.Fori(0, 5) as i:
                    for par in range(2):
                        step(par, 2 * i + par, True)
                step(0, 10, True)
                step(1, 11, False)

            attention_weights("L0", "L0_xattn")
            load_ctx("L0", 0, 0)
            load_ctx("L0", 1, CK)
            for name in ("in_proj", "out_proj", "Wq", "Wk", "Wv", "Wo", "Wg"):
                load(w0[name], chunked(a["w0_" + name]), "w0_in")
            load(w0["x_proj"], chunked(a["w0_x_proj"]), "w0_in")
            load(w0["dt_proj"][0:RANK], a["w0_dt_proj"], "w0_in")
            load(w0["b2"][0:NE], a["w0_b2"], "w0_in")
            attention_loads("L0")
            if stop >= 2:
                sp.wait_ge(*done_of("L0_attended"))
                for e in range(4):
                    load(ew[e]["W1"], chunked(a["ffn_W1"][e]), f"expert_in{e}")
                    load(ew[e]["W2"], chunked(a["ffn_W2"][e]), f"expert_in{e}")
                attention_weights("L1", "L1_xattn")
                sp.wait_ge(*done_of("bcT_ready"))
                sp.dma_start(scratch_bc, m_["bcT"][RANK:RANK + 2 * NS]).then_inc(sem("bc_out"), 16)
                sp.wait_ge(sem("bc_out"), 16)
                load(m_["bc"], scratch_bc.rearrange("n t -> (n t)").partition_broadcast(P), "bc_in")
            if stop >= 3:
                sp.wait_ge(*done_of("mamba_done"))
                for e in range(4, NE):
                    load(ew[e]["W1"], chunked(a["ffn_W1"][e]), f"expert_in{e}")
                    load(ew[e]["W2"], chunked(a["ffn_W2"][e]), f"expert_in{e}")
            if stop >= 4:
                sp.wait_ge(*done_of("ffn_done"))
                load_ctx("L1", 0, 0)
                load_ctx("L1", 1, CK)
                for name in ("Wq", "Wk", "Wv", "Wphi_q", "Wphi_k", "W1", "controller"):
                    load(w1[name], chunked(a["w1_" + name]), "w1_in")
                load(w1["conv_w"], a["w1_conv_w"].rearrange("(k p) c o -> p k c o", p=P), "w1_in")
                attention_loads("L1")
            if stop >= 5:
                sp.wait_ge(*done_of("L1_attended"))
                load(rows1, a["rows1"].partition_broadcast(P), "rows1_in")
                load(mlp_w2, chunked(a["w1_W2"]), "W2_in")
                load(f1, a["f1"].rearrange("(k p) n -> p k n", p=P), "f1_in")
                load(f2, a["f2"].rearrange("(k p) n -> p k n", p=P), "f2_in")
            if stop >= 6:
                sp.wait_ge(*done_of("perm_ready"))
                sp.dma_start(scratch_perm, l_["permT"][0:ES]).then_inc(sem("perm_out"), 16)
                sp.wait_ge(sem("perm_out"), 16)
                for par in range(2):
                    load(permx[par * EF:(par + 1) * EF],
                         scratch_perm.rearrange("(q par) t -> par q t", par=2)[par].partition_broadcast(EF), "permx_in")
            sp.wait_ge(*done_of("result_ready"))
            sp.dma_start(out, xr[:, :]).then_inc(sem("stored"), 16)
            sp.wait_ge(sem("stored"), 16)

        @block.gpsimd
        def _(pool):
            def attention(lay):
                def rest(c, m):
                    pool.wait_ge(sem(f"{lay}_k1_done"), KC * c + m + 1)
                    nc.gpsimd.tensor_tensor(res[:, m * CK:(m + 1) * CK], ktf[:, m * CK:(m + 1) * CK],
                                            kparts[:, 0, m * CK:(m + 1) * CK], ALU.subtract
                                            ).then_inc(*signal(f"{lay}_r_done"))
                    pool.wait_ge(sem(f"{lay}_r_done"), KC * c + m + 1)

                def third(c, m):
                    pool.wait_ge(sem(f"{lay}_k2_done"), KC * c + m + 1)
                    nc.gpsimd.tensor_tensor(kparts[:, 2, m * CK:(m + 1) * CK], res[:, m * CK:(m + 1) * CK],
                                            kparts[:, 1, m * CK:(m + 1) * CK], ALU.subtract
                                            ).then_inc(*signal(f"{lay}_k3_done"))
                    pool.wait_ge(sem(f"{lay}_k3_done"), KC * c + m + 1)

                def split(c):
                    for m in range(KC):
                        rest(c, m)
                    for m in range(KC):
                        third(c, m)

                split(0)
                split(1)
                nc.gpsimd.memset(vv[:, :, :, :, HD:], 0.0).then_inc(*signal(f"{lay}_zeros_set"))
                pool.wait_ge(*done_of(f"{lay}_zeros_set"))
                nc.gpsimd.memset(vv[:, :, :, :, HD:HD + 1], 1.0).then_inc(*signal(f"{lay}_ones_set"))
                pool.wait_ge(sem(f"{lay}_ones_set"), 1)
                nc.gpsimd.memset(arena[CP:CP + 1, A_KST:A_V], PAIR_OF_ONES).then_inc(*signal(f"{lay}_ones_set"))
                pool.wait_ge(sem(f"{lay}_ones_set"), 2)
                with pool.Fori(2, NCH) as c:
                    split(c)

            attention("L0")
            if stop >= 2:
                pool.wait_ge(*done_of("dtu_ready"))
                pool.wait_ge(sem("bc_in"), 16)
                for b in range(NB):
                    if b >= 2:
                        pool.wait_ge(sem("scanned"), b - 1)
                    nc.gpsimd.tensor_tensor(
                        m_["dBu"][:, b % 2].rearrange("p (n t) -> p n t", n=NS),
                        m3["dtu"][:, b:b + 1].broadcast_to([P, NS, TOK]),
                        m_["bc"][:, 0:NS * TOK].rearrange("p (n t) -> p n t", n=NS), ALU.mult).then_inc(*signal("dBu_ready"))
            if stop >= 4:
                attention("L1")

        @block.tensor
        def _(pe):
            def mm(o, l, r, start=True, stop=True, **kw):
                return nc.tensor.matmul(o, l, r, start=start, stop=stop, **kw)

            def transpose2(src, bank, ready, done):
                pe.wait_ge(*done_of(ready))
                for k in range(KC):
                    last = nc.tensor.transpose(pb[bank][:, k * P:(k + 1) * P], src[:, k * P:(k + 1) * P], ident)
                last.then_inc(*signal(done))

            def project(bank, lhs, rhs, done, n=KC):
                for k in range(n):
                    last = mm(bank, lhs(k), rhs(k), start=(k == 0), stop=(k == n - 1))
                if done:
                    last.then_inc(*signal(done))
                return last

            def attention(lay):
                transpose2(xn, 5, f"{lay}_ln_normed", f"{lay}_xT_full")
                pe.wait_ge(*done_of(f"{lay}_xT_ready"))
                pe.wait_ge(sem(f"{lay}_w_in"), 64)
                for m in range(KC):
                    project(pb[6][:, m * P:(m + 1) * P], lambda k: wx[:, 0, k, m * P:(m + 1) * P],
                            lambda k: xT[:, k], f"{lay}_q_full")
                pe.wait_ge(*done_of(f"{lay}_q_split"))

                def k_group(n, par, bank):
                    m, hf = n // 2, n % 2
                    project(ring[:, bank, 0:HALF], lambda k: wkv[:, k, 0, m * P:(m + 1) * P],
                            lambda k: ctxt[0:CP, par, k, hf * HALF:(hf + 1) * HALF], f"{lay}_k_full", 2)

                def v_group(n, par, bank):
                    tiles = range(2 * n, min(2 * n + 2, TPC))
                    for t in tiles:
                        last = project(ring[:, bank, (t % 2) * D:(t % 2 + 1) * D],
                                       lambda k: ctxt[0:CP, par, k, t * P:(t + 1) * P],
                                       lambda k: wkv[:, k, 1, :], None, 2)
                    last.then_inc(*signal(f"{lay}_v_full"))

                def b_group(n, par, bank):
                    h, hf = n // 2, n % 2
                    return mm(ring[:, bank, 0:HALF], qst[0:CP, 0, h], kst[0:CP, par, h, hf * HALF:(hf + 1) * HALF])

                for step in PRO:
                    kind, n = step
                    bank, before = PRO_SLOTS[step]
                    if before:
                        name = FREE[before[0]][0]
                        pe.wait_ge(sem(f"{lay}_{name}"), before[1] + 1)
                    if kind == "k":
                        pe.wait_ge(sem(f"{lay}_ctx_in{n // 4}"), 16)
                        k_group(n % 4, n // 4, bank)
                    if kind == "v":
                        v_group(n, 0, bank)
                    if kind == "b":
                        if n == 0:
                            pe.wait_ge(sem(f"{lay}_kst_in0"), STACK)
                            pe.wait_ge(sem(f"{lay}_qst_in"), 2 * STACK)
                        ins = b_group(n, 0, bank).then_inc(*signal(f"{lay}_b_full"))

                def iteration(i, par, c, keys, nxt):
                    user = {bank: (step, c - 1) for bank, step in LOOP_LAST.items()}
                    for step in PLAN:
                        kind, n = step
                        if kind == "k" and not keys or kind in ("v", "b") and not nxt:
                            continue
                        if kind in RING_STEPS:
                            bank = LOOP_SLOTS[step][0]
                            ring_free(pe, lay, *user[bank])
                            user[bank] = (step, c)
                        if kind == "row":
                            pe.wait_ge(sem(f"{lay}_m_done"), c + 1)
                            nc.tensor.transpose(ring[0:H, bank, 0:TOK], nmf[:, par], ident).then_inc(*signal(f"{lay}_row_full"))
                        if kind == "v":
                            v_group(n, 1 - par, bank)
                        if kind == "o":
                            pe.wait_ge(sem(f"{lay}_ot_out"), c + 1)
                            for g in range(4):
                                last = nc.tensor.transpose(ring[:, bank, g * P:(g + 1) * P],
                                                           ots[:, g * P:(g + 1) * P], ident)
                            last.then_inc(*signal(f"{lay}_o_full"))
                        if kind == "s":
                            if n == 0:
                                pe.wait_ge(sem(f"{lay}_row_in"), 16 * (c + 1))
                                pe.wait_ge(sem(f"{lay}_ones_set"), 2)
                            pe.wait_ge(sem(f"{lay}_exp_done"), c * UNITS + n + 1)
                            t, hf = n // 2, n % 2
                            for hh in range(8):
                                h = 8 * hf + hh
                                last = mm(st[:, 2 * (n % 2) + hh // 4, (hh % 4) * TOK:(hh % 4 + 1) * TOK],
                                          kst[0:CP + 1, par, h, t * P:(t + 1) * P], qst[:, par, h])
                            last.then_inc(*signal(f"{lay}_s_full"))
                        if kind == "pv":
                            t, hf = n // 2, n % 2
                            if n == 0:
                                pe.wait_ge(sem(f"{lay}_v_out"), 4 * (c + 1))
                                pe.wait_ge(sem(f"{lay}_ot_out"), c + 1)
                            pe.wait_ge(sem(f"{lay}_exp_done"), c * UNITS + n + 3)
                            for hh in range(8):
                                h = 8 * hf + hh
                                g, j = h // 4, h % 4
                                last = mm(ot[32 * j:32 * j + 32, g * TOK:(g + 1) * TOK], vv[:, par, t, h],
                                          pbuf[:, n % 2, hh * TOK:(hh + 1) * TOK], start=(t == 0 and g == 0),
                                          stop=(t == TPC - 1 and g == 3), skip_group_check=True,
                                          tile_position=(0, 32 * j))
                            last.then_inc(*signal(f"{lay}_pv_done"))
                        if kind == "b":
                            if n == 0:
                                pe.wait_ge(sem(f"{lay}_kst_in{1 - par}"), (i + 1 if par == 1 else i) * STACK + STACK)
                            b_group(n, 1 - par, bank).then_inc(*signal(f"{lay}_b_full"))
                        if kind == "k":
                            if n == 0:
                                pe.wait_ge(sem(f"{lay}_ctx_in{par}"), i * 16 + 32)
                            k_group(n, par, bank)

                with pe.Fori(0, 6) as i:
                    for par in range(2):
                        iteration(i, par, 2 * i + par, True, True)
                iteration(6, 0, 12, False, True)
                iteration(6, 1, 13, False, False)
                pe.wait_ge(sem(f"{lay}_ot_out"), NCH + 1)
                pe.wait_ge(sem(f"{lay}_row_out"), NCH)
                for g in range(4):
                    last = nc.tensor.transpose(ring[:, 0, g * P:(g + 1) * P], ots[:, g * P:(g + 1) * P], ident)
                last.then_inc(*signal(f"{lay}_o_full"))
                transpose2(tmp[0], 6, f"{lay}_att_ready", f"{lay}_aT_full")
                pe.wait_ge(*done_of(f"{lay}_aT_ready"))
                project(pb[7][:, 0:D], lambda k: xT[:, k], lambda k: wx[:, 1, k], f"{lay}_out_full")

            def mamba():
                transpose2(tmp[0], 5, "rms_normed", "rmsT_full")
                pe.wait_ge(sem("w0_in"), 160)
                pe.wait_ge(*done_of("rmsT_ready"))
                for n in range(2 * NB):
                    project(pb[n // 4][:, (n % 4) * P:(n % 4 + 1) * P],
                            lambda k: w0["in_proj"][:, k, n * P:(n + 1) * P], lambda k: xT[:, k],
                            "in_proj_full" if n in (NB - 1, 2 * NB - 1) else None)
                pe.wait_ge(*done_of("xi_ready"))
                project(pb[2][0:RANK + 2 * NS, 0:TOK], lambda k: w0["x_proj"][:, k], lambda k: m2["xi"][:, k],
                        "x_dbl_full", NB)
                pe.wait_ge(*done_of("dr_ready"))
                for n in range(NB):
                    last = mm(pb[3][:, n * P:(n + 1) * P], w0["dt_proj"][0:RANK, n * P:(n + 1) * P],
                              m_["dr"][0:RANK])
                last.then_inc(*signal("dt_full"))
                pe.wait_ge(*done_of("y_ready"))
                project(pb[5][:, 0:D], lambda k: m3["u"][:, k], lambda k: w0["out_proj"][:, k], "mamba_full", NB)

            def ffn():
                transpose2(xn, 5, "F_normed", "FxT_full")
                pe.wait_ge(*done_of("FxT_ready"))
                for n, w in enumerate(("Wq", "Wk")):
                    for m in range(KC):
                        project(pb[n][:, m * P:(m + 1) * P], lambda k: w0[w][:, k, m * P:(m + 1) * P],
                                lambda k: xT[:, k], None if (n, m) != (1, 1) else "Fqk_full")
                project(pb[2][:, 0:D], lambda k: xT[:, k], lambda k: w0["Wv"][:, k], "Fv_full")
                pe.wait_ge(*done_of("Fqk_ready"))
                project(pb[3][:, 0:TOK], lambda k: f_["q"][:, k], lambda k: f_["k"][:, k], "Fs_full")
                pe.wait_ge(*done_of("Fp_ready"))
                nc.tensor.transpose(pb[5][:, 0:TOK], f_["p"], ident).then_inc(*signal("FpT_full"))
                pe.wait_ge(*done_of("FpT_ready"))
                mm(pb[6][:, 0:D], f_["pT"], f_["v"]).then_inc(*signal("Fa_full"))
                transpose2(tmp[0], 7, "Fa_ready", "FaT_full")
                pe.wait_ge(*done_of("FaT_ready"))
                project(pb[0][:, 0:D], lambda k: f_["aT"][:, k], lambda k: w0["Wo"][:, k], "Fo_full")
                transpose2(f_["x1"], 5, "Fx1_ready", "Fx1T_full")
                pe.wait_ge(*done_of("Fx1T_ready"))
                project(pb[4][:, 0:NE], lambda k: xT[:, k], lambda k: w0["Wg"][:, k], "Fg_full")

                def hidden(e):
                    pe.wait_ge(sem(f"expert_in{e}"), 32)
                    if e >= 2:
                        pe.wait_ge(sem("Fh_dve"), e - 1)
                        pe.wait_ge(sem("Fh_act"), e - 1)
                    for n in range(HB):
                        project(pb[2 * (e % 2) + n // 4][:, (n % 4) * P:(n % 4 + 1) * P],
                                lambda k: ew[e]["W1"][:, k, n * P:(n + 1) * P], lambda k: xT[:, k],
                                "Fh_full" if n % 4 == 3 else None)

                def down(e):
                    pe.wait_ge(sem("Fh_dve"), e + 1)
                    pe.wait_ge(sem("Fh_act"), e + 1)
                    if e >= 2:
                        pe.wait_ge(sem("Fy_added"), e - 1)
                    project(pb[5 + e % 2][:, 0:D], lambda k: hT2[e % 2][:, k], lambda k: ew[e]["W2"][:, k],
                            "Fy_full", HB)

                hidden(0)
                hidden(1)
                pe.wait_ge(*done_of("Fg_ready"))
                nc.tensor.transpose(pb[7][0:NE, 0:TOK], f_["g"], ident).then_inc(*signal("FgT_full"))
                pe.wait_ge(*done_of("FgT_ready"))
                mm(pb[4][:, 0:D], f_["gT"][0:NE], w0["b2"][0:NE]).then_inc(*signal("Fb2_full"))
                for e in range(NE):
                    down(e)
                    if e + 2 < NE:
                        hidden(e + 2)

            def linear_attention():
                transpose2(xn, 5, "G_normed", "GxT_full")
                pe.wait_ge(sem("w1_in"), 16 * 8)
                pe.wait_ge(*done_of("GxT_ready"))
                for n, w in enumerate(("Wq", "Wk", "Wv")):
                    project(pb[n][:, 0:D], lambda k: xT[:, k], lambda k: w1[w][:, k], "Gqkv_full")
                pe.wait_ge(*done_of("Gqkv_ready"))
                mm(pb[3][:, 0:D], l_["mean"], l_["qkv"][:, 0]).then_inc(*signal("Gqg_full"))
                for n in range(2):
                    for k in range(KC):
                        last = nc.tensor.transpose(pb[5][:, (2 * n + k) * P:(2 * n + k + 1) * P],
                                                   l_["qkv"][:, n, k * P:(k + 1) * P], ident)
                last.then_inc(*signal("GQT_full"))
                pe.wait_ge(*done_of("GQT_ready"))
                for n, w in enumerate(("Wphi_q", "Wphi_k")):
                    project(pb[n][:, 0:D], lambda k: l_["QT"][:, n, k], lambda k: w1[w][:, k], "Gphi_full")
                pe.wait_ge(*done_of("Gsc_ready"))
                nc.tensor.transpose(pb[6][0:H, 0:TOK], small[:, 0:H], ident).then_inc(*signal("GscT_full"))
                pe.wait_ge(*done_of("GalT_ready"))
                nc.tensor.transpose(pb[7][:, 0:H], l_["scT"][0:H, 1:TOK + 1], ident[0:H, 0:H])
                nc.tensor.transpose(pb[7][0:1, 64:64 + H], l_["scT"][0:H, 0:1], ident[0:H, 0:H]).then_inc(*signal("Gal_full"))
                pe.wait_ge(*done_of("Gphi_ready"))
                for k in range(KC):
                    last = nc.tensor.transpose(pb[2][:, k * P:(k + 1) * P], l_["phi"][:, 0, k * P:(k + 1) * P], ident)
                last.then_inc(*signal("GpQT_full"))
                pe.wait_ge(*done_of("Gpks_ready"))
                mm(pb[4][:, 0:D], l_["ones"], l_["pks"], stop=False)
                mm(pb[4][:, 0:D], l_["ones"][0:1], l_["pk0"][0:1], start=False).then_inc(*signal("Gks_full"))
                for k in range(KC):
                    last = mm(pb[3][:, k * P:(k + 1) * P], l_["pks"][:, k * P:(k + 1) * P],
                              l_["qkv"][:, 2, k * P:(k + 1) * P])
                last.then_inc(*signal("GKV_full"))
                pe.wait_ge(*done_of("GKV_ready"))
                for k in range(KC):
                    last = mm(pb[6][:, k * P:(k + 1) * P], l_["pQT"][:, k], l_["KV"][:, k])
                last.then_inc(*signal("Gnum_full"))
                transpose2(l_["attn"], 5, "Gattn_ready", "GaT_full")
                pe.wait_ge(*done_of("GaT_ready"))
                for k in range(KC):
                    for t in range(CONV):
                        last = mm(pb[7][:, k * P:(k + 1) * P], l_["cw"][:, k * CONV + t], l_["aT"][:, k, t:t + TOK],
                                  start=(t == 0), stop=(t == CONV - 1))
                last.then_inc(*signal("Gconv_full"))
                pe.wait_ge(*done_of("GaT2_ready"))
                for k in range(KC):
                    last = nc.tensor.transpose(pb[6][:, k * P:(k + 1) * P], l_["aT2"][:, k], ident)
                last.then_inc(*signal("Ga2_full"))
                transpose2(l_["a3"], 5, "Ga3_ready", "Ga3T_full")
                pe.wait_ge(*done_of("Ga3T_ready"))
                for n in range(HB):
                    project(pb[n // 4][:, (n % 4) * P:(n % 4 + 1) * P], lambda k: w1["W1"][:, k, n * P:(n + 1) * P],
                            lambda k: xT[:, k], "Gh_full" if n % 4 == 3 else None)
                pe.wait_ge(*done_of("GgT_ready"))
                pe.wait_ge(sem("W2_in"), 16)
                project(pb[7][:, 0:D], lambda k: l_["gT"][:, k], lambda k: mlp_w2[:, k], "Gy_full", HB)

            def sets():
                transpose2(xn, 5, "S_normed", "SxT_full")
                pe.wait_ge(*done_of("SxT_ready"))
                project(pb[6][0:ES, 0:TOK], lambda k: w1["controller"][:, k], lambda k: xT[:, k], "Slog_full")
                pe.wait_ge(*done_of("perm_ready"))
                nc.tensor.transpose(pb[7][:, 0:ES], l_["permT"][0:ES], ident[0:ES, 0:ES]).then_inc(*signal("Sperm_full"))
                pe.wait_ge(*done_of("Spd_ready"))
                for k in range(KC):
                    mm(pb[k][:, :], xn[:, k * P:(k + 1) * P], pdiag.rearrange("p e g -> p (e g)")).then_inc(*signal("Ssel_full"))
                pe.wait_ge(*done_of("Ssel_ready"))
                pe.wait_ge(sem("f1_in"), 16)
                for q in range(PAIRS):
                    for k in range(KC):
                        for par in range(2):
                            e = 2 * q + par
                            last = mm(pb[2 + par][par * EF:(par + 1) * EF, q * NG:(q + 1) * NG],
                                      f1[:, k, e * EF:(e + 1) * EF], selT[:, k, e * NG:(e + 1) * NG],
                                      start=(k == 0), stop=(k == KC - 1), tile_position=(0, par * EF))
                last.then_inc(*signal("Sinn_full"))
                pe.wait_ge(*done_of("Sgx_ready"))
                pe.wait_ge(sem("f2_in"), 16)
                project(pb[6][:, 0:D], lambda k: permx[:, k], lambda k: f2[:, k], "Sy_full", PAIRS)

            pe.wait_ge(sem("const_in"), 48)
            attention("L0")
            if stop >= 2:
                mamba()
            if stop >= 3:
                ffn()
            if stop >= 4:
                attention("L1")
            if stop >= 5:
                linear_attention()
            if stop >= 6:
                sets()

        @block.scalar
        def _(act):
            def root(tag, n=1):
                act.wait_ge(*done_of(f"{tag}_var"))
                nc.scalar.activation(std[:, 0:n], var[:, 0:n], ACT.Sqrt).then_inc(*signal(f"{tag}_std"))

            def copy_T(dst, bank, full, ready, n=D):
                act.wait_ge(*done_of(full))
                nc.scalar.copy(dst.rearrange("p k t -> p (k t)"), pb[bank][:, 0:n]).then_inc(*signal(ready))

            def attention(lay, bk):
                root(f"{lay}_ln")
                copy_T(xT, 5, f"{lay}_xT_full", f"{lay}_xT_ready")

                def key_out(bank, n, count):
                    m, hf = n // 2, n % 2
                    act.wait_ge(sem(f"{lay}_k_full"), count + n + 1)
                    nc.scalar.activation(ktf[:, m * CK + hf * HALF:m * CK + (hf + 1) * HALF], ring[:, bank, 0:HALF],
                                         ACT.Identity, bias=bk[:, m:m + 1]).then_inc(*signal(f"{lay}_k_out"))

                def value_out(bank, n, par, count):
                    tiles = min(2, TPC - 2 * n)
                    act.wait_ge(sem(f"{lay}_v_full"), count + n + 1)
                    nc.scalar.copy(vv[:, par, 2 * n:2 * n + tiles, :, 0:HD],
                                   ring[:, bank, 0:tiles * D].rearrange("p (t h d) -> p t h d", t=tiles, h=H)
                                   ).then_inc(*signal(f"{lay}_v_out"))

                def first_part(c, m):
                    act.wait_ge(sem(f"{lay}_k_out"), 4 * c + 2 * m + 2)
                    nc.scalar.copy(kparts[:, 0, m * CK:(m + 1) * CK], ktf[:, m * CK:(m + 1) * CK]
                                   ).then_inc(*signal(f"{lay}_k1_done"))

                def second_part(c, m):
                    act.wait_ge(sem(f"{lay}_r_done"), KC * c + m + 1)
                    nc.scalar.copy(kparts[:, 1, m * CK:(m + 1) * CK], res[:, m * CK:(m + 1) * CK]
                                   ).then_inc(*signal(f"{lay}_k2_done"))

                for c in range(2):
                    for m in range(KC):
                        if m == 0 and c == 1:
                            act.wait_ge(sem(f"{lay}_r_done"), KC)
                        for n in (2 * m, 2 * m + 1):
                            key_out(PRO_SLOTS[("k", 4 * c + n)][0], n, 4 * c)
                        if m == 0 and c == 1:
                            act.wait_ge(sem(f"{lay}_kst_in0"), STACK)
                        first_part(c, m)
                    for m in range(KC):
                        second_part(c, m)
                for n in range(4):
                    value_out(PRO_SLOTS[("v", n)][0], n, 0, 0)

                def iteration(i, par, c, keys, nxt):
                    for step in PLAN:
                        kind, n = step
                        if kind in ("k", "k1", "k2") and not keys or kind in ("v",) and not nxt:
                            continue
                        if kind == "row":
                            act.wait_ge(sem(f"{lay}_row_full"), c + 1)
                            nc.scalar.copy(rowb[:, :], ring[0:H, LOOP_SLOTS[step][0], 0:TOK]).then_inc(*signal(f"{lay}_row_out"))
                            act.wait_ge(sem(f"{lay}_row_out"), c + 1)
                            act.dma_start(qst[CP:CP + 1, par], rowb[:, :]).then_inc(sem(f"{lay}_row_in"), 16)
                            nc.scalar.activation(alpha[:, par], mdiff[:, :], ACT.Exp).then_inc(*signal(f"{lay}_alpha_done"))
                        if kind == "v":
                            if n == 0:
                                act.wait_ge(sem(f"{lay}_pv_done"), c * UNITS + 2)
                            value_out(LOOP_SLOTS[step][0], n, 1 - par, 4 * (c + 1))
                        if kind == "e":
                            act.wait_ge(sem(f"{lay}_s_full"), c * UNITS + n + 1)
                            act.wait_ge(sem(f"{lay}_pv_done"), c * UNITS + n + 1)
                            nc.scalar.activation(pbuf[:, n % 2],
                                                 st[:, 2 * (n % 2):2 * (n % 2) + 2].rearrange("p b k -> p (b k)"),
                                                 ACT.Exp).then_inc(*signal(f"{lay}_exp_done"))
                        if kind == "k":
                            if n == 0:
                                act.wait_ge(sem(f"{lay}_r_done"), KC * (c + 2))
                            key_out(LOOP_SLOTS[step][0], n, 4 * (c + 2))
                        if kind == "k1":
                            if n == 0:
                                act.wait_ge(sem(f"{lay}_kst_in{1 - par}"),
                                            (i + (2 if par == 1 else 1)) * STACK)
                            first_part(c + 2, n)
                        if kind == "k2":
                            second_part(c + 2, n)
                        if kind == "ot":
                            act.wait_ge(sem(f"{lay}_pv_done"), (c + 1) * UNITS + 2)
                            act.wait_ge(sem(f"{lay}_o_full"), c + 1)
                            nc.scalar.copy(ots[:, :], ot[:, :]).then_inc(*signal(f"{lay}_ot_out"))

                with act.Fori(0, 6) as i:
                    for par in range(2):
                        iteration(i, par, 2 * i + par, True, True)
                iteration(6, 0, 12, False, True)
                iteration(6, 1, 13, False, False)
                copy_T(xT, 6, f"{lay}_aT_full", f"{lay}_aT_ready")

            def mamba():
                root("M")
                act.wait_ge(*done_of("M2_var"))
                nc.scalar.activation(std[:, 0:1], var[:, 0:1], ACT.Sqrt).then_inc(*signal("M2_std"))
                nc.scalar.activation(m_["A"], col("A_log"), ACT.Exp).then_inc(*signal("A_exp"))
                act.wait_ge(sem("in_proj_full"), 2)
                nc.scalar.activation(m2["sres"].rearrange("p b t -> p (b t)"), pb[1][:, :], ACT.Exp,
                                     scale=-1.0).then_inc(*signal("res_exp"))
                act.wait_ge(*done_of("conv_ready"))
                nc.scalar.activation(m3["e"], m3["z"], ACT.Exp, scale=-1.0).then_inc(*signal("xc_exp"))
                act.wait_ge(*done_of("negabs_ready"))
                nc.scalar.activation(m3["e"], m3["l"], ACT.Exp).then_inc(*signal("sp_exp"))
                act.wait_ge(*done_of("sp_u"))
                nc.scalar.activation(m3["l"], m3["u"], ACT.Ln).then_inc(*signal("sp_ln"))
                act.wait_ge(*done_of("delta_ready"))
                act.wait_ge(*done_of("A_ready"))
                for b in range(NB):
                    if b >= 2:
                        act.wait_ge(sem("scanned"), b - 1)
                    for n in range(NS):
                        ins = nc.scalar.activation(m_["dA"][:, b % 2, n * TOK + 1:(n + 1) * TOK], m3["z"][:, b, 1:],
                                                   ACT.Exp, scale=m_["A"][:, b * NS + n:b * NS + n + 1])
                    ins.then_inc(*signal("dA_ready"))

            def ffn():
                root("F")
                copy_T(xT, 5, "FxT_full", "FxT_ready")
                act.wait_ge(*done_of("Fmax_ready"))
                nc.scalar.activation(f_["p"], pb[3][:, 0:TOK], ACT.Exp, bias=small[:, 0:1], scale=1.0 / 16,
                                     accum_out=small[:, 1:2]).then_inc(*signal("Fexp_done"))
                act.wait_ge(*done_of("FpT_full"))
                nc.scalar.copy(f_["pT"], pb[5][:, 0:TOK]).then_inc(*signal("FpT_ready"))
                act.wait_ge(*done_of("Fa_full"))
                nc.scalar.copy(tmp[0][:, :], pb[6][:, 0:D]).then_inc(*signal("Fa_ready"))
                copy_T(f_["aT"], 7, "FaT_full", "FaT_ready")
                copy_T(xT, 5, "Fx1T_full", "Fx1T_ready")
                act.wait_ge(*done_of("Fgmax_ready"))
                nc.scalar.activation(small[:, 16:24], small[:, 8:16], ACT.Exp, bias=small[:, 2:3],
                                     accum_out=small[:, 3:4]).then_inc(*signal("Fgexp_done"))
                act.wait_ge(*done_of("FgT_full"))
                nc.scalar.copy(f_["gT"][0:NE], pb[7][0:NE, 0:TOK]).then_inc(*signal("FgT_ready"))
                for e in range(NE):
                    act.wait_ge(sem("Fh_full"), 2 * e + 2)
                    if e >= 2:
                        act.wait_ge(sem("Fy_full"), e - 1)
                    for n in range(4, 8):
                        ins = nc.scalar.activation(hT2[e % 2][:, n], pb[2 * (e % 2) + 1][:, (n - 4) * P:(n - 3) * P],
                                                   ACT.Relu, bias=col("ffn_b1")[:, e * HB + n:e * HB + n + 1])
                    ins.then_inc(*signal("Fh_act"))

            def linear_attention():
                root("G")
                copy_T(xT, 5, "GxT_full", "GxT_ready")
                root("GQ", 3)
                act.wait_ge(*done_of("GQT_full"))
                nc.scalar.copy(l_["QT"].rearrange("p n k t -> p (n k t)"), pb[5][:, :]).then_inc(*signal("GQT_ready"))
                act.wait_ge(*done_of("GscT_ready"))
                nc.scalar.activation(l_["scT"][0:H], l_["scT"][0:H], ACT.Exp, bias=small[0:H, 32:33],
                                     accum_out=small[0:H, 33:34]).then_inc(*signal("Gexp_done"))
                act.wait_ge(*done_of("Gphi_biased"))
                nc.scalar.activation(l_["phi"], l_["phi"], ACT.Tanh).then_inc(*signal("Gtanh_done"))
                nc.scalar.activation(l_["pk0"][0:1], row1("bphi_k")[0:1], ACT.Tanh).then_inc(*signal("Gtanh_done"))
                act.wait_ge(*done_of("GpQT_full"))
                nc.scalar.copy(l_["pQT"].rearrange("p k t -> p (k t)"), pb[2][:, 0:D]).then_inc(*signal("GpQT_ready"))
                act.wait_ge(*done_of("GaT_full"))
                nc.scalar.copy(l_["aT"][:, :, 2:2 + TOK], pb[5][:, 0:D].rearrange("p (k t) -> p k t", k=KC)
                               ).then_inc(*signal("GaT_ready"))
                root("GA")
                copy_T(xT, 5, "Ga3T_full", "Ga3T_ready")
                for n in range(HB):
                    if n % 4 == 0:
                        act.wait_ge(sem("Gh_full"), n // 4 + 1)
                    ins = nc.scalar.activation(l_["gT"][:, n], pb[n // 4][:, (n % 4) * P:(n % 4 + 1) * P], ACT.Gelu,
                                               bias=col("mlp_b1")[:, n:n + 1])
                ins.then_inc(*signal("GgT_ready"))

            def sets():
                root("S")
                copy_T(xT, 5, "SxT_full", "SxT_ready")
                act.wait_ge(sem("Ssel_full"), 2)
                for k in range(KC):
                    ins = nc.scalar.copy(selT[:, k], pb[k][:, :])
                ins.then_inc(*signal("Ssel_ready"))

            act.wait_ge(sem("const_in"), 48)
            attention("L0", col("L0_xattn_bk"))
            if stop >= 2:
                mamba()
            if stop >= 3:
                ffn()
            if stop >= 4:
                attention("L1", col("L1_xattn_k_b"))
            if stop >= 5:
                linear_attention()
            if stop >= 6:
                sets()

        @block.vector
        def _(dve):
            steps = [0]

            def link(ins):
                steps[0] += 1
                ins.then_inc(*signal("dve_step"))
                dve.wait_ge(sem("dve_step"), steps[0])

            V = nc.vector

            def norm(tag, src, dst):
                link(V.bn_stats(stats[:, 0], src))
                link(V.bn_aggr(mv[:, 0], stats[:, 0]))
                V.tensor_scalar(var[:, 0:1], mv[:, 0, 1:2], EPS, None, ALU.add).then_inc(*signal(f"{tag}_var"))
                dve.wait_ge(*done_of(f"{tag}_std"))
                link(V.reciprocal(rstd[:, 0:1], std[:, 0:1]))
                V.tensor_scalar(dst, src, mv[:, 0, 0:1], rstd[:, 0:1], ALU.subtract, ALU.mult).then_inc(*signal(f"{tag}_normed"))
                dve.wait_ge(*done_of(f"{tag}_normed"))

            def attention(lay, bq, bv, bo):
                norm(f"{lay}_ln", xr[:, :], xn[:, :])
                q = tmp[1].rearrange("p (k t) -> p k t", k=KC)
                r = tmp[0].rearrange("p (k t) -> p k t", k=KC)
                dve.wait_ge(sem(f"{lay}_q_full"), KC)
                for m in range(KC):
                    ins = V.tensor_scalar(q[:, m], pb[6][:, m * P:(m + 1) * P], bq[:, m:m + 1], HD ** -0.5,
                                          ALU.add, ALU.mult)
                link(ins)
                link(V.tensor_copy(qparts[:, 0], q))
                link(V.tensor_tensor(r, q, qparts[:, 0], ALU.subtract))
                link(V.tensor_copy(qparts[:, 1], r))
                V.tensor_tensor(qparts[:, 2], r, qparts[:, 1], ALU.subtract).then_inc(*signal(f"{lay}_q_split"))
                V.memset(nmb[:, 1], 1e30)
                V.memset(alpha[:, 1], 0.0).then_inc(sem(f"{lay}_exp_done"), 2)
                V.memset(oacc[:, :, :], 0.0).then_inc(*signal(f"{lay}_o_added"))
                V.memset(ots[:, :], 0.0).then_inc(*signal(f"{lay}_ots_zero"))
                dve.wait_ge(*done_of(f"{lay}_ots_zero"))
                V.memset(mneg[:, :], 0.0).then_inc(*signal(f"{lay}_ot_out"))
                V.memset(small[:, 0:1], 0.0).then_inc(sem(f"{lay}_pv_done"), 2)

                def row_max(n, bank, count):
                    dve.wait_ge(sem(f"{lay}_b_full"), count + n + 1)
                    V.reduce_max(mpart[:, n:n + 1], ring[:, bank, 0:HALF], AX_X).then_inc(*signal(f"{lay}_b_max"))

                def maxima(c, par):
                    dve.wait_ge(sem(f"{lay}_b_max"), (c + 1) * 2 * H)
                    V.tensor_reduce(mneg[:, :], mpart[:, :].rearrange("p (h f) -> p h f", f=2), AX_X, ALU.max,
                                    negate=True).then_inc(*signal(f"{lay}_mneg"))
                    dve.wait_ge(sem(f"{lay}_mneg"), c + 1)
                    V.tensor_tensor(nmb[:, par], mneg[:, :], nmb[:, 1 - par], ALU.min).then_inc(*signal(f"{lay}_nmb"))
                    dve.wait_ge(sem(f"{lay}_nmb"), c + 1)
                    if not (isinstance(c, int) and c == 0):
                        dve.wait_ge(sem(f"{lay}_alpha_done"), c)
                    V.tensor_tensor(mdiff[:, :], nmb[:, par], nmb[:, 1 - par], ALU.subtract)
                    V.tensor_copy(nmf[:, par], nmb[:, par]).then_inc(*signal(f"{lay}_m_done"))

                for n in range(2 * H):
                    row_max(n, PRO_SLOTS[("b", n)][0], 0)
                maxima(0, 0)

                def add_chunk(bank, c, par):
                    dve.wait_ge(sem(f"{lay}_o_full"), c + 1)
                    V.tensor_tensor(oacc[:, :, :], oacc[:, :, :],
                                    alpha[:, 1 - par].rearrange("p (h o) -> p h o", o=1).broadcast_to([P, H, VW]),
                                    ALU.mult).then_inc(*signal(f"{lay}_o_scaled"))
                    dve.wait_ge(sem(f"{lay}_o_scaled"), c + 1)
                    V.tensor_tensor(oacc[:, :, :], ring[:, bank].rearrange("p (h d) -> p h d", h=H), oacc[:, :, :],
                                    ALU.add).then_inc(*signal(f"{lay}_o_added"))

                def iteration(i, par, c, keys, nxt):
                    for step in PLAN:
                        kind, n = step
                        if kind in ("b", "m") and not nxt:
                            continue
                        if kind == "o":
                            dve.wait_ge(sem(f"{lay}_o_added"), c + 1)
                            add_chunk(LOOP_SLOTS[step][0], c, par)
                        if kind == "b":
                            row_max(n, LOOP_SLOTS[step][0], 2 * H * (c + 1))
                        if kind == "m":
                            maxima(c + 1, 1 - par)

                with dve.Fori(0, 6) as i:
                    for par in range(2):
                        iteration(i, par, 2 * i + par, True, True)
                iteration(6, 0, 12, False, True)
                iteration(6, 1, 13, False, False)
                dve.wait_ge(sem(f"{lay}_o_added"), NCH + 1)
                add_chunk(0, NCH, 0)
                dve.wait_ge(sem(f"{lay}_o_added"), NCH + 2)
                link(V.reciprocal(small[:, 0:H], oacc[:, :, HD]))
                t3 = tmp[0].rearrange("p (h d) -> p h d", h=H)
                link(V.tensor_tensor(t3, oacc[:, :, 0:HD],
                                     small[:, 0:H].rearrange("p (h o) -> p h o", o=1).broadcast_to([P, H, HD]),
                                     ALU.mult))
                V.tensor_tensor(tmp[0][:, :], tmp[0][:, :], bv, ALU.add).then_inc(*signal(f"{lay}_att_ready"))
                link(V.tensor_tensor(xr[:, :], xr[:, :], bo, ALU.add))
                dve.wait_ge(*done_of(f"{lay}_out_full"))
                V.tensor_tensor(xr[:, :], pb[7][:, 0:D], xr[:, :], ALU.add).then_inc(*signal(f"{lay}_attended"))
                dve.wait_ge(*done_of(f"{lay}_attended"))

            def sigmoid_of_exp(t):
                link(V.tensor_scalar(t, t, 1.0, None, ALU.add))
                link(V.reciprocal(t, t))

            def mamba():
                V.memset(m2["xpad"][:, :, 0:TAPS - 1], 0.0)
                for b in range(2):
                    V.memset(m_["dA"][:, b].rearrange("p (n t) -> p n t", n=NS)[:, :, 0:1], 0.0)
                norm("M", xr[:, :], xn[:, :])
                link(V.tensor_tensor_reduce(tmp[1][:, :], xn[:, :], xn[:, :], 1.0, 0.0, ALU.mult, ALU.add,
                                            small[:, 0:1]))
                V.tensor_scalar(var[:, 0:1], small[:, 0:1], 1.0 / D, EPS, ALU.mult, ALU.add).then_inc(*signal("M2_var"))
                dve.wait_ge(*done_of("M2_std"))
                link(V.reciprocal(rstd[:, 0:1], std[:, 0:1]))
                V.tensor_scalar(tmp[0][:, :], xn[:, :], rstd[:, 0:1], None, ALU.mult).then_inc(*signal("rms_normed"))
                dve.wait_ge(*done_of("rmsT_full"))
                for k in range(KC):
                    ins = V.tensor_scalar(xT[:, k], pb[5][:, k * P:(k + 1) * P], col("norm_w")[:, k:k + 1], None,
                                          ALU.mult)
                ins.then_inc(*signal("rmsT_ready"))
                dve.wait_ge(*done_of("A_exp"))
                V.tensor_scalar(m_["A"], m_["A"], -1.0, None, ALU.mult).then_inc(*signal("A_ready"))
                dve.wait_ge(*done_of("in_proj_full"))
                link(V.tensor_copy(m2["xpad"][:, :, TAPS - 1:], pb[0].rearrange("p (b t) -> p b t", b=NB)))
                for t in range(TAPS):
                    for b in range(NB):
                        w = col("conv_w")[:, b * TAPS + t:b * TAPS + t + 1]
                        if t == 0:
                            ins = V.tensor_scalar(m3["z"][:, b], m2["xpad"][:, b, 0:TOK], w,
                                                  col("conv_b")[:, b:b + 1], ALU.mult, ALU.add)
                        else:
                            ins = V.scalar_tensor_tensor(out=m3["z"][:, b], in0=m2["xpad"][:, b, t:t + TOK],
                                                         scalar=w, in1=m3["z"][:, b], op0=ALU.mult, op1=ALU.add)
                    if t < TAPS - 1:
                        link(ins)
                ins.then_inc(*signal("conv_ready"))
                dve.wait_ge(*done_of("res_exp"))
                sigmoid_of_exp(m2["sres"])
                link(V.tensor_tensor(m2["sres"].rearrange("p b t -> p (b t)"), pb[1][:, :],
                                     m2["sres"].rearrange("p b t -> p (b t)"), ALU.mult))
                dve.wait_ge(*done_of("xc_exp"))
                sigmoid_of_exp(m3["e"])
                V.tensor_tensor(m2["xi"], m3["z"], m3["e"], ALU.mult).then_inc(*signal("xi_ready"))
                dve.wait_ge(*done_of("xi_ready"))
                dve.wait_ge(*done_of("x_dbl_full"))
                V.tensor_copy(m_["dr"][0:RANK], pb[2][0:RANK, 0:TOK]).then_inc(*signal("dr_ready"))
                V.tensor_copy(m_["bcT"][RANK:RANK + 2 * NS], pb[2][RANK:RANK + 2 * NS, 0:TOK]).then_inc(*signal("bcT_ready"))
                dve.wait_ge(*done_of("dt_full"))
                for b in range(NB):
                    ins = V.tensor_scalar(m3["z"][:, b], pb[3][:, b * P:(b + 1) * P], col("dt_b")[:, b:b + 1], None,
                                          ALU.add)
                link(ins)
                V.scalar_tensor_tensor(out=m3["l"], in0=m3["z"], scalar=-1.0, in1=m3["z"], op0=ALU.mult,
                                       op1=ALU.min).then_inc(*signal("negabs_ready"))
                dve.wait_ge(*done_of("sp_exp"))
                V.tensor_scalar(m3["u"], m3["e"], 1.0, None, ALU.add).then_inc(*signal("sp_u"))
                dve.wait_ge(*done_of("sp_u"))
                dve.wait_ge(*done_of("sp_ln"))
                link(V.tensor_scalar(m3["u"], m3["u"], 1.0, None, ALU.subtract))
                link(V.tensor_scalar(m3["dtu"], m3["u"], 0.0, None, ALU.is_equal))
                link(V.tensor_tensor(m3["u"], m3["u"], m3["dtu"], ALU.add))
                link(V.reciprocal(m3["u"], m3["u"]))
                link(V.tensor_tensor(m3["l"], m3["l"], m3["dtu"], ALU.add))
                link(V.tensor_tensor(m3["l"], m3["l"], m3["u"], ALU.mult))
                link(V.tensor_tensor(m3["l"], m3["l"], m3["e"], ALU.mult))
                V.scalar_tensor_tensor(out=m3["z"], in0=m3["z"], scalar=0.0, in1=m3["l"], op0=ALU.max,
                                       op1=ALU.add).then_inc(*signal("delta_ready"))
                dve.wait_ge(*done_of("delta_ready"))
                V.tensor_tensor(m3["dtu"], m3["z"], m2["xi"], ALU.mult).then_inc(*signal("dtu_ready"))
                for b in range(NB):
                    dve.wait_ge(sem("dA_ready"), b + 1)
                    dve.wait_ge(sem("dBu_ready"), b + 1)
                    V.tensor_tensor_scan(m_["h"], m_["dA"][:, b % 2], m_["dBu"][:, b % 2], 0.0, ALU.mult,
                                         ALU.add).then_inc(*signal("scanned"))
                    dve.wait_ge(sem("scanned"), b + 1)
                    link(V.tensor_tensor(m_["h"], m_["h"], m_["bc"][:, NS * TOK:], ALU.mult))
                    link(V.reduce_sum(m3["u"][:, b], m_["h"].rearrange("p (n t) -> p t n", n=NS), AX_X))
                    link(V.scalar_tensor_tensor(out=m3["u"][:, b], in0=m2["xi"][:, b], scalar=col("D")[:, b:b + 1],
                                                in1=m3["u"][:, b], op0=ALU.mult, op1=ALU.add))
                V.tensor_tensor(m3["u"], m3["u"], m2["sres"], ALU.mult).then_inc(*signal("y_ready"))
                link(V.tensor_tensor(xr[:, :], xr[:, :], xn[:, :], ALU.add))
                dve.wait_ge(*done_of("mamba_full"))
                V.tensor_tensor(xr[:, :], pb[5][:, 0:D], xr[:, :], ALU.add).then_inc(*signal("mamba_done"))
                dve.wait_ge(*done_of("mamba_done"))

            def ffn():
                norm("F", xr[:, :], xn[:, :])
                dve.wait_ge(*done_of("Fqk_full"))
                for n, (dst, b) in enumerate(((f_["q"], col("ffn_bq")), (f_["k"], col("ffn_bk")))):
                    for m in range(KC):
                        ins = V.tensor_scalar(dst[:, m], pb[n][:, m * P:(m + 1) * P], b[:, m:m + 1], None, ALU.add)
                ins.then_inc(*signal("Fqk_ready"))
                dve.wait_ge(*done_of("Fv_full"))
                V.tensor_tensor(f_["v"], pb[2][:, 0:D], row("ffn_bv"), ALU.add)
                dve.wait_ge(*done_of("Fs_full"))
                link(V.reduce_max(small[:, 4:5], pb[3][:, 0:TOK], AX_X))
                V.tensor_scalar(small[:, 0:1], small[:, 4:5], -1.0 / 16, None, ALU.mult).then_inc(*signal("Fmax_ready"))
                dve.wait_ge(*done_of("Fexp_done"))
                link(V.reciprocal(small[:, 5:6], small[:, 1:2]))
                V.tensor_scalar(f_["p"], f_["p"], small[:, 5:6], None, ALU.mult).then_inc(*signal("Fp_ready"))
                link(V.tensor_tensor(f_["x1"], xn[:, :], row("ffn_bo"), ALU.add))
                dve.wait_ge(*done_of("Fo_full"))
                V.tensor_tensor(f_["x1"], pb[0][:, 0:D], f_["x1"], ALU.add).then_inc(*signal("Fx1_ready"))
                dve.wait_ge(*done_of("Fx1_ready"))
                dve.wait_ge(*done_of("Fg_full"))
                link(V.tensor_tensor(small[:, 8:16], pb[4][:, 0:NE], row("ffn_bg"), ALU.add))
                V.tensor_reduce(small[:, 2:3], small[:, 8:16], AX_X, ALU.max, negate=True).then_inc(*signal("Fgmax_ready"))
                link(V.tensor_tensor(xr[:, :], xr[:, :], f_["x1"], ALU.add))
                dve.wait_ge(*done_of("Fgexp_done"))
                link(V.reciprocal(small[:, 6:7], small[:, 3:4]))
                V.tensor_scalar(f_["g"], small[:, 16:24], small[:, 6:7], None, ALU.mult).then_inc(*signal("Fg_ready"))
                dve.wait_ge(*done_of("Fg_ready"))

                def hidden(e):
                    dve.wait_ge(sem("Fh_full"), 2 * e + 1)
                    if e >= 2:
                        dve.wait_ge(sem("Fy_full"), e - 1)
                    for n in range(4):
                        ins = V.tensor_scalar(hT2[e % 2][:, n], pb[2 * (e % 2)][:, n * P:(n + 1) * P],
                                              col("ffn_b1")[:, e * HB + n:e * HB + n + 1], 0.0, ALU.add, ALU.max)
                    ins.then_inc(*signal("Fh_dve"))

                def add(e):
                    dve.wait_ge(sem("Fy_full"), e + 1)
                    V.scalar_tensor_tensor(out=xr[:, :], in0=pb[5 + e % 2][:, 0:D], scalar=f_["g"][:, e:e + 1],
                                           in1=xr[:, :], op0=ALU.mult, op1=ALU.add).then_inc(*signal("Fy_added"))
                    dve.wait_ge(sem("Fy_added"), e + 1)

                hidden(0)
                dve.wait_ge(*done_of("Fb2_full"))
                link(V.tensor_tensor(xr[:, :], pb[4][:, 0:D], xr[:, :], ALU.add))
                for e in range(NE):
                    if e + 1 < NE:
                        hidden(e + 1)
                    add(e)
                V.memset(small[:, 7:8], 0.0).then_inc(*signal("ffn_done"))
                dve.wait_ge(*done_of("ffn_done"))

            def linear_attention():
                V.memset(l_["mean"], HD ** -0.5 / TOK)
                V.memset(l_["aT"][:, :, 0:2], 0.0)
                V.memset(l_["aT"][:, :, 2 + TOK:], 0.0)
                link(V.memset(l_["ones"], 1.0))
                norm("G", xr[:, :], xn[:, :])
                dve.wait_ge(sem("Gqkv_full"), 3)
                dve.wait_ge(sem("rows1_in"), 16)
                for n, b in enumerate(("bq", "bk", "bv")):
                    ins = V.tensor_tensor(l_["qkv"][:, n], pb[n][:, 0:D], row1(b), ALU.add)
                link(ins)
                for n in range(3):
                    ins = V.bn_stats(stats[:, n], l_["qkv"][:, n])
                link(ins)
                for n in range(3):
                    ins = V.bn_aggr(mv[:, n], stats[:, n])
                link(ins)
                V.tensor_scalar(var[:, :], mv[:, :, 1], EPS, None, ALU.add).then_inc(*signal("GQ_var"))
                dve.wait_ge(*done_of("GQ_std"))
                link(V.reciprocal(rstd[:, :], std[:, :]))
                for n in range(3):
                    ins = V.tensor_scalar(l_["qkv"][:, n], l_["qkv"][:, n], mv[:, n, 0:1], rstd[:, n:n + 1],
                                          ALU.subtract, ALU.mult)
                link(ins)
                g0, b0 = ROWS1["lnq_g"][0], ROWS1["lnq_b"][0]
                q3 = l_["qkv"].rearrange("p n d -> p (n d)")
                link(V.tensor_tensor(q3, q3, rows1[:, g0:g0 + 3 * D], ALU.mult))
                V.tensor_tensor(q3, q3, rows1[:, b0:b0 + 3 * D], ALU.add).then_inc(*signal("Gqkv_ready"))
                dve.wait_ge(*done_of("Gqkv_ready"))
                dve.wait_ge(*done_of("Gqg_full"))
                link(V.tensor_tensor(l_["prod"], pb[3][:, 0:D], l_["qkv"][:, 1], ALU.mult))
                V.reduce_sum(small[:, 0:H], l_["prod"].rearrange("p (h d) -> p h d", h=H), AX_X).then_inc(*signal("Gsc_ready"))
                V.memset(l_["scT"][0:H, 0:1], 0.0)
                dve.wait_ge(*done_of("GscT_full"))
                link(V.tensor_copy(l_["scT"][0:H, 1:TOK + 1], pb[6][0:H, 0:TOK]))
                V.tensor_reduce(small[0:H, 32:33], l_["scT"][0:H], AX_X, ALU.max, negate=True).then_inc(*signal("GscT_ready"))
                dve.wait_ge(sem("Gphi_full"), 2)
                for n, b in enumerate(("bphi_q", "bphi_k")):
                    ins = V.tensor_tensor(l_["phi"][:, n], pb[n][:, 0:D], row1(b), ALU.add)
                ins.then_inc(*signal("Gphi_biased"))
                dve.wait_ge(*done_of("Gexp_done"))
                link(V.reciprocal(small[0:H, 34:35], small[0:H, 33:34]))
                V.tensor_scalar(l_["scT"][0:H], l_["scT"][0:H], small[0:H, 34:35], float(TOK), ALU.mult,
                                ALU.mult).then_inc(*signal("GalT_ready"))
                dve.wait_ge(sem("Gtanh_done"), 2)
                link(V.tensor_scalar(l_["pk0"][0:1], l_["pk0"][0:1], 1.0, None, ALU.add))
                V.tensor_scalar(l_["phi"], l_["phi"], 1.0, None, ALU.add).then_inc(*signal("Gphi_ready"))
                dve.wait_ge(*done_of("Gphi_ready"))
                dve.wait_ge(*done_of("Gal_full"))
                link(V.tensor_copy(l_["alpha"], pb[7][:, 0:H]))
                link(V.tensor_copy(small[0:1, 40:40 + H], pb[7][0:1, 64:64 + H]))
                v3 = lambda t: t.rearrange("p (h d) -> p h d", h=H)
                link(V.tensor_tensor(v3(l_["pk0"])[0:1], v3(l_["pk0"])[0:1],
                                     small[0:1, 40:40 + H].rearrange("p (h o) -> p h o", o=1)
                                     .broadcast_to([1, H, HD]), ALU.mult))
                V.tensor_tensor(v3(l_["pks"]), v3(l_["phi"][:, 1]),
                                l_["alpha"].rearrange("p (h o) -> p h o", o=1).broadcast_to([P, H, HD]),
                                ALU.mult).then_inc(*signal("Gpks_ready"))
                dve.wait_ge(*done_of("Gks_full"))
                link(V.tensor_copy(l_["ksum"], pb[4][:, 0:D]))
                dve.wait_ge(*done_of("GpQT_ready"))
                dve.wait_ge(*done_of("GKV_full"))
                V.tensor_tensor(l_["KV"], pb[3][:, 0:D].rearrange("p (k d) -> p k d", k=KC),
                                blockmask.rearrange("p (o d) -> p o d", o=1).broadcast_to([P, KC, P]),
                                ALU.mult).then_inc(*signal("GKV_ready"))
                link(V.tensor_tensor(l_["prod"], l_["phi"][:, 0], l_["ksum"], ALU.mult))
                link(V.reduce_sum(l_["den"], v3(l_["prod"]), AX_X))
                link(V.tensor_scalar(l_["den"], l_["den"], 1e-6, None, ALU.add))
                link(V.reciprocal(l_["den"], l_["den"]))
                for k in range(KC):
                    for t in range(CONV):
                        ins = V.tensor_tensor(l_["cw"][:, k * CONV + t].rearrange("p (g o) -> p g o", o=HD),
                                              w1["conv_w"][:, k, t:t + 1].broadcast_to([P, P // HD, HD]),
                                              blockmask.rearrange("p (g o) -> p g o", o=HD), ALU.mult)
                dve.wait_ge(*done_of("Gnum_full"))
                V.tensor_tensor(v3(l_["attn"]), v3(pb[6][:, 0:D]),
                                l_["den"].rearrange("p (h o) -> p h o", o=1).broadcast_to([P, H, HD]),
                                ALU.mult).then_inc(*signal("Gattn_ready"))
                dve.wait_ge(*done_of("GaT_ready"))
                dve.wait_ge(*done_of("Gconv_full"))
                for k in range(KC):
                    ins = V.tensor_scalar(l_["aT2"][:, k], pb[7][:, k * P:(k + 1) * P], col("lconv_b")[:, k:k + 1],
                                          row("gamma"), ALU.add, ALU.mult)
                link(ins)
                V.tensor_tensor(l_["aT2"], l_["aT2"], l_["aT"][:, :, 2:2 + TOK], ALU.add).then_inc(*signal("GaT2_ready"))
                dve.wait_ge(*done_of("Ga2_full"))
                link(V.tensor_copy(l_["attn"], pb[6][:, 0:D]))
                norm("GA", l_["attn"], l_["a3"])
                link(V.tensor_tensor(l_["a3"], l_["a3"], row1("lna_g"), ALU.mult))
                V.tensor_tensor(l_["a3"], l_["a3"], row1("lna_b"), ALU.add).then_inc(*signal("Ga3_ready"))
                dve.wait_ge(*done_of("Ga3_ready"))
                link(V.tensor_tensor(xr[:, :], xr[:, :], xn[:, :], ALU.add))
                link(V.tensor_tensor(xr[:, :], xr[:, :], l_["a3"], ALU.add))
                link(V.tensor_tensor(xr[:, :], xr[:, :], row1("b2"), ALU.add))
                dve.wait_ge(*done_of("Gy_full"))
                link(V.tensor_tensor(xr[:, :], pb[7][:, 0:D], xr[:, :], ALU.add))

            def sets():
                norm("S", xr[:, :], xn[:, :])
                dve.wait_ge(*done_of("Slog_full"))
                lg = tmp[0][0:ES, 0:TOK]
                g3 = lambda t: t.rearrange("p (g t) -> p g t", t=GR)
                link(V.tensor_tensor(lg, pb[6][0:ES, 0:TOK], row("tie")[0:ES], ALU.add))
                link(V.reduce_max(l_["gmax"][0:ES], g3(lg), AX_X))
                V.tensor_tensor(g3(l_["permT"][0:ES]), g3(lg),
                                l_["gmax"][0:ES].rearrange("p (g o) -> p g o", o=1).broadcast_to([ES, NG, GR]),
                                ALU.is_equal).then_inc(*signal("perm_ready"))
                dve.wait_ge(*done_of("Sperm_full"))
                link(V.tensor_copy(l_["perm"], pb[7][:, 0:ES]))
                V.tensor_tensor(pdiag, l_["perm"].rearrange("p (e o) -> p e o", o=1).broadcast_to([P, ES, NG]),
                                groupmask.rearrange("p (o g) -> p o g", o=1).broadcast_to([P, ES, NG]),
                                ALU.mult).then_inc(*signal("Spd_ready"))
                dve.wait_ge(*done_of("Sinn_full"))
                for par in range(2):
                    sl = slice(par * EF, (par + 1) * EF)
                    ins = V.tensor_tensor(innT[sl], pb[2 + par][sl, 0:PAIRS * NG].rearrange("p (q g) -> p q g", g=NG),
                                          col("bias")[sl].rearrange("p (q o) -> p q o", o=1)
                                          .broadcast_to([EF, PAIRS, NG]), ALU.add)
                link(ins)
                link(V.tensor_scalar(innT, innT, 0.0, None, ALU.max))
                dve.wait_ge(sem("permx_in"), 32)
                V.tensor_tensor(permx.rearrange("p q (g t) -> p (q g) t", t=GR),
                                permx.rearrange("p q (g t) -> p (q g) t", t=GR),
                                innT.rearrange("p q (g o) -> p (q g) o", o=1).broadcast_to([P, PAIRS * NG, GR]),
                                ALU.mult).then_inc(*signal("Sgx_ready"))
                dve.wait_ge(*done_of("Sy_full"))
                link(V.tensor_tensor(xr[:, :], pb[6][:, 0:D], xr[:, :], ALU.add))

            dve.wait_ge(sem("x_in"), 16)
            dve.wait_ge(sem("const_in"), 48)
            attention("L0", col("L0_xattn_bq"), row("L0_xattn_bv"), row("L0_xattn_bo"))
            if stop >= 2:
                mamba()
            if stop >= 3:
                ffn()
            if stop >= 4:
                attention("L1", col("L1_xattn_q_b"), row("L1_xattn_v_b"), row("L1_xattn_proj_b"))
            if stop >= 5:
                linear_attention()
            if stop >= 6:
                sets()
            V.memset(small[:, 63:64], 0.0).then_inc(*signal("result_ready"))


_ARRAYS = []


def _lay_out(t):
    import numpy as np
    f = {k: np.asarray(v) for k, v in t.items()}

    def per_partition(v):
        return v.reshape(-1, P).T

    def head_last(v):
        return v.reshape(v.shape[:-1] + (KC, H // KC, HD)).swapaxes(-1, -2).reshape(v.shape)

    kv_w, kv_b = f["L1_xattn_kv_w"], f["L1_xattn_kv_b"]
    cols = {
        "L0_xattn_bq": per_partition(head_last(f["L0_xattn_bq"])),
        "L0_xattn_bk": per_partition(head_last(f["L0_xattn_bk"])),
        "L1_xattn_q_b": per_partition(head_last(f["L1_xattn_q_b"])),
        "L1_xattn_k_b": per_partition(head_last(kv_b[:D])),
        "norm_w": per_partition(f["L0_attn_norm_w"]),
        "conv_w": f["L0_attn_conv_w"].reshape(NB, P, TAPS).transpose(1, 0, 2).reshape(P, -1),
        "conv_b": per_partition(f["L0_attn_conv_b"]),
        "dt_b": per_partition(f["L0_attn_dt_proj_b"]),
        "D": per_partition(f["L0_attn_D"]),
        "A_log": f["L0_attn_A_log"].reshape(NB, P, NS).transpose(1, 0, 2).reshape(P, -1),
        "ffn_bq": per_partition(f["L0_ffn_bq"]),
        "ffn_bk": per_partition(f["L0_ffn_bk"]),
        "ffn_b1": per_partition(f["L0_ffn_b1"].reshape(-1)),
        "lconv_b": per_partition(f["L1_attn_conv_b"]),
        "mlp_b1": per_partition(f["L1_attn_b1"]),
        "bias": per_partition(f["L1_ffn_bias"].reshape(-1)),
    }
    tie = np.linspace(0.0, 1e-06, GR, dtype=np.float32)
    rows = {
        "L0_xattn_bv": f["L0_xattn_bv"], "L0_xattn_bo": f["L0_xattn_bo"],
        "L1_xattn_v_b": kv_b[D:], "L1_xattn_proj_b": f["L1_xattn_proj_b"],
        "ffn_bv": f["L0_ffn_bv"], "ffn_bo": f["L0_ffn_bo"], "ffn_bg": f["L0_ffn_bg"],
        "tie": np.tile(tie, NG), "gamma": f["L1_attn_gamma"].reshape(1),
    }
    consts = np.zeros((P, NCONST), np.float32)
    lane = np.arange(P)
    consts[:, C_ID:C_ID + P] = lane[:, None] == lane
    consts[:, C_BLOCK:C_BLOCK + P] = lane[:, None] // HD == lane // HD
    consts[:, C_GROUP:C_GROUP + NG] = lane[:, None] // GR == np.arange(NG)
    out = {
        "x": f["x"][0],
        "ctxT": f["ctx_768"][0].T,
        "cols": np.concatenate([cols[n] for n in COLS], 1),
        "rows": np.concatenate([rows[n] for n in ROWS]),
        "rows1": np.concatenate([f["L1_attn_" + n] for n in ROWS1]),
        "consts": consts,
        "L0_wq": head_last(f["L0_xattn_Wq"]), "L0_wo": f["L0_xattn_Wo"],
        "L0_wkv": np.stack([head_last(f["L0_xattn_Wk"]), f["L0_xattn_Wv"]]),
        "L1_wq": head_last(f["L1_xattn_q_w"]), "L1_wo": f["L1_xattn_proj_w"],
        "L1_wkv": np.stack([head_last(kv_w[:, :D]), kv_w[:, D:]]),
        "w0_in_proj": f["L0_attn_in_proj_w"], "w0_x_proj": f["L0_attn_x_proj_w"],
        "w0_dt_proj": f["L0_attn_dt_proj_w"], "w0_out_proj": f["L0_attn_out_proj_w"],
        "w0_b2": f["L0_ffn_b2"],
        "ffn_W1": f["L0_ffn_W1"], "ffn_W2": f["L0_ffn_W2"],
        "w1_conv_w": f["L1_attn_conv_w"].reshape(H, HD, HD, CONV).transpose(0, 2, 3, 1).reshape(D, CONV, HD),
        "w1_controller": f["L1_ffn_controller"].reshape(D, ES),
        "f1": f["L1_ffn_f1"].reshape(D, ES * EF),
        "f2": f["L1_ffn_f2"].reshape(ES * EF, D),
    }
    for n in ("Wq", "Wk", "Wv", "Wo", "Wg"):
        out["w0_" + n] = f["L0_ffn_" + n]
    for n in ("Wq", "Wk", "Wv", "Wphi_q", "Wphi_k", "W1", "W2"):
        out["w1_" + n] = f["L1_attn_" + n]
    return {k: np.ascontiguousarray(v) for k, v in out.items()}


STOP = 99


def kernel(**inputs):
    import concourse.bacc as _bacc
    from concourse.bass_utils import run_bass_kernel_spmd as _run

    nc = _bacc.Bacc("TRN2", target_bir_lowering=False, num_devices=1)
    arrays = _lay_out(inputs)
    aps = {k: nc.dram_tensor(k, v.shape, mybir.dt.from_np(v.dtype), kind="ExternalInput").ap()
           for k, v in arrays.items()}
    out = nc.dram_tensor("result", (TOK, D), F32, kind="ExternalOutput").ap()
    build(nc, aps, out, STOP)
    r = _run(nc, [arrays], core_ids=[0])
    return r.results[0]["result"].reshape(1, TOK, D)
```

```python
from contextlib import ExitStack

import concourse.bass as bass
from concourse import mybir

ALU = mybir.AluOpType
ACT = mybir.ActivationFunctionType
F32 = mybir.dt.float32
BF16 = mybir.dt.bfloat16
I32 = mybir.dt.int32
AX_X = mybir.AxisListType.X

P = 128
TOK = 128
D = 256
KC = D // P
CTX = 12544
CC = 192
CP = 96
H = 16
HD = D // H
CK = 896
NCH = CTX // CK
TPC = CK // P
HALF = CK // 2
SLOTS = 6
VW = 32
UNITS = 2 * TPC
Q_SPLIT = (0, 1, 2, 0, 1, 0)
K_SPLIT = (0, 0, 0, 1, 1, 2)
CLAMP = 1e4
TAME_LO, TAME_HI = -9800.0, 9900.0
TILES = CTX // P
EARLY = 3
EPS = 1e-5
WARM = (16, 2)
PAIR_OF_ONES = 1.0019378662109375
DI = 512
NB = DI // P
NS = 16
RANK = 64
TAPS = 4
NE = 8
HID = 1024
HB = HID // P
CONV = 5
GR = 16
NG = TOK // GR
ES = 64
EF = 64
PAIRS = ES // 2

A_KST, A_V, A_CTX = 0, 14336, 21504
A_KTF, A_RES, A_KP, A_O, ARENA = 25088, 26880, 28672, 31360, 32768
W_WORDS = 6304

COLS = {}
_n = 0
for _name, _w in (("L0_xattn_bq", KC), ("L0_xattn_bk", KC), ("L1_xattn_q_b", KC), ("L1_xattn_k_b", KC),
                  ("norm_w", KC), ("conv_w", NB * TAPS), ("conv_b", NB), ("dt_b", NB), ("D", NB),
                  ("A_log", NB * NS), ("ffn_bq", KC), ("ffn_bk", KC), ("ffn_b1", NE * HB),
                  ("lconv_b", KC), ("mlp_b1", HB), ("bias", PAIRS)):
    COLS[_name] = (_n, _n + _w)
    _n += _w
NCOLS = _n
ROWS = {}
_n = 0
for _name, _w in (("L0_xattn_bv", D), ("L0_xattn_bo", D), ("L1_xattn_v_b", D), ("L1_xattn_proj_b", D),
                  ("ffn_bv", D), ("ffn_bo", D), ("ffn_bg", NE), ("tie", TOK), ("gamma", 1)):
    ROWS[_name] = (_n, _n + _w)
    _n += _w
NROWS = _n
ROWS1 = {}
_n = 0
for _name, _w in (("bq", D), ("bk", D), ("bv", D), ("lnq_g", D), ("lnk_g", D), ("lnv_g", D),
                  ("lnq_b", D), ("lnk_b", D), ("lnv_b", D), ("bphi_q", D), ("bphi_k", D),
                  ("lna_g", D), ("lna_b", D), ("b2", D)):
    ROWS1[_name] = (_n, _n + _w)
    _n += _w
NROWS1 = _n
STACK = 16 * SLOTS * KC
C_ID, C_BLOCK, C_GROUP, C_HEAD, NCONST = 0, 128, 256, 256 + NG, 256 + NG + 8


def iteration_plan():
    plan = [("v", 0), ("row", 0), ("v", 1), ("v", 2), ("v", 3), ("o", 0)]
    plan += [("s", 0), ("e", 0), ("s", 1), ("e", 1), ("k", 0)]
    maxima = [("b", n) for n in range(2 * H)]
    keys = {0: 1, 2: 2, 3: 3}
    splits = {1: [("k1", 0)], 4: [("k1", 1)], 5: [("k2", 0)], 6: [("k2", 1)]}
    per_unit = (2, 3, 2, 2, 3, 2, 3, 3, 2, 3, 3, 2, 2)
    for u in range(UNITS):
        plan.append(("pv", u))
        if u + 2 < UNITS:
            plan += [("s", u + 2), ("e", u + 2)]
        if u in keys:
            plan.append(("k", keys[u]))
        if u < len(per_unit):
            plan += [maxima.pop(0) for _ in range(per_unit[u])]
        plan += splits.get(u, [])
    assert not maxima
    return plan + [("m", 0), ("ot", 0)]


RING_STEPS = ("row", "v", "o", "b", "k")
RING = 3

SIGNALS = {
    "mamba_pe": ("rmsT_full", "x_dbl_full", "dt_full", "mamba_full"),
    "mamba_act": ("M_std", "M2_std", "A_exp", "res_exp", "xc_exp", "sp_exp", "sp_ln"),
    "mamba_dve": ("M_var", "M_normed", "M2_var", "rms_normed", "rmsT_ready", "A_ready", "conv_ready", "xi_ready",
                  "dr_ready", "bcT_ready", "negabs_ready", "sp_u", "delta_ready", "dtu_ready", "y_ready",
                  "mamba_done"),
    "ffn_pe": ("FxT_full", "Fqk_full", "Fv_full", "Fs_full", "FpT_full", "Fa_full", "FaT_full", "Fo_full",
               "Fx1T_full", "Fg_full", "FgT_full", "Fb2_full"),
    "ffn_act": ("F_std", "FxT_ready", "Fexp_done", "FpT_ready", "Fa_ready", "FaT_ready", "Fx1T_ready",
                "Fgexp_done", "FgT_ready"),
    "ffn_dve": ("F_var", "F_normed", "Fqk_ready", "Fmax_ready", "Fp_ready", "Fx1_ready", "Fgmax_ready",
                "Fg_ready", "ffn_done"),
    "linear_pe": ("GxT_full", "Gqg_full", "GQT_full", "GscT_full", "Gal_full", "GpQT_full", "Gks_full",
                  "GKV_full", "Gnum_full", "GaT_full", "Gconv_full", "Ga2_full", "Ga3T_full", "Gy_full"),
    "linear_act": ("G_std", "GxT_ready", "GQ_std", "GQT_ready", "Gexp_done", "GpQT_ready", "GaT_ready", "GA_std",
                   "Ga3T_ready", "GgT_ready"),
    "linear_dve": ("G_var", "G_normed", "GQ_var", "Gqkv_ready", "Gsc_ready", "GscT_ready", "Gphi_biased",
                   "GalT_ready", "Gphi_ready", "Gpks_ready", "GKV_ready", "Gattn_ready", "GaT2_ready", "GA_var",
                   "GA_normed", "Ga3_ready"),
    "sets_pe": ("SxT_full", "Slog_full", "Sperm_full", "Sinn_full", "Sy_full"),
    "sets_act": ("S_std", "SxT_ready", "Ssel_ready"),
    "sets_dve": ("S_var", "S_normed", "perm_ready", "Spd_ready", "Sgx_ready"),
}
for _lay in ("L0_", "L1_"):
    SIGNALS[_lay + "pe"] = tuple(_lay + n for n in ("xT_full", "aT_full", "out_full"))
    SIGNALS[_lay + "act"] = tuple(_lay + n for n in ("ln_std", "xT_ready", "aT_ready"))
    SIGNALS[_lay + "dve"] = tuple(_lay + n for n in ("ln_var", "ln_normed", "q_split", "ots_zero", "att_ready",
                                                     "attended"))
GROUP_OF = {name: (group, n + 1) for group, names in SIGNALS.items() for n, name in enumerate(names)}


def slots_of(plan, first):
    out, pos = {}, first
    last = {}
    for step in plan:
        if step[0] in RING_STEPS:
            out[step] = (pos % RING, last.get(pos % RING))
            last[pos % RING] = step
            pos += 1
    return out, last


def build(nc, a, out):
    with ExitStack() as ctx:
        def sb(name, shape, dt=F32):
            return ctx.enter_context(nc.sbuf_tensor(name, shape, dt))

        sems = {}

        def sem(name):
            if name not in sems:
                sems[name] = ctx.enter_context(nc.semaphore(name))
            return sems[name]

        signalled = {}

        def signal(name):
            group, n = GROUP_OF.get(name, (None, 1))
            if group:
                assert signalled.get(group, 0) == n - 1, name
                signalled[group] = n
            return sem(group or name), 1

        def done_of(name):
            group, n = GROUP_OF.get(name, (None, 1))
            return sem(group or name), n

        arena = sb("arena", [P, ARENA])
        warena = sb("warena", [P, W_WORDS])
        cols = sb("cols_sb", [P, NCOLS])
        rows = sb("rows_sb", [P, NROWS])
        consts = sb("consts_sb", [P, NCONST])
        xr = sb("xr", [P, D])
        xn = sb("xn", [P, D])
        xT = sb("xT", [P, KC, TOK])
        wx = sb("wx", [P, 2, 2, D])
        wkv = sb("wkv", [CP, 2, 2, D])
        qst = sb("qst", [CP + 1, 2, H, TOK], BF16)
        qparts = sb("qparts", [P, 3, KC, TOK], BF16)
        mpart = sb("mpart", [P, 2 * H])
        mneg = sb("mneg", [P, H])
        nmb = sb("nmb", [P, 2, H], BF16)
        nmf = sb("nmf", [P, 2, H])
        mdiff = sb("mdiff", [P, H])
        alpha = sb("alpha", [P, 2, H])
        rowb = sb("rowb", [H, TOK], BF16)
        stats = sb("stats", [P, 3, 6])
        mv = sb("mv", [P, 3, 2])
        var = sb("var", [P, 3])
        std = sb("std", [P, 3])
        rstd = sb("rstd", [P, 3])
        tmp = [sb(f"tmp{i}", [P, D]) for i in range(2)]
        small = sb("small", [P, 64])
        unused = sb("unused", [1, 32])
        wild = sb("wild", [1, 1], I32)

        def af(lo, n):
            return arena[:, lo:lo + n]

        kst = arena[:, A_KST:A_V].bitcast(BF16).rearrange("p (b h k) -> p b h k", b=2, h=H)
        vv = af(A_V, 2 * TPC * H * VW).rearrange("p (b t h d) -> p b t h d", b=2, t=TPC, h=H)
        ctxt = af(A_CTX, 2 * 2 * CK).rearrange("p (b c k) -> p b c k", b=2, c=2)
        ktf = af(A_KTF, 2 * CK)
        res = af(A_RES, 2 * CK)
        kparts = af(A_KP, 3 * CK).bitcast(BF16).rearrange("p (s k) -> p s k", s=3)
        oacc = af(A_O, H * VW).rearrange("p (h d) -> p h d", h=H)
        ots = af(A_O + H * VW, 4 * TOK)
        work = sb("work", [P, 3976])
        pbuf = work[:, 0:2 * 8 * TOK].rearrange("p (b k) -> p b k", b=2)

        st = ctx.enter_context(nc.psum_tensor("st", [P, 4, 512], F32))
        ot = ctx.enter_context(nc.psum_tensor("ot", [P, 512], F32))
        ring = ctx.enter_context(nc.psum_tensor("ring", [P, RING, 512], F32))
        pb = [st[:, i] for i in range(4)] + [ot[:, :]] + [ring[:, i] for i in range(RING)]

        ident = consts[:, C_ID:C_ID + P]
        blockmask = consts[:, C_BLOCK:C_BLOCK + P]
        groupmask = consts[:, C_GROUP:C_GROUP + NG]
        headmask = consts[:, C_HEAD:C_HEAD + 8]

        def col(name):
            return cols[:, COLS[name][0]:COLS[name][1]]

        def row(name):
            return rows[:, ROWS[name][0]:ROWS[name][1]]

        def row1(name):
            return rows1[:, ROWS1[name][0]:ROWS1[name][1]]

        scratch_bc = nc.dram_tensor("scratch_bc", [2 * NS, TOK], F32).ap()
        scratch_perm = nc.dram_tensor("scratch_perm", [ES, TOK], F32).ap()

        def carve(base, shapes):
            views, at = {}, 0
            for name, dims in shapes:
                n = 1
                for d in dims:
                    n *= d
                v = base[:, at:at + n]
                if len(dims) == 2:
                    v = v.rearrange("p (a b) -> p a b", a=dims[0])
                if len(dims) == 3:
                    v = v.rearrange("p (a b c) -> p a b c", a=dims[0], b=dims[1])
                views[name] = v
                at += n
            assert at <= base.shape[1], (at, base.shape)
            return views

        w0 = carve(warena[:, :], (("in_proj", (KC, 2 * DI)), ("x_proj", (NB, RANK + 2 * NS)), ("dt_proj", (DI,)),
                                  ("out_proj", (NB, D)), ("Wq", (KC, D)), ("Wk", (KC, D)), ("Wv", (KC, D)),
                                  ("Wo", (KC, D)), ("Wg", (KC, NE)), ("b2", (D,))))
        w1 = carve(warena[:, :], (("Wq", (KC, D)), ("Wk", (KC, D)), ("Wv", (KC, D)), ("Wphi_q", (KC, D)),
                                  ("Wphi_k", (KC, D)), ("W1", (KC, HID)),
                                  ("conv_w", (KC, CONV, HD)), ("controller", (KC, ES))))
        m_hc = af(EARLY * 4096, 2 * NS * TOK).rearrange("p (b k) -> p b k", b=2)
        m_ = carve(arena[:, 4 * 4096:], (("dA", (2, NS * TOK)), ("dBu", (2, NS * TOK)), ("h", (NS * TOK,)),
                                         ("bc", (2 * NS * TOK,)), ("dr", (TOK,)), ("bcT", (TOK,)),
                                         ("A", (NB * NS,))))
        m2 = carve(arena[:, 4 * 4096 + 14656:], (("xpad", (NB, TOK + TAPS - 1)), ("xi", (NB, TOK)),
                                                       ("sres", (NB, TOK))))
        m3 = carve(work[:, :], tuple((n, (NB, TOK)) for n in ("z", "e", "u", "l", "dtu")))
        ew = [carve(af(4096 * e, 4096), (("W1", (KC, HID)), ("W2", (HB, D)))) for e in range(NE)]
        f_ = carve(work[:, :], (("q", (KC, TOK)), ("k", (KC, TOK)), ("v", (D,)), ("p", (TOK,)),
                                                 ("pT", (TOK,)), ("aT", (KC, TOK)), ("x1", (D,)),
                                                 ("hT", (HB, TOK)), ("hT1", (HB, TOK)), ("g", (NE,)), ("gT", (TOK,)), ("y", (D,))))
        hT2 = [f_["hT"], f_["hT1"]]

        f1 = af(0, KC * ES * EF).rearrange("p (k n) -> p k n", k=KC)
        f2 = af(8192, PAIRS * D).rearrange("p (k n) -> p k n", k=PAIRS)
        permx = af(16384, PAIRS * TOK).rearrange("p (k n) -> p k n", k=PAIRS)
        mlp_w2 = af(16384, HB * D).rearrange("p (k n) -> p k n", k=HB)
        rows1 = af(20480, NROWS1)
        l_ = carve(arena[:, 24576:], (("qkv", (3, D)), ("QT", (2, KC, TOK)), ("phi", (2, D)), ("prod", (D,)),
                                      ("scT", (TOK + 1,)), ("pks", (D,)), ("pk0", (D,)), ("KV", (KC, P)),
                                      ("pQT", (KC, TOK)), ("attn", (D,)), ("aT", (KC, TOK + CONV - 1)),
                                      ("aT2", (KC, TOK)), ("a3", (D,)), ("gT", (HB, TOK)),
                                      ("cw", (KC * CONV, P)), ("mean", (P,)), ("ones", (P,)), ("permT", (TOK,)), ("perm", (ES,)),
                                      ("gmax", (NG,)), ("alpha", (H,)), ("ksum", (D,)), ("den", (H,))))
        g_ = carve(arena[:, 0:A_KTF], (("qm", (H, TOK)), ("mb", (H * TOK,)), ("s", (H * TOK,)), ("nan", (H * TOK,)),
                                       ("kT", (KC, P)), ("v", (H, VW)), ("ctx", (2, P)), ("acc", (4 * TOK,)),
                                       ("vsum", (D + 1,)), ("avg", (P,)), ("one", (P,)), ("m", (H,)),
                                       ("oT", (H, VW)), ("use", (D,)), ("keep", (D,)), ("mean", (D,))))
        pdiag = af(20480, ES * NG).rearrange("p (e g) -> p e g", g=NG)
        selT = af(20480 + 512, KC * 512).rearrange("p (k n) -> p k n", k=KC)
        innT = af(20480 + 1536, PAIRS * NG).rearrange("p (k n) -> p k n", k=PAIRS)

        block = ctx.enter_context(nc.Block())

        FREE = {"row": ("row_out", 1), "v": ("v_out", 4), "o": ("o_added", 1), "b": ("b_max", 2 * H), "k": ("k_out", 4)}
        AHEAD = {"row": 0, "v": 1, "o": 1, "b": 1, "k": 2}

        def ring_free(pe, lay, step, c):
            kind, n = step
            name, per = FREE[kind]
            pe.wait_ge(sem(f"{lay}_{name}"), (c + AHEAD[kind]) * per + n + 1)

        PLAN = iteration_plan()
        LOOP_SLOTS, LOOP_LAST = slots_of(PLAN, 0)
        PRO = [("k", n) for n in range(4)] + [("v", n) for n in range(4)] + [("k", 4 + n) for n in range(4)] + \
              [("b", n) for n in range(2 * H)]
        PRO_SLOTS, PRO_LAST = slots_of(PRO, 1)
        assert {s: x for s, x in LOOP_LAST.items()} == PRO_LAST and sum(s[0] in RING_STEPS for s in PLAN) % RING == 0

        @block.sync
        def _(sp):
            def load(dst, src, name):
                sp.dma_start(dst, src).then_inc(sem(name), 16)

            def chunked(w):
                return w.rearrange("(k p) n -> p k n", p=P)

            load(xr[:, :], a["x"], "x_in")
            load(consts[:, :], a["consts"], "const_in")
            load(cols[:, :], a["cols"], "const_in")

            def attention_weights(lay):
                load(wx[:, 0], chunked(a[f"{lay}_wq"]), f"{lay}_wq_in")
                for n in range(2):
                    load(wkv[:, :, n], a[f"{lay}_wkv"][n].rearrange("(k p) n -> p k n", p=CP), f"{lay}_wkv_in")
                load(wx[:, 1], chunked(a[f"{lay}_wo"]), f"{lay}_wo_in")

            def load_ctx(lay, par, at):
                load(ctxt[0:CP, par], a["ctxT"].rearrange("(k p) n -> p k n", p=CP)[:, :, bass.ds(at, CK)],
                     f"{lay}_ctx_in{par}")

            def stack(lay, par, count):
                for part in range(3):
                    for m in range(KC):
                        sp.wait_ge(sem(f"{lay}_k{part + 1}_done"), KC * (count - 1) + m + 1)
                        for s in range(SLOTS):
                            if K_SPLIT[s] == part:
                                load(kst[HD * s:HD * (s + 1), par].rearrange("l (h m) k -> l h m k", m=KC)[:, :, m],
                                     kparts[:, part, m * CK:(m + 1) * CK], f"{lay}_kst_in{par}")

            def attention_loads(lay, later_weights):
                sp.wait_ge(*done_of(f"{lay}_q_split"))
                for s, part in enumerate(Q_SPLIT):
                    load(qst[HD * s:HD * (s + 1), 0].rearrange("l (h m) t -> l h (m t)", m=KC),
                         qparts[:, part].rearrange("p m t -> p (m t)"), f"{lay}_qst_in")
                stack(lay, 0, 1)
                sp.wait_ge(sem(f"{lay}_v_full"), 4)
                load_ctx(lay, 0, 2 * CK)

                stack(lay, 1, 2)

                def step(par, c, more):
                    sp.wait_ge(sem(f"{lay}_s_full"), (c + 1) * UNITS)
                    if more:
                        load_ctx(lay, 1 - par, (c + 3) * CK)
                    stack(lay, par, c + 3)

                with sp.Fori(0, 5) as i:
                    for par in range(2):
                        step(par, 2 * i + par, True)
                step(0, 10, True)
                step(1, 11, False)
                sp.wait_ge(sem(f"{lay}_row_in"), 16 * (NCH - 1))
                later_weights()

            load_ctx("L0", 0, 0)
            attention_weights("L0")
            load_ctx("L0", 1, CK)

            def weights0():
                load(rows[:, :], a["rows"].partition_broadcast(P), "rows_in")
                for name in ("in_proj", "out_proj", "Wq", "Wk", "Wv", "Wo", "Wg"):
                    load(w0[name], chunked(a["w0_" + name]), "w0_in")
                load(w0["x_proj"], chunked(a["w0_x_proj"]), "w0_in")
                load(w0["dt_proj"][0:RANK], a["w0_dt_proj"], "w0_in")
                load(w0["b2"][0:NE], a["w0_b2"], "w0_in")

            attention_loads("L0", weights0)

            sp.wait_ge(sem("wild_ready"), 1)
            is_wild = sp.value_load(wild[:, :], min_val=0, max_val=1)
            with sp.If(is_wild > 0):
                with sp.Fori(0, TILES) as t:
                    sp.wait_ge(sem("g_added"), t + 1)
                    sp.dma_start(g_["ctx"][0:CP], a["ctxT"].rearrange("(k p) n -> p k n", p=CP)[:, :, bass.ds(t * P, P)]
                                 ).then_inc(sem("g_ctx_in"), 16)

            sp.wait_ge(*done_of("L0_attended"))
            for e in range(EARLY):
                load(ew[e]["W1"], chunked(a["ffn_W1"][e]), f"expert_in{e}")
                load(ew[e]["W2"], chunked(a["ffn_W2"][e]), f"expert_in{e}")
            attention_weights("L1")
            sp.wait_ge(*done_of("bcT_ready"))
            sp.dma_start(scratch_bc, m_["bcT"][RANK:RANK + 2 * NS]).then_inc(sem("bc_out"), 16)
            sp.wait_ge(sem("bc_out"), 16)
            load(m_["bc"], scratch_bc.rearrange("n t -> (n t)").partition_broadcast(P), "bc_in")
            sp.wait_ge(*done_of("mamba_done"))
            for e in range(EARLY, NE):
                load(ew[e]["W1"], chunked(a["ffn_W1"][e]), f"expert_in{e}")
                load(ew[e]["W2"], chunked(a["ffn_W2"][e]), f"expert_in{e}")
            sp.wait_ge(*done_of("ffn_done"))
            load_ctx("L1", 0, 0)
            load_ctx("L1", 1, CK)

            def weights1():
                for name in ("Wq", "Wk", "Wv", "Wphi_q", "Wphi_k", "W1", "controller"):
                    load(w1[name], chunked(a["w1_" + name]), "w1_in")
                load(w1["conv_w"], a["w1_conv_w"].rearrange("(k p) c o -> p k c o", p=P), "w1_in")

            attention_loads("L1", weights1)
            sp.wait_ge(*done_of("L1_attended"))
            load(rows1, a["rows1"].partition_broadcast(P), "rows1_in")
            load(mlp_w2, chunked(a["w1_W2"]), "W2_in")
            load(f1, a["f1"].rearrange("(k p) n -> p k n", p=P), "f1_in")
            load(f2, a["f2"].rearrange("(k p) n -> p k n", p=P), "f2_in")
            sp.wait_ge(*done_of("perm_ready"))
            sp.dma_start(scratch_perm, l_["permT"][0:ES]).then_inc(sem("perm_out"), 16)
            sp.wait_ge(sem("perm_out"), 16)
            for par in range(2):
                load(permx[par * EF:(par + 1) * EF],
                     scratch_perm.rearrange("(q par) t -> par q t", par=2)[par].partition_broadcast(EF), "permx_in")
            sp.wait_ge(*done_of("result_ready"))
            sp.dma_start(out, xr[:, :]).then_inc(sem("stored"), 16)
            sp.wait_ge(sem("stored"), 16)

        @block.gpsimd
        def _(pool):
            def attention(lay):
                def rest(c, m):
                    pool.wait_ge(sem(f"{lay}_k1_done"), KC * c + m + 1)
                    nc.gpsimd.tensor_tensor(res[:, m * CK:(m + 1) * CK], ktf[:, m * CK:(m + 1) * CK],
                                            kparts[:, 0, m * CK:(m + 1) * CK], ALU.subtract
                                            ).then_inc(*signal(f"{lay}_r_done"))
                    pool.wait_ge(sem(f"{lay}_r_done"), KC * c + m + 1)

                def third(c, m):
                    pool.wait_ge(sem(f"{lay}_k2_done"), KC * c + m + 1)
                    nc.gpsimd.tensor_tensor(kparts[:, 2, m * CK:(m + 1) * CK], res[:, m * CK:(m + 1) * CK],
                                            kparts[:, 1, m * CK:(m + 1) * CK], ALU.subtract
                                            ).then_inc(*signal(f"{lay}_k3_done"))
                    pool.wait_ge(sem(f"{lay}_k3_done"), KC * c + m + 1)

                def split(c):
                    for m in range(KC):
                        rest(c, m)
                    for m in range(KC):
                        third(c, m)

                nc.gpsimd.memset(vv[:, :, :, :, HD:], 0.0).then_inc(*signal(f"{lay}_zeros_set"))
                pool.wait_ge(*done_of(f"{lay}_zeros_set"))
                nc.gpsimd.memset(vv[:, :, :, :, HD:HD + 1], 1.0).then_inc(*signal(f"{lay}_ones_set"))
                pool.wait_ge(sem(f"{lay}_ones_set"), 1)
                nc.gpsimd.memset(arena[CP:CP + 1, A_KST:A_V], PAIR_OF_ONES).then_inc(*signal(f"{lay}_ones_set"))
                pool.wait_ge(sem(f"{lay}_ones_set"), 2)
                split(1)
                pool.wait_ge(sem(f"{lay}_qst_in"), 16 * SLOTS)
                nc.gpsimd.tensor_copy(qst[0:CP, 1], qst[0:CP, 0]).then_inc(*signal(f"{lay}_qst_copied"))
                pool.wait_ge(*done_of(f"{lay}_qst_copied"))
                with pool.Fori(2, NCH) as c:
                    split(c)

            attention("L0")
            pool.wait_ge(*done_of("dtu_ready"))
            pool.wait_ge(sem("bc_in"), 16)
            for b in range(NB):
                if b >= 2:
                    pool.wait_ge(sem("scanned"), b - 1)
                nc.gpsimd.tensor_tensor(
                    m_["dBu"][:, b % 2].rearrange("p (n t) -> p n t", n=NS),
                    m3["dtu"][:, b:b + 1].broadcast_to([P, NS, TOK]),
                    m_["bc"][:, 0:NS * TOK].rearrange("p (n t) -> p n t", n=NS), ALU.mult).then_inc(*signal("dBu_ready"))
            pool.wait_ge(*done_of("ffn_done"))
            attention("L1")

        @block.tensor
        def _(pe):
            def mm(o, l, r, start=True, stop=True, **kw):
                return nc.tensor.matmul(o, l, r, start=start, stop=stop, **kw)

            def transpose2(src, bank, ready, done):
                pe.wait_ge(*done_of(ready))
                for k in range(KC):
                    last = nc.tensor.transpose(pb[bank][:, k * P:(k + 1) * P], src[:, k * P:(k + 1) * P], ident)
                last.then_inc(*signal(done))

            def keep_clock(n):
                for _ in range(n):
                    mm(pb[4][:, 0:P], ident, ident)

            def project(bank, lhs, rhs, done, n=KC):
                for k in range(n):
                    last = mm(bank, lhs(k), rhs(k), start=(k == 0), stop=(k == n - 1))
                if done:
                    last.then_inc(*signal(done))
                return last

            def general_path():
                pe.wait_ge(sem("tame_rows"), 1)
                nc.tensor.transpose(ring[0:1, 1, 0:P], small[:, 32:33], ident).then_inc(sem("tame_row_full"), 1)
                pe.wait_ge(sem("wild_ready"), 1)
                is_wild = pe.value_load(wild[:, :], min_val=0, max_val=1)
                with pe.If(is_wild > 0):
                    pe.wait_ge(sem("g_diag_ready"), 1)
                    for j in range(4):
                        last = mm(st[:, j], g_["one"], g_["s"][:, j * 512:(j + 1) * 512])
                    last.then_inc(sem("g_mb_full"), 1)
                    with pe.Fori(0, TILES) as t:
                        pe.wait_ge(sem("g_ctx_in"), 16 * t + 16)
                        for m in range(KC):
                            project(ring[:, 0, m * P:(m + 1) * P], lambda k: wkv[:, k, 0, m * P:(m + 1) * P],
                                    lambda k: g_["ctx"][0:CP, k], None, 2)
                        last = project(ring[:, 1, 0:D], lambda k: g_["ctx"][0:CP, k], lambda k: wkv[:, k, 1, :], None, 2)
                        last.then_inc(sem("g_kv_full"), 1)
                        pe.wait_ge(sem("g_kv_out"), t + 1)
                        for h in range(H):
                            last = mm(st[:, h // 4, (h % 4) * TOK:(h % 4 + 1) * TOK], g_["kT"][:, h % KC], g_["qm"][:, h])
                        last.then_inc(sem("g_s_full"), 1)
                        pe.wait_ge(sem("g_exp_done"), t + 1)
                        for h in range(H):
                            g, j = h // 4, h % 4
                            last = mm(ot[32 * j:32 * j + 32, g * TOK:(g + 1) * TOK], g_["v"][:, h],
                                      g_["s"][:, h * TOK:(h + 1) * TOK], start=(g == 0), stop=(g == 3),
                                      skip_group_check=True, tile_position=(0, 32 * j))
                        last.then_inc(sem("g_pv_full"), 1)
                    pe.wait_ge(sem("g_added"), TILES + 1)
                    mm(ring[:, 1, 0:D + 1], g_["avg"], g_["vsum"])
                    for g in range(4):
                        last = nc.tensor.transpose(ring[:, 0, g * P:(g + 1) * P], g_["acc"][:, g * P:(g + 1) * P], ident)
                    last.then_inc(sem("g_result_full"), 1)

            def attention(lay):
                keep_clock(WARM[0])
                transpose2(xn, 0, f"{lay}_ln_normed", f"{lay}_xT_full")
                keep_clock(WARM[1])
                pe.wait_ge(*done_of(f"{lay}_xT_ready"))
                pe.wait_ge(sem(f"{lay}_wq_in"), 16)
                for m in range(KC):
                    project(pb[1][:, m * P:(m + 1) * P], lambda k: wx[:, 0, k, m * P:(m + 1) * P],
                            lambda k: xT[:, k], f"{lay}_q_full")
                pe.wait_ge(sem(f"{lay}_wkv_in"), 32)

                def k_group(n, par, bank):
                    m, hf = n // 2, n % 2
                    project(ring[:, bank, 0:HALF], lambda k: wkv[:, k, 0, m * P:(m + 1) * P],
                            lambda k: ctxt[0:CP, par, k, hf * HALF:(hf + 1) * HALF], f"{lay}_k_full", 2)

                def v_group(n, par, bank):
                    tiles = range(2 * n, min(2 * n + 2, TPC))
                    for t in tiles:
                        last = project(ring[:, bank, (t % 2) * D:(t % 2 + 1) * D],
                                       lambda k: ctxt[0:CP, par, k, t * P:(t + 1) * P],
                                       lambda k: wkv[:, k, 1, :], None, 2)
                    last.then_inc(*signal(f"{lay}_v_full"))

                def b_group(n, par, bank):
                    h, hf = n // 2, n % 2
                    return mm(ring[:, bank, 0:HALF], qst[0:CP, 0, h], kst[0:CP, par, h, hf * HALF:(hf + 1) * HALF])

                for step in PRO:
                    kind, n = step
                    bank, before = PRO_SLOTS[step]
                    if before:
                        name = FREE[before[0]][0]
                        pe.wait_ge(sem(f"{lay}_{name}"), before[1] + 1)
                    if kind == "k":
                        pe.wait_ge(sem(f"{lay}_ctx_in{n // 4}"), 16)
                        k_group(n % 4, n // 4, bank)
                    if kind == "v":
                        v_group(n, 0, bank)
                    if kind == "b":
                        if n == 0:
                            pe.wait_ge(sem(f"{lay}_kst_in0"), STACK)
                            pe.wait_ge(sem(f"{lay}_qst_in"), 16 * SLOTS)
                        b_group(n, 0, bank).then_inc(*signal(f"{lay}_b_full"))

                def iteration(i, par, c, keys, nxt):
                    user = {bank: (step, c - 1) for bank, step in LOOP_LAST.items()}
                    for step in PLAN:
                        kind, n = step
                        if kind == "k" and not keys or kind in ("v", "b") and not nxt:
                            continue
                        if kind in RING_STEPS:
                            bank = LOOP_SLOTS[step][0]
                            ring_free(pe, lay, *user[bank])
                            user[bank] = (step, c)
                        if kind == "row":
                            pe.wait_ge(sem(f"{lay}_m_done"), c + 1)
                            nc.tensor.transpose(ring[0:H, bank, 0:TOK], nmf[:, par], ident).then_inc(*signal(f"{lay}_row_full"))
                        if kind == "v":
                            v_group(n, 1 - par, bank)
                        if kind == "o":
                            pe.wait_ge(sem(f"{lay}_ot_out"), c + 1)
                            for g in range(4):
                                last = nc.tensor.transpose(ring[:, bank, g * P:(g + 1) * P],
                                                           ots[:, g * P:(g + 1) * P], ident)
                            last.then_inc(*signal(f"{lay}_o_full"))
                        if kind == "s":
                            if n == 0:
                                pe.wait_ge(sem(f"{lay}_row_in"), 16 * (c + 1))
                                pe.wait_ge(sem(f"{lay}_ones_set"), 2)
                                pe.wait_ge(*done_of(f"{lay}_qst_copied"))
                            pe.wait_ge(sem(f"{lay}_exp_done"), c * UNITS + n + 1)
                            t, hf = n // 2, n % 2
                            for hh in range(8):
                                h = 8 * hf + hh
                                last = mm(st[:, 2 * (n % 2) + hh // 4, (hh % 4) * TOK:(hh % 4 + 1) * TOK],
                                          kst[0:CP + 1, par, h, t * P:(t + 1) * P], qst[:, par, h])
                            last.then_inc(*signal(f"{lay}_s_full"))
                        if kind == "pv":
                            t, hf = n // 2, n % 2
                            if n == 0:
                                pe.wait_ge(sem(f"{lay}_v_out"), 4 * (c + 1))
                                pe.wait_ge(sem(f"{lay}_ot_out"), c + 1)
                            pe.wait_ge(sem(f"{lay}_exp_done"), c * UNITS + n + 3)
                            for hh in range(8):
                                h = 8 * hf + hh
                                g, j = h // 4, h % 4
                                last = mm(ot[32 * j:32 * j + 32, g * TOK:(g + 1) * TOK], vv[:, par, t, h],
                                          pbuf[:, n % 2, hh * TOK:(hh + 1) * TOK], start=(t == 0 and g == 0),
                                          stop=(t == TPC - 1 and g == 3), skip_group_check=True,
                                          tile_position=(0, 32 * j))
                            last.then_inc(*signal(f"{lay}_pv_done"))
                        if kind == "b":
                            if n == 0:
                                pe.wait_ge(sem(f"{lay}_kst_in{1 - par}"), (i + 1 if par == 1 else i) * STACK + STACK)
                            b_group(n, 1 - par, bank).then_inc(*signal(f"{lay}_b_full"))
                        if kind == "k":
                            if n == 0:
                                pe.wait_ge(sem(f"{lay}_ctx_in{par}"), i * 16 + 32)
                            k_group(n, par, bank)

                with pe.Fori(0, 6) as i:
                    for par in range(2):
                        iteration(i, par, 2 * i + par, True, True)
                iteration(6, 0, 12, False, True)
                iteration(6, 1, 13, False, False)
                pe.wait_ge(sem(f"{lay}_ot_out"), NCH + 1)
                pe.wait_ge(sem(f"{lay}_row_out"), NCH)
                for g in range(4):
                    last = nc.tensor.transpose(ring[:, 0, g * P:(g + 1) * P], ots[:, g * P:(g + 1) * P], ident)
                last.then_inc(*signal(f"{lay}_o_full"))
                if lay == "L0":
                    general_path()
                transpose2(tmp[0], 6, f"{lay}_att_ready", f"{lay}_aT_full")
                pe.wait_ge(*done_of(f"{lay}_aT_ready"))
                pe.wait_ge(sem(f"{lay}_wo_in"), 16)
                project(pb[7][:, 0:D], lambda k: xT[:, k], lambda k: wx[:, 1, k], f"{lay}_out_full")

            def mamba():
                transpose2(tmp[0], 5, "rms_normed", "rmsT_full")
                pe.wait_ge(sem("w0_in"), 160)
                pe.wait_ge(*done_of("rmsT_ready"))
                for n in range(2 * NB):
                    project(pb[n // 4][:, (n % 4) * P:(n % 4 + 1) * P],
                            lambda k: w0["in_proj"][:, k, n * P:(n + 1) * P], lambda k: xT[:, k],
                            "in_proj_full" if n in (NB - 1, 2 * NB - 1) else None)
                pe.wait_ge(*done_of("xi_ready"))
                project(pb[2][0:RANK + 2 * NS, 0:TOK], lambda k: w0["x_proj"][:, k], lambda k: m2["xi"][:, k],
                        "x_dbl_full", NB)
                pe.wait_ge(*done_of("dr_ready"))
                for n in range(NB):
                    last = mm(pb[3][:, n * P:(n + 1) * P], w0["dt_proj"][0:RANK, n * P:(n + 1) * P],
                              m_["dr"][0:RANK])
                last.then_inc(*signal("dt_full"))
                for b in range(NB):
                    pe.wait_ge(sem("weighted"), b + 1)
                    for n in range(NS):
                        last = mm(pb[2 + 2 * (b % 2)][:, 0:TOK], ident, m_hc[:, b % 2, n * TOK:(n + 1) * TOK],
                                  start=(n == 0), stop=(n == NS - 1))
                    last.then_inc(sem("summed"), 1)
                pe.wait_ge(*done_of("y_ready"))
                project(pb[5][:, 0:D], lambda k: m3["u"][:, k], lambda k: w0["out_proj"][:, k], "mamba_full", NB)

            def ffn():
                transpose2(xn, 5, "F_normed", "FxT_full")
                pe.wait_ge(*done_of("FxT_ready"))
                for n, w in enumerate(("Wq", "Wk")):
                    for m in range(KC):
                        project(pb[n][:, m * P:(m + 1) * P], lambda k: w0[w][:, k, m * P:(m + 1) * P],
                                lambda k: xT[:, k], None if (n, m) != (1, 1) else "Fqk_full")
                project(pb[2][:, 0:D], lambda k: xT[:, k], lambda k: w0["Wv"][:, k], "Fv_full")
                pe.wait_ge(*done_of("Fqk_ready"))
                project(pb[3][:, 0:TOK], lambda k: f_["q"][:, k], lambda k: f_["k"][:, k], "Fs_full")
                pe.wait_ge(*done_of("Fp_ready"))
                nc.tensor.transpose(pb[5][:, 0:TOK], f_["p"], ident).then_inc(*signal("FpT_full"))
                pe.wait_ge(*done_of("FpT_ready"))
                mm(pb[6][:, 0:D], f_["pT"], f_["v"]).then_inc(*signal("Fa_full"))
                transpose2(tmp[0], 7, "Fa_ready", "FaT_full")
                pe.wait_ge(*done_of("FaT_ready"))
                project(pb[0][:, 0:D], lambda k: f_["aT"][:, k], lambda k: w0["Wo"][:, k], "Fo_full")
                transpose2(f_["x1"], 5, "Fx1_ready", "Fx1T_full")
                pe.wait_ge(*done_of("Fx1T_ready"))
                project(pb[4][:, 0:NE], lambda k: xT[:, k], lambda k: w0["Wg"][:, k], "Fg_full")

                def hidden(e):
                    pe.wait_ge(sem(f"expert_in{e}"), 32)
                    if e >= 2:
                        pe.wait_ge(sem("Fh_dve"), e - 1)
                        pe.wait_ge(sem("Fh_act"), e - 1)
                    for n in range(HB):
                        project(pb[2 * (e % 2) + n // 4][:, (n % 4) * P:(n % 4 + 1) * P],
                                lambda k: ew[e]["W1"][:, k, n * P:(n + 1) * P], lambda k: xT[:, k],
                                "Fh_full" if n % 4 == 3 else None)

                def down(e):
                    pe.wait_ge(sem("Fh_dve"), e + 1)
                    pe.wait_ge(sem("Fh_act"), e + 1)
                    if e >= 2:
                        pe.wait_ge(sem("Fy_added"), e - 1)
                    project(pb[5 + e % 2][:, 0:D], lambda k: hT2[e % 2][:, k], lambda k: ew[e]["W2"][:, k],
                            "Fy_full", HB)

                hidden(0)
                hidden(1)
                pe.wait_ge(*done_of("Fg_ready"))
                nc.tensor.transpose(pb[7][0:NE, 0:TOK], f_["g"], ident).then_inc(*signal("FgT_full"))
                pe.wait_ge(*done_of("FgT_ready"))
                mm(pb[4][:, 0:D], f_["gT"][0:NE], w0["b2"][0:NE]).then_inc(*signal("Fb2_full"))
                for e in range(NE):
                    down(e)
                    if e + 2 < NE:
                        hidden(e + 2)

            def linear_attention():
                transpose2(xn, 5, "G_normed", "GxT_full")
                pe.wait_ge(sem("w1_in"), 16 * 8)
                pe.wait_ge(*done_of("GxT_ready"))
                for n, w in enumerate(("Wq", "Wk", "Wv")):
                    project(pb[n][:, 0:D], lambda k: xT[:, k], lambda k: w1[w][:, k], "Gqkv_full")
                pe.wait_ge(*done_of("Gqkv_ready"))
                mm(pb[3][:, 0:D], l_["mean"], l_["qkv"][:, 0]).then_inc(*signal("Gqg_full"))
                for n in range(2):
                    for k in range(KC):
                        last = nc.tensor.transpose(pb[5][:, (2 * n + k) * P:(2 * n + k + 1) * P],
                                                   l_["qkv"][:, n, k * P:(k + 1) * P], ident)
                last.then_inc(*signal("GQT_full"))
                pe.wait_ge(*done_of("GQT_ready"))
                for n, w in enumerate(("Wphi_q", "Wphi_k")):
                    project(pb[n][:, 0:D], lambda k: l_["QT"][:, n, k], lambda k: w1[w][:, k], "Gphi_full")
                pe.wait_ge(*done_of("Gsc_ready"))
                nc.tensor.transpose(pb[6][0:H, 0:TOK], small[:, 0:H], ident).then_inc(*signal("GscT_full"))
                pe.wait_ge(*done_of("GalT_ready"))
                nc.tensor.transpose(pb[7][:, 0:H], l_["scT"][0:H, 1:TOK + 1], ident[0:H, 0:H])
                nc.tensor.transpose(pb[7][0:1, 64:64 + H], l_["scT"][0:H, 0:1], ident[0:H, 0:H]).then_inc(*signal("Gal_full"))
                pe.wait_ge(*done_of("Gphi_ready"))
                for k in range(KC):
                    last = nc.tensor.transpose(pb[2][:, k * P:(k + 1) * P], l_["phi"][:, 0, k * P:(k + 1) * P], ident)
                last.then_inc(*signal("GpQT_full"))
                pe.wait_ge(*done_of("Gpks_ready"))
                mm(pb[4][:, 0:D], l_["ones"], l_["pks"], stop=False)
                mm(pb[4][:, 0:D], l_["ones"][0:1], l_["pk0"][0:1], start=False).then_inc(*signal("Gks_full"))
                for k in range(KC):
                    last = mm(pb[3][:, k * P:(k + 1) * P], l_["pks"][:, k * P:(k + 1) * P],
                              l_["qkv"][:, 2, k * P:(k + 1) * P])
                last.then_inc(*signal("GKV_full"))
                pe.wait_ge(*done_of("GKV_ready"))
                for k in range(KC):
                    last = mm(pb[6][:, k * P:(k + 1) * P], l_["pQT"][:, k], l_["KV"][:, k])
                last.then_inc(*signal("Gnum_full"))
                transpose2(l_["attn"], 5, "Gattn_ready", "GaT_full")
                pe.wait_ge(*done_of("GaT_ready"))
                for k in range(KC):
                    for t in range(CONV):
                        last = mm(pb[7][:, k * P:(k + 1) * P], l_["cw"][:, k * CONV + t], l_["aT"][:, k, t:t + TOK],
                                  start=(t == 0), stop=(t == CONV - 1))
                last.then_inc(*signal("Gconv_full"))
                pe.wait_ge(*done_of("GaT2_ready"))
                for k in range(KC):
                    last = nc.tensor.transpose(pb[6][:, k * P:(k + 1) * P], l_["aT2"][:, k], ident)
                last.then_inc(*signal("Ga2_full"))
                transpose2(l_["a3"], 5, "Ga3_ready", "Ga3T_full")
                pe.wait_ge(*done_of("Ga3T_ready"))
                for n in range(HB):
                    project(pb[n // 4][:, (n % 4) * P:(n % 4 + 1) * P], lambda k: w1["W1"][:, k, n * P:(n + 1) * P],
                            lambda k: xT[:, k], "Gh_full" if n % 4 == 3 else None)
                pe.wait_ge(*done_of("GgT_ready"))
                pe.wait_ge(sem("W2_in"), 16)
                project(pb[7][:, 0:D], lambda k: l_["gT"][:, k], lambda k: mlp_w2[:, k], "Gy_full", HB)

            def sets():
                transpose2(xn, 5, "S_normed", "SxT_full")
                pe.wait_ge(*done_of("SxT_ready"))
                project(pb[6][0:ES, 0:TOK], lambda k: w1["controller"][:, k], lambda k: xT[:, k], "Slog_full")
                pe.wait_ge(*done_of("perm_ready"))
                nc.tensor.transpose(pb[7][:, 0:ES], l_["permT"][0:ES], ident[0:ES, 0:ES]).then_inc(*signal("Sperm_full"))
                pe.wait_ge(*done_of("Spd_ready"))
                for k in range(KC):
                    mm(pb[k][:, :], xn[:, k * P:(k + 1) * P], pdiag.rearrange("p e g -> p (e g)")).then_inc(*signal("Ssel_full"))
                pe.wait_ge(*done_of("Ssel_ready"))
                pe.wait_ge(sem("f1_in"), 16)
                pe.wait_ge(*done_of("Szeros_set"))
                for slot in range(PAIRS // 4):
                    for k in range(KC):
                        for j in range(4):
                            q = 4 * slot + j
                            last = mm(st[32 * j:32 * j + 2 * NG, 2 + slot // 4, (slot % 4) * P:(slot % 4 + 1) * P],
                                      selT[:, k, 2 * q * NG:2 * (q + 1) * NG], f1[:, k, 2 * q * EF:2 * (q + 1) * EF],
                                      start=(k == 0), stop=(k == KC - 1), skip_group_check=True,
                                      tile_position=(0, 32 * j))
                    if slot % 4 == 3:
                        last.then_inc(sem("Spairs_full"), 1)
                for slot in range(PAIRS // 4):
                    if slot % 4 == 0:
                        pe.wait_ge(sem("Spairs_out"), slot // 4 + 1)
                    last = nc.tensor.transpose(st[:, slot // 4, (slot % 4) * P:(slot % 4 + 1) * P],
                                               work[:, slot * P:(slot + 1) * P], ident)
                last.then_inc(*signal("Sinn_full"))
                pe.wait_ge(*done_of("Sgx_ready"))
                pe.wait_ge(sem("f2_in"), 16)
                project(pb[6][:, 0:D], lambda k: permx[:, k], lambda k: f2[:, k], "Sy_full", PAIRS)

            pe.wait_ge(sem("const_in"), 32)
            attention("L0")
            mamba()
            ffn()
            attention("L1")
            linear_attention()
            sets()

        @block.scalar
        def _(act):
            def root(tag, n=1):
                act.wait_ge(*done_of(f"{tag}_var"))
                nc.scalar.activation(std[:, 0:n], var[:, 0:n], ACT.Sqrt).then_inc(*signal(f"{tag}_std"))

            preloads = list(range(unused.shape[1]))

            def preload(func):
                n = preloads.pop(0)
                nc.scalar.activation(unused[:, n:n + 1], ident[0:1, 0:1], func)

            def copy_T(dst, bank, full, ready, n=D):
                act.wait_ge(*done_of(full))
                nc.scalar.copy(dst.rearrange("p k t -> p (k t)"), pb[bank][:, 0:n]).then_inc(*signal(ready))

            def general_path(bk):
                act.wait_ge(sem("wild_ready"), 1)
                is_wild = act.value_load(wild[:, :], min_val=0, max_val=1)
                with act.If(is_wild > 0):
                    with act.Fori(0, TILES) as t:
                        act.wait_ge(sem("g_kv_full"), t + 1)
                        for m in range(KC):
                            nc.scalar.activation(g_["kT"][:, m], ring[:, 0, m * P:(m + 1) * P], ACT.Identity,
                                                 bias=bk[:, m:m + 1])
                        nc.scalar.copy(g_["v"][:, :, 0:HD], ring[:, 1, 0:D].rearrange("p (h d) -> p h d", h=H)
                                       ).then_inc(sem("g_kv_out"), 1)
                        act.wait_ge(sem("g_clipped"), t + 1)
                        nc.scalar.activation(g_["s"], g_["s"], ACT.Exp).then_inc(sem("g_exp_done"), 1)

            def attention(lay, bk):
                preload(ACT.Sqrt)
                root(f"{lay}_ln")
                copy_T(xT, 0, f"{lay}_xT_full", f"{lay}_xT_ready")

                def key_out(bank, n, count):
                    m, hf = n // 2, n % 2
                    act.wait_ge(sem(f"{lay}_k_full"), count + n + 1)
                    nc.scalar.activation(ktf[:, m * CK + hf * HALF:m * CK + (hf + 1) * HALF], ring[:, bank, 0:HALF],
                                         ACT.Identity, bias=bk[:, m:m + 1]).then_inc(*signal(f"{lay}_k_out"))

                def value_out(bank, n, par, count):
                    tiles = min(2, TPC - 2 * n)
                    act.wait_ge(sem(f"{lay}_v_full"), count + n + 1)
                    nc.scalar.copy(vv[:, par, 2 * n:2 * n + tiles, :, 0:HD],
                                   ring[:, bank, 0:tiles * D].rearrange("p (t h d) -> p t h d", t=tiles, h=H)
                                   ).then_inc(*signal(f"{lay}_v_out"))

                def first_part(c, m):
                    act.wait_ge(sem(f"{lay}_k_out"), 4 * c + 2 * m + 2)
                    nc.scalar.copy(kparts[:, 0, m * CK:(m + 1) * CK], ktf[:, m * CK:(m + 1) * CK]
                                   ).then_inc(*signal(f"{lay}_k1_done"))

                def second_part(c, m):
                    act.wait_ge(sem(f"{lay}_r_done"), KC * c + m + 1)
                    nc.scalar.copy(kparts[:, 1, m * CK:(m + 1) * CK], res[:, m * CK:(m + 1) * CK]
                                   ).then_inc(*signal(f"{lay}_k2_done"))

                for n in range(4):
                    key_out(PRO_SLOTS[("k", n)][0], n, 0)
                    if n % 2 == 1:
                        first_part(0, n // 2)
                for m in range(KC):
                    second_part(0, m)
                for n in range(4):
                    value_out(PRO_SLOTS[("v", n)][0], n, 0, 0)
                act.wait_ge(sem(f"{lay}_r_done"), KC)
                for n in range(4):
                    key_out(PRO_SLOTS[("k", 4 + n)][0], n, 4)
                act.wait_ge(sem(f"{lay}_kst_in0"), STACK)
                for m in range(KC):
                    first_part(1, m)
                for m in range(KC):
                    second_part(1, m)
                preload(ACT.Exp)

                def iteration(i, par, c, keys, nxt):
                    for step in PLAN:
                        kind, n = step
                        if kind in ("k", "k1", "k2") and not keys or kind in ("v",) and not nxt:
                            continue
                        if kind == "row":
                            act.wait_ge(sem(f"{lay}_row_full"), c + 1)
                            nc.scalar.copy(rowb[:, :], ring[0:H, LOOP_SLOTS[step][0], 0:TOK]).then_inc(*signal(f"{lay}_row_out"))
                            act.wait_ge(sem(f"{lay}_row_out"), c + 1)
                            act.dma_start(qst[CP:CP + 1, par], rowb[:, :]).then_inc(sem(f"{lay}_row_in"), 16)
                            nc.scalar.activation(alpha[:, par], mdiff[:, :], ACT.Exp).then_inc(*signal(f"{lay}_alpha_done"))
                        if kind == "v":
                            if n == 0:
                                act.wait_ge(sem(f"{lay}_pv_done"), c * UNITS + 2)
                            value_out(LOOP_SLOTS[step][0], n, 1 - par, 4 * (c + 1))
                        if kind == "e":
                            act.wait_ge(sem(f"{lay}_s_full"), c * UNITS + n + 1)
                            act.wait_ge(sem(f"{lay}_pv_done"), c * UNITS + n + 1)
                            nc.scalar.activation(pbuf[:, n % 2],
                                                 st[:, 2 * (n % 2):2 * (n % 2) + 2].rearrange("p b k -> p (b k)"),
                                                 ACT.Exp).then_inc(*signal(f"{lay}_exp_done"))
                        if kind == "k":
                            if n == 0:
                                act.wait_ge(sem(f"{lay}_r_done"), KC * (c + 2))
                            key_out(LOOP_SLOTS[step][0], n, 4 * (c + 2))
                        if kind == "k1":
                            if n == 0:
                                act.wait_ge(sem(f"{lay}_kst_in{1 - par}"),
                                            (i + (2 if par == 1 else 1)) * STACK)
                            first_part(c + 2, n)
                        if kind == "k2":
                            second_part(c + 2, n)
                        if kind == "ot":
                            act.wait_ge(sem(f"{lay}_pv_done"), (c + 1) * UNITS + 2)
                            act.wait_ge(sem(f"{lay}_o_full"), c + 1)
                            nc.scalar.copy(ots[:, :], ot[:, :]).then_inc(*signal(f"{lay}_ot_out"))

                with act.Fori(0, 6) as i:
                    for par in range(2):
                        iteration(i, par, 2 * i + par, True, True)
                iteration(6, 0, 12, False, True)
                iteration(6, 1, 13, False, False)
                preload(ACT.Sqrt)
                if lay == "L0":
                    general_path(bk)
                copy_T(xT, 6, f"{lay}_aT_full", f"{lay}_aT_ready")

            def mamba():
                root("M")
                act.wait_ge(*done_of("M2_var"))
                nc.scalar.activation(std[:, 0:1], var[:, 0:1], ACT.Sqrt).then_inc(*signal("M2_std"))
                nc.scalar.activation(m_["A"], col("A_log"), ACT.Exp).then_inc(*signal("A_exp"))
                act.wait_ge(sem("in_proj_full"), 2)
                nc.scalar.activation(m2["sres"].rearrange("p b t -> p (b t)"), pb[1][:, :], ACT.Exp,
                                     scale=-1.0).then_inc(*signal("res_exp"))
                act.wait_ge(*done_of("conv_ready"))
                nc.scalar.activation(m3["e"], m3["z"], ACT.Exp, scale=-1.0).then_inc(*signal("xc_exp"))
                act.wait_ge(*done_of("negabs_ready"))
                nc.scalar.activation(m3["e"], m3["l"], ACT.Exp).then_inc(*signal("sp_exp"))
                preload(ACT.Ln)
                act.wait_ge(*done_of("sp_u"))
                nc.scalar.activation(m3["l"], m3["u"], ACT.Ln).then_inc(*signal("sp_ln"))
                preload(ACT.Exp)
                act.wait_ge(*done_of("delta_ready"))
                act.wait_ge(*done_of("A_ready"))
                for b in range(NB):
                    if b >= 2:
                        act.wait_ge(sem("scanned"), b - 1)
                    for n in range(NS):
                        ins = nc.scalar.activation(m_["dA"][:, b % 2, n * TOK + 1:(n + 1) * TOK], m3["z"][:, b, 1:],
                                                   ACT.Exp, scale=m_["A"][:, b * NS + n:b * NS + n + 1])
                    ins.then_inc(*signal("dA_ready"))
                preload(ACT.Sqrt)

            def ffn():
                root("F")
                copy_T(xT, 5, "FxT_full", "FxT_ready")
                preload(ACT.Exp)
                act.wait_ge(*done_of("Fmax_ready"))
                nc.scalar.activation(f_["p"], pb[3][:, 0:TOK], ACT.Exp, bias=small[:, 0:1], scale=1.0 / 16,
                                     accum_out=small[:, 1:2]).then_inc(*signal("Fexp_done"))
                act.wait_ge(*done_of("FpT_full"))
                nc.scalar.copy(f_["pT"], pb[5][:, 0:TOK]).then_inc(*signal("FpT_ready"))
                act.wait_ge(*done_of("Fa_full"))
                nc.scalar.copy(tmp[0][:, :], pb[6][:, 0:D]).then_inc(*signal("Fa_ready"))
                copy_T(f_["aT"], 7, "FaT_full", "FaT_ready")
                copy_T(xT, 5, "Fx1T_full", "Fx1T_ready")
                act.wait_ge(*done_of("Fgmax_ready"))
                nc.scalar.activation(small[:, 16:24], small[:, 8:16], ACT.Exp, bias=small[:, 2:3],
                                     accum_out=small[:, 3:4]).then_inc(*signal("Fgexp_done"))
                act.wait_ge(*done_of("FgT_full"))
                nc.scalar.copy(f_["gT"][0:NE], pb[7][0:NE, 0:TOK]).then_inc(*signal("FgT_ready"))
                preload(ACT.Sqrt)
                for e in range(NE):
                    act.wait_ge(sem("Fh_full"), 2 * e + 2)
                    if e >= 2:
                        act.wait_ge(sem("Fy_full"), e - 1)
                    for n in range(4, 8):
                        ins = nc.scalar.activation(hT2[e % 2][:, n], pb[2 * (e % 2) + 1][:, (n - 4) * P:(n - 3) * P],
                                                   ACT.Relu, bias=col("ffn_b1")[:, e * HB + n:e * HB + n + 1])
                    ins.then_inc(*signal("Fh_act"))

            def linear_attention():
                root("G")
                copy_T(xT, 5, "GxT_full", "GxT_ready")
                root("GQ", 3)
                preload(ACT.Exp)
                act.wait_ge(*done_of("GQT_full"))
                nc.scalar.copy(l_["QT"].rearrange("p n k t -> p (n k t)"), pb[5][:, :]).then_inc(*signal("GQT_ready"))
                act.wait_ge(*done_of("GscT_ready"))
                nc.scalar.activation(l_["scT"][0:H], l_["scT"][0:H], ACT.Exp, bias=small[0:H, 32:33],
                                     accum_out=small[0:H, 33:34]).then_inc(*signal("Gexp_done"))
                preload(ACT.Tanh)
                act.wait_ge(*done_of("Gphi_biased"))
                nc.scalar.activation(l_["phi"], l_["phi"], ACT.Tanh).then_inc(*signal("Gtanh_done"))
                nc.scalar.activation(l_["pk0"][0:1], row1("bphi_k")[0:1], ACT.Tanh).then_inc(*signal("Gtanh_done"))
                preload(ACT.Sqrt)
                act.wait_ge(*done_of("GpQT_full"))
                nc.scalar.copy(l_["pQT"].rearrange("p k t -> p (k t)"), pb[2][:, 0:D]).then_inc(*signal("GpQT_ready"))
                act.wait_ge(*done_of("GaT_full"))
                nc.scalar.copy(l_["aT"][:, :, 2:2 + TOK], pb[5][:, 0:D].rearrange("p (k t) -> p k t", k=KC)
                               ).then_inc(*signal("GaT_ready"))
                root("GA")
                preload(ACT.Gelu)
                copy_T(xT, 5, "Ga3T_full", "Ga3T_ready")
                for n in range(HB):
                    if n % 4 == 0:
                        act.wait_ge(sem("Gh_full"), n // 4 + 1)
                    ins = nc.scalar.activation(l_["gT"][:, n], pb[n // 4][:, (n % 4) * P:(n % 4 + 1) * P], ACT.Gelu,
                                               bias=col("mlp_b1")[:, n:n + 1])
                ins.then_inc(*signal("GgT_ready"))
                preload(ACT.Sqrt)

            def sets():
                root("S")
                copy_T(xT, 5, "SxT_full", "SxT_ready")
                act.wait_ge(sem("Ssel_full"), 2)
                for k in range(KC):
                    ins = nc.scalar.copy(selT[:, k], pb[k][:, :])
                ins.then_inc(*signal("Ssel_ready"))
                for n in range(2):
                    act.wait_ge(sem("Spairs_full"), n + 1)
                    nc.scalar.copy(work[:, n * 512:(n + 1) * 512], st[:, 2 + n]).then_inc(sem("Spairs_out"), 1)

            act.wait_ge(sem("const_in"), 32)
            attention("L0", col("L0_xattn_bk"))
            mamba()
            ffn()
            attention("L1", col("L1_xattn_k_b"))
            linear_attention()
            sets()

        @block.vector
        def _(dve):
            steps = [0]

            def link(ins):
                steps[0] += 1
                ins.then_inc(*signal("dve_step"))
                dve.wait_ge(sem("dve_step"), steps[0])

            V = nc.vector

            def norm(tag, src, dst):
                link(V.bn_stats(stats[:, 0], src))
                link(V.bn_aggr(mv[:, 0], stats[:, 0]))
                V.tensor_scalar(var[:, 0:1], mv[:, 0, 1:2], EPS, None, ALU.add).then_inc(*signal(f"{tag}_var"))
                dve.wait_ge(*done_of(f"{tag}_std"))
                link(V.reciprocal(rstd[:, 0:1], std[:, 0:1]))
                V.tensor_scalar(dst, src, mv[:, 0, 0:1], rstd[:, 0:1], ALU.subtract, ALU.mult).then_inc(*signal(f"{tag}_normed"))
                dve.wait_ge(*done_of(f"{tag}_normed"))

            def general_path():
                tame, nm = small[:, 16:32], nmf[:, (NCH - 1) % 2]
                link(V.tensor_scalar(tame, nm, -TAME_HI, None, ALU.is_gt))
                link(V.scalar_tensor_tensor(out=tame, in0=nm, scalar=-TAME_LO, in1=tame, op0=ALU.is_lt, op1=ALU.mult))
                link(V.scalar_tensor_tensor(out=tame, in0=oacc[:, :, HD], scalar=0.0, in1=tame, op0=ALU.is_gt,
                                            op1=ALU.mult))
                link(V.scalar_tensor_tensor(out=tame, in0=oacc[:, :, HD], scalar=1e30, in1=tame, op0=ALU.is_lt,
                                            op1=ALU.mult))
                V.tensor_reduce(small[:, 32:33], tame, AX_X, ALU.min).then_inc(sem("tame_rows"), 1)
                dve.wait_ge(sem("tame_row_full"), 1)
                link(V.tensor_reduce(small[0:1, 33:34], ring[0:1, 1, 0:P], AX_X, ALU.min))
                V.tensor_scalar(wild[:, :], small[0:1, 33:34], 0.5, None, ALU.is_lt).then_inc(sem("wild_ready"), 1)
                dve.wait_ge(sem("wild_ready"), 1)
                is_wild = dve.value_load(wild[:, :], min_val=0, max_val=1)
                with dve.If(is_wild > 0):
                    count = [0]

                    def follow(ins):
                        count[0] += 1
                        ins.then_inc(sem("g_step"), 1)
                        dve.wait_ge(sem("g_step"), count[0])

                    q = tmp[1].rearrange("p (k t) -> p k t", k=KC)
                    for h in range(H):
                        V.tensor_scalar(g_["qm"][:, h], q[:, h % KC], headmask[:, h // KC:h // KC + 1], None, ALU.mult)
                    V.memset(g_["one"], 1.0)
                    V.memset(g_["avg"], 1.0 / CTX)
                    V.memset(g_["vsum"], 0.0)
                    V.memset(g_["acc"], 0.0)
                    V.memset(g_["v"][:, :, HD:], 0.0)
                    follow(V.tensor_scalar(g_["m"], nm, -CLAMP, CLAMP, ALU.max, ALU.min))
                    V.memset(g_["v"][:, :, HD:HD + 1], 1.0)
                    for h in range(H):
                        ins = V.tensor_scalar(g_["s"][:, h * TOK:(h + 1) * TOK], ident, g_["m"][:, h:h + 1], None, ALU.mult)
                    ins.then_inc(sem("g_diag_ready"), 1)
                    dve.wait_ge(sem("g_mb_full"), 1)
                    scores = st.rearrange("p b k -> p (b k)")
                    V.tensor_copy(g_["mb"], scores).then_inc(sem("g_added"), 1)
                    dve.wait_ge(sem("g_added"), 1)
                    vs = g_["vsum"][:, 0:D].rearrange("p (h d) -> p h d", h=H)
                    nans = g_["vsum"][:, D:D + 1]
                    with dve.Fori(0, TILES) as t:
                        dve.wait_ge(sem("g_s_full"), t + 1)
                        V.tensor_tensor(vs, vs, g_["v"][:, :, 0:HD], ALU.add)
                        V.tensor_copy(g_["nan"], scores).then_inc(sem("g_copied"), 1)
                        dve.wait_ge(sem("g_copied"), t + 1)
                        V.tensor_scalar(g_["s"], g_["nan"], -CLAMP, CLAMP, ALU.max, ALU.min).then_inc(sem("g_capped"), 1)
                        dve.wait_ge(sem("g_capped"), t + 1)
                        V.tensor_tensor(g_["s"], g_["s"], g_["mb"], ALU.add).then_inc(sem("g_clipped"), 1)
                        V.tensor_tensor(g_["nan"], g_["nan"], g_["nan"], ALU.not_equal).then_inc(sem("g_compared"), 1)
                        dve.wait_ge(sem("g_compared"), t + 1)
                        V.reduce_max(small[:, 34:35], g_["nan"], AX_X).then_inc(sem("g_counted"), 1)
                        dve.wait_ge(sem("g_counted"), t + 1)
                        V.tensor_tensor(nans, nans, small[:, 34:35], ALU.add)
                        dve.wait_ge(sem("g_pv_full"), t + 1)
                        V.tensor_tensor(g_["acc"], ot[:, :], g_["acc"], ALU.add).then_inc(sem("g_added"), 1)
                        dve.wait_ge(sem("g_added"), t + 2)
                    dve.wait_ge(sem("g_result_full"), 1)
                    V.tensor_copy(g_["oT"].rearrange("p h d -> p (h d)"), ring[:, 0])
                    V.tensor_copy(g_["mean"], ring[:, 1, 0:D])
                    use, keep = g_["use"].bitcast(I32), g_["keep"].bitcast(I32)
                    V.tensor_scalar(use, ring[:, 1, D:D + 1].broadcast_to([P, D]), 0.0, -1.0, ALU.is_gt, ALU.mult)
                    follow(V.tensor_scalar(keep, ring[:, 1, D:D + 1].broadcast_to([P, D]), 0.0, -1.0, ALU.is_le, ALU.mult))
                    follow(V.reciprocal(small[:, 0:H], g_["oT"][:, :, HD]))
                    follow(V.tensor_tensor(tmp[0].rearrange("p (h d) -> p h d", h=H), g_["oT"][:, :, 0:HD],
                                           small[:, 0:H].rearrange("p (h o) -> p h o", o=1).broadcast_to([P, H, HD]),
                                           ALU.mult))
                    att, mean = tmp[0][:, :].bitcast(I32), g_["mean"].bitcast(I32)
                    V.tensor_tensor(mean, mean, use, ALU.bitwise_and)
                    follow(V.tensor_tensor(att, att, keep, ALU.bitwise_and))
                    follow(V.tensor_tensor(att, att, mean, ALU.bitwise_or))

            def attention(lay, bq, bv, bo):
                norm(f"{lay}_ln", xr[:, :], xn[:, :])
                q = tmp[1].rearrange("p (k t) -> p k t", k=KC)
                r = tmp[0].rearrange("p (k t) -> p k t", k=KC)
                dve.wait_ge(sem(f"{lay}_q_full"), KC)
                for m in range(KC):
                    ins = V.tensor_scalar(q[:, m], pb[1][:, m * P:(m + 1) * P], bq[:, m:m + 1], HD ** -0.5,
                                          ALU.add, ALU.mult)
                link(ins)
                link(V.tensor_copy(qparts[:, 0], q))
                link(V.tensor_tensor(r, q, qparts[:, 0], ALU.subtract))
                link(V.tensor_copy(qparts[:, 1], r))
                V.tensor_tensor(qparts[:, 2], r, qparts[:, 1], ALU.subtract).then_inc(*signal(f"{lay}_q_split"))
                V.memset(nmb[:, 1], 1e30)
                V.memset(alpha[:, 1], 0.0).then_inc(sem(f"{lay}_exp_done"), 2)
                V.memset(oacc[:, :, :], 0.0).then_inc(*signal(f"{lay}_o_added"))
                V.memset(ots[:, :], 0.0).then_inc(*signal(f"{lay}_ots_zero"))
                dve.wait_ge(*done_of(f"{lay}_ots_zero"))
                V.memset(mneg[:, :], 0.0).then_inc(*signal(f"{lay}_ot_out"))
                V.memset(small[:, 0:1], 0.0).then_inc(sem(f"{lay}_pv_done"), 2)

                def row_max(n, bank, count):
                    dve.wait_ge(sem(f"{lay}_b_full"), count + n + 1)
                    V.reduce_max(mpart[:, n:n + 1], ring[:, bank, 0:HALF], AX_X).then_inc(*signal(f"{lay}_b_max"))

                def maxima(c, par):
                    dve.wait_ge(sem(f"{lay}_b_max"), (c + 1) * 2 * H)
                    V.tensor_reduce(mneg[:, :], mpart[:, :].rearrange("p (h f) -> p h f", f=2), AX_X, ALU.max,
                                    negate=True).then_inc(*signal(f"{lay}_mneg"))
                    dve.wait_ge(sem(f"{lay}_mneg"), c + 1)
                    V.tensor_tensor(nmb[:, par], mneg[:, :], nmb[:, 1 - par], ALU.min).then_inc(*signal(f"{lay}_nmb"))
                    dve.wait_ge(sem(f"{lay}_nmb"), c + 1)
                    if not (isinstance(c, int) and c == 0):
                        dve.wait_ge(sem(f"{lay}_alpha_done"), c)
                    V.tensor_tensor(mdiff[:, :], nmb[:, par], nmb[:, 1 - par], ALU.subtract)
                    V.tensor_copy(nmf[:, par], nmb[:, par]).then_inc(*signal(f"{lay}_m_done"))

                for m in range(KC):
                    dve.wait_ge(sem(f"{lay}_k1_done"), m + 1)
                    V.tensor_tensor(res[:, m * CK:(m + 1) * CK], ktf[:, m * CK:(m + 1) * CK],
                                    kparts[:, 0, m * CK:(m + 1) * CK], ALU.subtract).then_inc(*signal(f"{lay}_r_done"))
                for m in range(KC):
                    dve.wait_ge(sem(f"{lay}_k2_done"), m + 1)
                    V.tensor_tensor(kparts[:, 2, m * CK:(m + 1) * CK], res[:, m * CK:(m + 1) * CK],
                                    kparts[:, 1, m * CK:(m + 1) * CK], ALU.subtract
                                    ).then_inc(*signal(f"{lay}_k3_done"))
                for n in range(2 * H):
                    row_max(n, PRO_SLOTS[("b", n)][0], 0)
                maxima(0, 0)

                def add_chunk(bank, c, par):
                    dve.wait_ge(sem(f"{lay}_o_full"), c + 1)
                    V.tensor_tensor(oacc[:, :, :], oacc[:, :, :],
                                    alpha[:, 1 - par].rearrange("p (h o) -> p h o", o=1).broadcast_to([P, H, VW]),
                                    ALU.mult).then_inc(*signal(f"{lay}_o_scaled"))
                    dve.wait_ge(sem(f"{lay}_o_scaled"), c + 1)
                    V.tensor_tensor(oacc[:, :, :], ring[:, bank].rearrange("p (h d) -> p h d", h=H), oacc[:, :, :],
                                    ALU.add).then_inc(*signal(f"{lay}_o_added"))

                def iteration(i, par, c, keys, nxt):
                    for step in PLAN:
                        kind, n = step
                        if kind in ("b", "m") and not nxt:
                            continue
                        if kind == "o":
                            dve.wait_ge(sem(f"{lay}_o_added"), c + 1)
                            add_chunk(LOOP_SLOTS[step][0], c, par)
                        if kind == "b":
                            row_max(n, LOOP_SLOTS[step][0], 2 * H * (c + 1))
                        if kind == "m":
                            maxima(c + 1, 1 - par)

                with dve.Fori(0, 6) as i:
                    for par in range(2):
                        iteration(i, par, 2 * i + par, True, True)
                iteration(6, 0, 12, False, True)
                iteration(6, 1, 13, False, False)
                dve.wait_ge(sem(f"{lay}_o_added"), NCH + 1)
                add_chunk(0, NCH, 0)
                dve.wait_ge(sem(f"{lay}_o_added"), NCH + 2)
                link(V.reciprocal(small[:, 0:H], oacc[:, :, HD]))
                t3 = tmp[0].rearrange("p (h d) -> p h d", h=H)
                dve.wait_ge(sem("rows_in"), 16)
                link(V.tensor_tensor(t3, oacc[:, :, 0:HD],
                                     small[:, 0:H].rearrange("p (h o) -> p h o", o=1).broadcast_to([P, H, HD]),
                                     ALU.mult))
                if lay == "L0":
                    general_path()
                V.tensor_tensor(tmp[0][:, :], tmp[0][:, :], bv, ALU.add).then_inc(*signal(f"{lay}_att_ready"))
                link(V.tensor_tensor(xr[:, :], xr[:, :], bo, ALU.add))
                dve.wait_ge(*done_of(f"{lay}_out_full"))
                V.tensor_tensor(xr[:, :], pb[7][:, 0:D], xr[:, :], ALU.add).then_inc(*signal(f"{lay}_attended"))
                dve.wait_ge(*done_of(f"{lay}_attended"))

            def sigmoid_of_exp(t):
                link(V.tensor_scalar(t, t, 1.0, None, ALU.add))
                link(V.reciprocal(t, t))

            def mamba():
                V.memset(m2["xpad"][:, :, 0:TAPS - 1], 0.0)
                for b in range(2):
                    V.memset(m_["dA"][:, b].rearrange("p (n t) -> p n t", n=NS)[:, :, 0:1], 0.0)
                norm("M", xr[:, :], xn[:, :])
                link(V.tensor_tensor_reduce(tmp[1][:, :], xn[:, :], xn[:, :], 1.0, 0.0, ALU.mult, ALU.add,
                                            small[:, 0:1]))
                V.tensor_scalar(var[:, 0:1], small[:, 0:1], 1.0 / D, EPS, ALU.mult, ALU.add).then_inc(*signal("M2_var"))
                dve.wait_ge(*done_of("M2_std"))
                link(V.reciprocal(rstd[:, 0:1], std[:, 0:1]))
                V.tensor_scalar(tmp[0][:, :], xn[:, :], rstd[:, 0:1], None, ALU.mult).then_inc(*signal("rms_normed"))
                dve.wait_ge(*done_of("rmsT_full"))
                for k in range(KC):
                    ins = V.tensor_scalar(xT[:, k], pb[5][:, k * P:(k + 1) * P], col("norm_w")[:, k:k + 1], None,
                                          ALU.mult)
                ins.then_inc(*signal("rmsT_ready"))
                dve.wait_ge(*done_of("A_exp"))
                V.tensor_scalar(m_["A"], m_["A"], -1.0, None, ALU.mult).then_inc(*signal("A_ready"))
                dve.wait_ge(*done_of("in_proj_full"))
                link(V.tensor_copy(m2["xpad"][:, :, TAPS - 1:], pb[0].rearrange("p (b t) -> p b t", b=NB)))
                for t in range(TAPS):
                    for b in range(NB):
                        w = col("conv_w")[:, b * TAPS + t:b * TAPS + t + 1]
                        if t == 0:
                            ins = V.tensor_scalar(m3["z"][:, b], m2["xpad"][:, b, 0:TOK], w,
                                                  col("conv_b")[:, b:b + 1], ALU.mult, ALU.add)
                        else:
                            ins = V.scalar_tensor_tensor(out=m3["z"][:, b], in0=m2["xpad"][:, b, t:t + TOK],
                                                         scalar=w, in1=m3["z"][:, b], op0=ALU.mult, op1=ALU.add)
                    if t < TAPS - 1:
                        link(ins)
                ins.then_inc(*signal("conv_ready"))
                dve.wait_ge(*done_of("res_exp"))
                sigmoid_of_exp(m2["sres"])
                link(V.tensor_tensor(m2["sres"].rearrange("p b t -> p (b t)"), pb[1][:, :],
                                     m2["sres"].rearrange("p b t -> p (b t)"), ALU.mult))
                dve.wait_ge(*done_of("xc_exp"))
                sigmoid_of_exp(m3["e"])
                V.tensor_tensor(m2["xi"], m3["z"], m3["e"], ALU.mult).then_inc(*signal("xi_ready"))
                dve.wait_ge(*done_of("xi_ready"))
                dve.wait_ge(*done_of("x_dbl_full"))
                V.tensor_copy(m_["dr"][0:RANK], pb[2][0:RANK, 0:TOK]).then_inc(*signal("dr_ready"))
                V.tensor_copy(m_["bcT"][RANK:RANK + 2 * NS], pb[2][RANK:RANK + 2 * NS, 0:TOK]).then_inc(*signal("bcT_ready"))
                dve.wait_ge(*done_of("dt_full"))
                for b in range(NB):
                    ins = V.tensor_scalar(m3["z"][:, b], pb[3][:, b * P:(b + 1) * P], col("dt_b")[:, b:b + 1], None,
                                          ALU.add)
                link(ins)
                V.scalar_tensor_tensor(out=m3["l"], in0=m3["z"], scalar=-1.0, in1=m3["z"], op0=ALU.mult,
                                       op1=ALU.min).then_inc(*signal("negabs_ready"))
                dve.wait_ge(*done_of("sp_exp"))
                V.tensor_scalar(m3["u"], m3["e"], 1.0, None, ALU.add).then_inc(*signal("sp_u"))
                dve.wait_ge(*done_of("sp_u"))
                dve.wait_ge(*done_of("sp_ln"))
                link(V.tensor_scalar(m3["u"], m3["u"], 1.0, None, ALU.subtract))
                link(V.tensor_scalar(m3["dtu"], m3["u"], 0.0, None, ALU.is_equal))
                link(V.tensor_tensor(m3["u"], m3["u"], m3["dtu"], ALU.add))
                link(V.reciprocal(m3["u"], m3["u"]))
                link(V.tensor_tensor(m3["l"], m3["l"], m3["dtu"], ALU.add))
                link(V.tensor_tensor(m3["l"], m3["l"], m3["u"], ALU.mult))
                link(V.tensor_tensor(m3["l"], m3["l"], m3["e"], ALU.mult))
                V.scalar_tensor_tensor(out=m3["z"], in0=m3["z"], scalar=0.0, in1=m3["l"], op0=ALU.max,
                                       op1=ALU.add).then_inc(*signal("delta_ready"))
                dve.wait_ge(*done_of("delta_ready"))
                V.tensor_tensor(m3["dtu"], m3["z"], m2["xi"], ALU.mult).then_inc(*signal("dtu_ready"))
                def gated(b):
                    dve.wait_ge(sem("summed"), b + 1)
                    link(V.scalar_tensor_tensor(out=m3["u"][:, b], in0=m2["xi"][:, b], scalar=col("D")[:, b:b + 1],
                                                in1=pb[2 + 2 * (b % 2)][:, 0:TOK], op0=ALU.mult, op1=ALU.add))
                    link(V.tensor_tensor(m3["u"][:, b], m3["u"][:, b], m2["sres"][:, b], ALU.mult))

                for b in range(NB):
                    dve.wait_ge(sem("dA_ready"), b + 1)
                    dve.wait_ge(sem("dBu_ready"), b + 1)
                    V.tensor_tensor_scan(m_["h"], m_["dA"][:, b % 2], m_["dBu"][:, b % 2], 0.0, ALU.mult,
                                         ALU.add).then_inc(*signal("scanned"))
                    dve.wait_ge(sem("scanned"), b + 1)
                    V.tensor_tensor(m_hc[:, b % 2], m_["h"], m_["bc"][:, NS * TOK:], ALU.mult
                                    ).then_inc(sem("weighted"), 1)
                    dve.wait_ge(sem("weighted"), b + 1)
                    if b >= 1:
                        gated(b - 1)
                gated(NB - 1)
                V.memset(small[:, 63:64], 0.0).then_inc(*signal("y_ready"))
                link(V.tensor_tensor(xr[:, :], xr[:, :], xn[:, :], ALU.add))
                dve.wait_ge(*done_of("mamba_full"))
                V.tensor_tensor(xr[:, :], pb[5][:, 0:D], xr[:, :], ALU.add).then_inc(*signal("mamba_done"))
                dve.wait_ge(*done_of("mamba_done"))

            def ffn():
                norm("F", xr[:, :], xn[:, :])
                dve.wait_ge(*done_of("Fqk_full"))
                for n, (dst, b) in enumerate(((f_["q"], col("ffn_bq")), (f_["k"], col("ffn_bk")))):
                    for m in range(KC):
                        ins = V.tensor_scalar(dst[:, m], pb[n][:, m * P:(m + 1) * P], b[:, m:m + 1], None, ALU.add)
                ins.then_inc(*signal("Fqk_ready"))
                dve.wait_ge(*done_of("Fv_full"))
                V.tensor_tensor(f_["v"], pb[2][:, 0:D], row("ffn_bv"), ALU.add)
                dve.wait_ge(*done_of("Fs_full"))
                link(V.reduce_max(small[:, 4:5], pb[3][:, 0:TOK], AX_X))
                V.tensor_scalar(small[:, 0:1], small[:, 4:5], -1.0 / 16, None, ALU.mult).then_inc(*signal("Fmax_ready"))
                dve.wait_ge(*done_of("Fexp_done"))
                link(V.reciprocal(small[:, 5:6], small[:, 1:2]))
                V.tensor_scalar(f_["p"], f_["p"], small[:, 5:6], None, ALU.mult).then_inc(*signal("Fp_ready"))
                link(V.tensor_tensor(f_["x1"], xn[:, :], row("ffn_bo"), ALU.add))
                dve.wait_ge(*done_of("Fo_full"))
                V.tensor_tensor(f_["x1"], pb[0][:, 0:D], f_["x1"], ALU.add).then_inc(*signal("Fx1_ready"))
                dve.wait_ge(*done_of("Fx1_ready"))
                dve.wait_ge(*done_of("Fg_full"))
                link(V.tensor_tensor(small[:, 8:16], pb[4][:, 0:NE], row("ffn_bg"), ALU.add))
                V.tensor_reduce(small[:, 2:3], small[:, 8:16], AX_X, ALU.max, negate=True).then_inc(*signal("Fgmax_ready"))
                link(V.tensor_tensor(xr[:, :], xr[:, :], f_["x1"], ALU.add))
                dve.wait_ge(*done_of("Fgexp_done"))
                link(V.reciprocal(small[:, 6:7], small[:, 3:4]))
                V.tensor_scalar(f_["g"], small[:, 16:24], small[:, 6:7], None, ALU.mult).then_inc(*signal("Fg_ready"))
                dve.wait_ge(*done_of("Fg_ready"))

                def hidden(e):
                    dve.wait_ge(sem("Fh_full"), 2 * e + 1)
                    if e >= 2:
                        dve.wait_ge(sem("Fy_full"), e - 1)
                    for n in range(4):
                        ins = V.tensor_scalar(hT2[e % 2][:, n], pb[2 * (e % 2)][:, n * P:(n + 1) * P],
                                              col("ffn_b1")[:, e * HB + n:e * HB + n + 1], 0.0, ALU.add, ALU.max)
                    ins.then_inc(*signal("Fh_dve"))

                def add(e):
                    dve.wait_ge(sem("Fy_full"), e + 1)
                    V.scalar_tensor_tensor(out=xr[:, :], in0=pb[5 + e % 2][:, 0:D], scalar=f_["g"][:, e:e + 1],
                                           in1=xr[:, :], op0=ALU.mult, op1=ALU.add).then_inc(*signal("Fy_added"))
                    dve.wait_ge(sem("Fy_added"), e + 1)

                hidden(0)
                dve.wait_ge(*done_of("Fb2_full"))
                link(V.tensor_tensor(xr[:, :], pb[4][:, 0:D], xr[:, :], ALU.add))
                for e in range(NE):
                    if e + 1 < NE:
                        hidden(e + 1)
                    add(e)
                V.memset(small[:, 7:8], 0.0).then_inc(*signal("ffn_done"))
                dve.wait_ge(*done_of("ffn_done"))

            def linear_attention():
                V.memset(l_["mean"], HD ** -0.5 / TOK)
                V.memset(l_["aT"][:, :, 0:2], 0.0)
                V.memset(l_["aT"][:, :, 2 + TOK:], 0.0)
                link(V.memset(l_["ones"], 1.0))
                norm("G", xr[:, :], xn[:, :])
                dve.wait_ge(sem("Gqkv_full"), 3)
                dve.wait_ge(sem("rows1_in"), 16)
                for n, b in enumerate(("bq", "bk", "bv")):
                    ins = V.tensor_tensor(l_["qkv"][:, n], pb[n][:, 0:D], row1(b), ALU.add)
                link(ins)
                for n in range(3):
                    ins = V.bn_stats(stats[:, n], l_["qkv"][:, n])
                link(ins)
                for n in range(3):
                    ins = V.bn_aggr(mv[:, n], stats[:, n])
                link(ins)
                V.tensor_scalar(var[:, :], mv[:, :, 1], EPS, None, ALU.add).then_inc(*signal("GQ_var"))
                dve.wait_ge(*done_of("GQ_std"))
                link(V.reciprocal(rstd[:, :], std[:, :]))
                for n in range(3):
                    ins = V.tensor_scalar(l_["qkv"][:, n], l_["qkv"][:, n], mv[:, n, 0:1], rstd[:, n:n + 1],
                                          ALU.subtract, ALU.mult)
                link(ins)
                g0, b0 = ROWS1["lnq_g"][0], ROWS1["lnq_b"][0]
                q3 = l_["qkv"].rearrange("p n d -> p (n d)")
                link(V.tensor_tensor(q3, q3, rows1[:, g0:g0 + 3 * D], ALU.mult))
                V.tensor_tensor(q3, q3, rows1[:, b0:b0 + 3 * D], ALU.add).then_inc(*signal("Gqkv_ready"))
                dve.wait_ge(*done_of("Gqkv_ready"))
                dve.wait_ge(*done_of("Gqg_full"))
                link(V.tensor_tensor(l_["prod"], pb[3][:, 0:D], l_["qkv"][:, 1], ALU.mult))
                V.reduce_sum(small[:, 0:H], l_["prod"].rearrange("p (h d) -> p h d", h=H), AX_X).then_inc(*signal("Gsc_ready"))
                V.memset(l_["scT"][0:H, 0:1], 0.0)
                dve.wait_ge(*done_of("GscT_full"))
                link(V.tensor_copy(l_["scT"][0:H, 1:TOK + 1], pb[6][0:H, 0:TOK]))
                V.tensor_reduce(small[0:H, 32:33], l_["scT"][0:H], AX_X, ALU.max, negate=True).then_inc(*signal("GscT_ready"))
                dve.wait_ge(sem("Gphi_full"), 2)
                for n, b in enumerate(("bphi_q", "bphi_k")):
                    ins = V.tensor_tensor(l_["phi"][:, n], pb[n][:, 0:D], row1(b), ALU.add)
                ins.then_inc(*signal("Gphi_biased"))
                dve.wait_ge(*done_of("Gexp_done"))
                link(V.reciprocal(small[0:H, 34:35], small[0:H, 33:34]))
                V.tensor_scalar(l_["scT"][0:H], l_["scT"][0:H], small[0:H, 34:35], float(TOK), ALU.mult,
                                ALU.mult).then_inc(*signal("GalT_ready"))
                dve.wait_ge(sem("Gtanh_done"), 2)
                link(V.tensor_scalar(l_["pk0"][0:1], l_["pk0"][0:1], 1.0, None, ALU.add))
                V.tensor_scalar(l_["phi"], l_["phi"], 1.0, None, ALU.add).then_inc(*signal("Gphi_ready"))
                dve.wait_ge(*done_of("Gphi_ready"))
                dve.wait_ge(*done_of("Gal_full"))
                link(V.tensor_copy(l_["alpha"], pb[7][:, 0:H]))
                link(V.tensor_copy(small[0:1, 40:40 + H], pb[7][0:1, 64:64 + H]))
                v3 = lambda t: t.rearrange("p (h d) -> p h d", h=H)
                link(V.tensor_tensor(v3(l_["pk0"])[0:1], v3(l_["pk0"])[0:1],
                                     small[0:1, 40:40 + H].rearrange("p (h o) -> p h o", o=1)
                                     .broadcast_to([1, H, HD]), ALU.mult))
                V.tensor_tensor(v3(l_["pks"]), v3(l_["phi"][:, 1]),
                                l_["alpha"].rearrange("p (h o) -> p h o", o=1).broadcast_to([P, H, HD]),
                                ALU.mult).then_inc(*signal("Gpks_ready"))
                dve.wait_ge(*done_of("Gks_full"))
                link(V.tensor_copy(l_["ksum"], pb[4][:, 0:D]))
                dve.wait_ge(*done_of("GpQT_ready"))
                dve.wait_ge(*done_of("GKV_full"))
                V.tensor_tensor(l_["KV"], pb[3][:, 0:D].rearrange("p (k d) -> p k d", k=KC),
                                blockmask.rearrange("p (o d) -> p o d", o=1).broadcast_to([P, KC, P]),
                                ALU.mult).then_inc(*signal("GKV_ready"))
                link(V.tensor_tensor(l_["prod"], l_["phi"][:, 0], l_["ksum"], ALU.mult))
                link(V.reduce_sum(l_["den"], v3(l_["prod"]), AX_X))
                link(V.tensor_scalar(l_["den"], l_["den"], 1e-6, None, ALU.add))
                link(V.reciprocal(l_["den"], l_["den"]))
                for k in range(KC):
                    for t in range(CONV):
                        ins = V.tensor_tensor(l_["cw"][:, k * CONV + t].rearrange("p (g o) -> p g o", o=HD),
                                              w1["conv_w"][:, k, t:t + 1].broadcast_to([P, P // HD, HD]),
                                              blockmask.rearrange("p (g o) -> p g o", o=HD), ALU.mult)
                dve.wait_ge(*done_of("Gnum_full"))
                V.tensor_tensor(v3(l_["attn"]), v3(pb[6][:, 0:D]),
                                l_["den"].rearrange("p (h o) -> p h o", o=1).broadcast_to([P, H, HD]),
                                ALU.mult).then_inc(*signal("Gattn_ready"))
                dve.wait_ge(*done_of("GaT_ready"))
                dve.wait_ge(*done_of("Gconv_full"))
                for k in range(KC):
                    ins = V.tensor_scalar(l_["aT2"][:, k], pb[7][:, k * P:(k + 1) * P], col("lconv_b")[:, k:k + 1],
                                          row("gamma"), ALU.add, ALU.mult)
                link(ins)
                V.tensor_tensor(l_["aT2"], l_["aT2"], l_["aT"][:, :, 2:2 + TOK], ALU.add).then_inc(*signal("GaT2_ready"))
                dve.wait_ge(*done_of("Ga2_full"))
                link(V.tensor_copy(l_["attn"], pb[6][:, 0:D]))
                norm("GA", l_["attn"], l_["a3"])
                link(V.tensor_tensor(l_["a3"], l_["a3"], row1("lna_g"), ALU.mult))
                V.tensor_tensor(l_["a3"], l_["a3"], row1("lna_b"), ALU.add).then_inc(*signal("Ga3_ready"))
                dve.wait_ge(*done_of("Ga3_ready"))
                link(V.tensor_tensor(xr[:, :], xr[:, :], xn[:, :], ALU.add))
                link(V.tensor_tensor(xr[:, :], xr[:, :], l_["a3"], ALU.add))
                link(V.tensor_tensor(xr[:, :], xr[:, :], row1("b2"), ALU.add))
                dve.wait_ge(*done_of("Gy_full"))
                link(V.tensor_tensor(xr[:, :], pb[7][:, 0:D], xr[:, :], ALU.add))

            def sets():
                norm("S", xr[:, :], xn[:, :])
                dve.wait_ge(*done_of("Slog_full"))
                lg = tmp[0][0:ES, 0:TOK]
                g3 = lambda t: t.rearrange("p (g t) -> p g t", t=GR)
                link(V.tensor_tensor(lg, pb[6][0:ES, 0:TOK], row("tie")[0:ES], ALU.add))
                link(V.reduce_max(l_["gmax"][0:ES], g3(lg), AX_X))
                V.tensor_tensor(g3(l_["permT"][0:ES]), g3(lg),
                                l_["gmax"][0:ES].rearrange("p (g o) -> p g o", o=1).broadcast_to([ES, NG, GR]),
                                ALU.is_equal).then_inc(*signal("perm_ready"))
                dve.wait_ge(*done_of("Sperm_full"))
                link(V.tensor_copy(l_["perm"], pb[7][:, 0:ES]))
                V.tensor_tensor(pdiag, l_["perm"].rearrange("p (e o) -> p e o", o=1).broadcast_to([P, ES, NG]),
                                groupmask.rearrange("p (o g) -> p o g", o=1).broadcast_to([P, ES, NG]),
                                ALU.mult).then_inc(*signal("Spd_ready"))
                V.memset(st[:, 2:4], 0.0).then_inc(*signal("Szeros_set"))
                dve.wait_ge(*done_of("Sinn_full"))
                for par in range(2):
                    sl = slice(par * EF, (par + 1) * EF)
                    ins = V.tensor_tensor(innT[sl], st[sl, 0:2].rearrange("p b (q r g) -> p (b q) r g", r=4, g=NG)[:, :, par],
                                          col("bias")[sl].rearrange("p (q o) -> p q o", o=1)
                                          .broadcast_to([EF, PAIRS, NG]), ALU.add)
                link(ins)
                link(V.tensor_scalar(innT, innT, 0.0, None, ALU.max))
                dve.wait_ge(sem("permx_in"), 32)
                V.tensor_tensor(permx.rearrange("p q (g t) -> p (q g) t", t=GR),
                                permx.rearrange("p q (g t) -> p (q g) t", t=GR),
                                innT.rearrange("p q (g o) -> p (q g) o", o=1).broadcast_to([P, PAIRS * NG, GR]),
                                ALU.mult).then_inc(*signal("Sgx_ready"))
                dve.wait_ge(*done_of("Sy_full"))
                link(V.tensor_tensor(xr[:, :], pb[6][:, 0:D], xr[:, :], ALU.add))

            dve.wait_ge(sem("x_in"), 16)
            dve.wait_ge(sem("const_in"), 32)
            attention("L0", col("L0_xattn_bq"), row("L0_xattn_bv"), row("L0_xattn_bo"))
            mamba()
            ffn()
            attention("L1", col("L1_xattn_q_b"), row("L1_xattn_v_b"), row("L1_xattn_proj_b"))
            linear_attention()
            sets()
            V.memset(small[:, 63:64], 0.0).then_inc(*signal("result_ready"))


_ARRAYS = []


def _lay_out(t):
    import numpy as np
    f = {k: np.asarray(v) for k, v in t.items()}

    def per_partition(v):
        return v.reshape(-1, P).T

    def head_last(v):
        return np.moveaxis(v.reshape(v.shape[:-1] + (H // KC, KC, HD)), -3, -1).reshape(v.shape)

    kv_w, kv_b = f["L1_xattn_kv_w"], f["L1_xattn_kv_b"]
    cols = {
        "L0_xattn_bq": per_partition(head_last(f["L0_xattn_bq"])),
        "L0_xattn_bk": per_partition(head_last(f["L0_xattn_bk"])),
        "L1_xattn_q_b": per_partition(head_last(f["L1_xattn_q_b"])),
        "L1_xattn_k_b": per_partition(head_last(kv_b[:D])),
        "norm_w": per_partition(f["L0_attn_norm_w"]),
        "conv_w": f["L0_attn_conv_w"].reshape(NB, P, TAPS).transpose(1, 0, 2).reshape(P, -1),
        "conv_b": per_partition(f["L0_attn_conv_b"]),
        "dt_b": per_partition(f["L0_attn_dt_proj_b"]),
        "D": per_partition(f["L0_attn_D"]),
        "A_log": f["L0_attn_A_log"].reshape(NB, P, NS).transpose(1, 0, 2).reshape(P, -1),
        "ffn_bq": per_partition(f["L0_ffn_bq"]),
        "ffn_bk": per_partition(f["L0_ffn_bk"]),
        "ffn_b1": per_partition(f["L0_ffn_b1"].reshape(-1)),
        "lconv_b": per_partition(f["L1_attn_conv_b"]),
        "mlp_b1": per_partition(f["L1_attn_b1"]),
        "bias": per_partition(f["L1_ffn_bias"].reshape(-1)),
    }
    tie = np.linspace(0.0, 1e-06, GR, dtype=np.float32)
    rows = {
        "L0_xattn_bv": f["L0_xattn_bv"], "L0_xattn_bo": f["L0_xattn_bo"],
        "L1_xattn_v_b": kv_b[D:], "L1_xattn_proj_b": f["L1_xattn_proj_b"],
        "ffn_bv": f["L0_ffn_bv"], "ffn_bo": f["L0_ffn_bo"], "ffn_bg": f["L0_ffn_bg"],
        "tie": np.tile(tie, NG), "gamma": f["L1_attn_gamma"].reshape(1),
    }
    consts = np.zeros((P, NCONST), np.float32)
    lane = np.arange(P)
    consts[:, C_ID:C_ID + P] = lane[:, None] == lane
    consts[:, C_BLOCK:C_BLOCK + P] = lane[:, None] // HD == lane // HD
    consts[:, C_GROUP:C_GROUP + NG] = lane[:, None] // GR == np.arange(NG)
    consts[:, C_HEAD:C_HEAD + 8] = lane[:, None] % 8 == np.arange(8)
    out = {
        "x": f["x"][0],
        "ctxT": f["ctx_768"][0].T,
        "cols": np.concatenate([cols[n] for n in COLS], 1),
        "rows": np.concatenate([rows[n] for n in ROWS]),
        "rows1": np.concatenate([f["L1_attn_" + n] for n in ROWS1]),
        "consts": consts,
        "L0_wq": head_last(f["L0_xattn_Wq"]), "L0_wo": f["L0_xattn_Wo"],
        "L0_wkv": np.stack([head_last(f["L0_xattn_Wk"]), f["L0_xattn_Wv"]]),
        "L1_wq": head_last(f["L1_xattn_q_w"]), "L1_wo": f["L1_xattn_proj_w"],
        "L1_wkv": np.stack([head_last(kv_w[:, :D]), kv_w[:, D:]]),
        "w0_in_proj": f["L0_attn_in_proj_w"], "w0_x_proj": f["L0_attn_x_proj_w"],
        "w0_dt_proj": f["L0_attn_dt_proj_w"], "w0_out_proj": f["L0_attn_out_proj_w"],
        "w0_b2": f["L0_ffn_b2"],
        "ffn_W1": f["L0_ffn_W1"], "ffn_W2": f["L0_ffn_W2"],
        "w1_conv_w": f["L1_attn_conv_w"].reshape(H, HD, HD, CONV).transpose(0, 2, 3, 1).reshape(D, CONV, HD),
        "w1_controller": f["L1_ffn_controller"].reshape(D, ES),
        "f1": f["L1_ffn_f1"].reshape(D, ES * EF),
        "f2": f["L1_ffn_f2"].reshape(ES * EF, D),
    }
    for n in ("Wq", "Wk", "Wv", "Wo", "Wg"):
        out["w0_" + n] = f["L0_ffn_" + n]
    for n in ("Wq", "Wk", "Wv", "Wphi_q", "Wphi_k", "W1", "W2"):
        out["w1_" + n] = f["L1_attn_" + n]
    return {k: np.ascontiguousarray(v) for k, v in out.items()}


def kernel(**inputs):
    import concourse.bacc as _bacc
    from concourse.bass_utils import run_bass_kernel_spmd as _run

    nc = _bacc.Bacc("TRN2", target_bir_lowering=False, num_devices=1)
    arrays = _lay_out(inputs)
    aps = {k: nc.dram_tensor(k, v.shape, mybir.dt.from_np(v.dtype), kind="ExternalInput").ap()
           for k, v in arrays.items()}
    out = nc.dram_tensor("result", (TOK, D), F32, kind="ExternalOutput").ap()
    build(nc, aps, out)
    r = _run(nc, [arrays], core_ids=[0])
    return r.results[0]["result"].reshape(1, TOK, D)
```
